# Optimizing a Trainium2 kernel written in Bass

```python
import numpy as np
import jax
import jax.numpy as jnp

def _softmax(x, axis=-1):
    return jax.nn.softmax(x, axis=axis)

def _gelu(x):
    return jax.nn.gelu(x, approximate=True)

def _silu(x):
    return jax.nn.silu(x)

def _sigmoid(x):
    return jax.nn.sigmoid(x)

def _layernorm(x, axis=-1, eps=1e-05):
    m = jnp.mean(x, axis=axis, keepdims=True)
    v = jnp.var(x, axis=axis, keepdims=True)
    return (x - m) / jnp.sqrt(v + eps)

def _scatter_add(tgt, idx, src, axis=0):
    return tgt.at[idx].add(src)

def _segment_sum(src, seg, n):
    return jax.ops.segment_sum(src, seg, n)
kernel_name = 'mk_adaln_ffn_d2_seqx_r4_9f340e'

def setup_inputs(seed: int=0):
    np.random.seed(seed)
    _w = jnp.asarray

    def _rec_inputs():
        import jax
        import jax.numpy as jnp
        _rk = jax.random.key(seed)
        x = -0.0003929 + 0.9999 * jax.random.normal(jax.random.fold_in(_rk, 1), (4, 512, 512), jnp.float32)
        _lenS = 512 - jax.random.randint(jax.random.fold_in(_rk, 7), (4,), 0, max(1, 512 // 4) + 1, jnp.int32)
        _lenS2 = 512 - jax.random.randint(jax.random.fold_in(_rk, 8), (4,), 0, max(1, 512 // 4) + 1, jnp.int32)
        cond_1 = jax.random.uniform(jax.random.fold_in(_rk, 11), (4, 1), jnp.float32, 0.0, 1.37214)
        itok_B_0_6 = jax.random.randint(jax.random.fold_in(_rk, 12), (4,), 0, 7, jnp.int32)
        return (x, cond_1, itok_B_0_6)
    x, cond_1, itok_B_0_6 = _rec_inputs()

    def _L0_cond_setup():
        import jax, jax.numpy as jnp
        import numpy as np
        B, S, D_MODEL, NHEAD = (4, 512, 512, 16)
        HEAD_DIM = D_MODEL // NHEAD
        key = jax.random.key(seed)
        ks = jax.random.split(key, 6)
        scale = 1.0 / np.sqrt(D_MODEL)
        return {'hidden_states': jax.random.normal(ks[0], (B, S, D_MODEL), dtype=jnp.float32), 'attention_precision': jax.random.uniform(ks[1], (B, 1, 1), dtype=jnp.float32, minval=0.5, maxval=2.0), 'Wq': jax.random.normal(ks[2], (D_MODEL, D_MODEL), dtype=jnp.float32) * scale, 'Wk': jax.random.normal(ks[3], (D_MODEL, D_MODEL), dtype=jnp.float32) * scale, 'Wv': jax.random.normal(ks[4], (D_MODEL, D_MODEL), dtype=jnp.float32) * scale, 'Wo': jax.random.normal(ks[5], (D_MODEL, D_MODEL), dtype=jnp.float32) * scale}
    _L0_cond_all = _L0_cond_setup()
    _L0_cond_in = {k: v for k, v in _L0_cond_all.items() if k in ('Wq', 'Wk', 'Wv', 'Wo')}
    del _L0_cond_all

    def _L0_ffn_setup():
        import jax, jax.numpy as jnp
        import numpy as np
        B, S, H, I, E, F, K, R, TOPK = (1, 256, 512, 352, 64, 8, 8, 8, 6)
        ISH = 2 * I

        def _fused_linear(x, W, qa, qb, scale, w):
            out = x @ W.T
            a = jnp.einsum('th,krh->tkr', x, qa)
            b = jnp.einsum('tkr,khr->tkh', a, qb)
            mix = jnp.einsum('tkh,tk->th', b, w)
            return out + scale[None, :] * mix

        def _moe_forward(hidden_states, gate_weight, inv_mapping, mask_up_W, gate_W, gate_qa, gate_qb, gate_scale, up_W, up_qa, up_qb, up_scale, down_W, down_qa, down_qb, down_scale, sh_gate_W, sh_up_W, sh_down_W):
            b, s, h = hidden_states.shape
            x = hidden_states.reshape(-1, h)
            T = x.shape[0]
            scores = jax.nn.softmax(x @ gate_weight.T, axis=-1)
            topk_w, topk_idx = jax.lax.top_k(scores, TOPK)
            w_dense = jnp.zeros((T, E), x.dtype).at[jnp.arange(T)[:, None], topk_idx].add(topk_w)
            flat = w_dense[:, inv_mapping]
            scalar = flat.sum(-1)
            soft = jax.nn.softmax(jnp.where(flat == 0, -1000000000.0, flat), axis=-1)

            def expert(muW, gW, gqa, gqb, gs, uW, uqa, uqb, us, dW, dqa, dqb, ds, w):
                xe = x + w @ muW.T
                gate = jax.nn.silu(_fused_linear(xe, gW, gqa, gqb, gs, w))
                up = _fused_linear(xe, uW, uqa, uqb, us, w)
                return _fused_linear(gate * up, dW, dqa, dqb, ds, w)
            outs = jax.vmap(expert, in_axes=(0,) * 13 + (1,))(mask_up_W, gate_W, gate_qa, gate_qb, gate_scale, up_W, up_qa, up_qb, up_scale, down_W, down_qa, down_qb, down_scale, soft)
            y = jnp.einsum('fth,tf->th', outs, scalar).reshape(b, s, h)
            sh = jax.nn.silu(hidden_states @ sh_gate_W.T) * (hidden_states @ sh_up_W.T) @ sh_down_W.T
            return y + sh
        key = jax.random.key(seed)
        ks = jax.random.split(key, 20)
        g = lambda k, shape, s=0.02: jax.random.normal(k, shape, jnp.float32) * s
        return {'hidden_states': jax.random.normal(ks[0], (B, S, H), jnp.float32), 'gate_weight': g(ks[1], (E, H)), 'inv_mapping': jnp.arange(E, dtype=jnp.int32).reshape(F, K), 'mask_up_W': g(ks[2], (F, H, K)), 'gate_W': g(ks[3], (F, I, H)), 'gate_qa': g(ks[4], (F, K, R, H)), 'gate_qb': g(ks[5], (F, K, I, R)), 'gate_scale': jnp.full((F, I), 0.1, jnp.float32), 'up_W': g(ks[6], (F, I, H)), 'up_qa': g(ks[7], (F, K, R, H)), 'up_qb': g(ks[8], (F, K, I, R)), 'up_scale': jnp.full((F, I), 0.1, jnp.float32), 'down_W': g(ks[9], (F, H, I)), 'down_qa': g(ks[10], (F, K, R, I)), 'down_qb': g(ks[11], (F, K, H, R)), 'down_scale': jnp.full((F, H), 0.1, jnp.float32), 'sh_gate_W': g(ks[12], (ISH, H)), 'sh_up_W': g(ks[13], (ISH, H)), 'sh_down_W': g(ks[14], (H, ISH))}
    _L0_ffn_all = _L0_ffn_setup()
    _L0_ffn_in = {k: v for k, v in _L0_ffn_all.items() if k in ('gate_weight', 'inv_mapping', 'mask_up_W', 'gate_W', 'gate_qa', 'gate_qb', 'gate_scale', 'up_W', 'up_qa', 'up_qb', 'up_scale', 'down_W', 'down_qa', 'down_qb', 'down_scale', 'sh_gate_W', 'sh_up_W', 'sh_down_W')}
    del _L0_ffn_all

    def _L1_cond_setup():
        import jax, jax.numpy as jnp
        import numpy as np
        B, T, D_IN, D_OUT = (16, 512, 512, 512)
        N_ADAPTERS, RANK = (8, 16)
        key = jax.random.key(seed)
        k_x, k_w, k_a, k_b, k_s, k_idx = jax.random.split(key, 6)
        x = jax.random.normal(k_x, (B, T, D_IN), dtype=jnp.float32)
        W = jax.random.normal(k_w, (D_OUT, D_IN), dtype=jnp.float32) * (1.0 / np.sqrt(D_IN))
        A = jax.random.normal(k_a, (N_ADAPTERS, RANK, D_IN), dtype=jnp.float32) * 0.02
        Bm = jax.random.normal(k_b, (N_ADAPTERS, D_OUT, RANK), dtype=jnp.float32) * 0.02
        scalings = jnp.ones((N_ADAPTERS,), dtype=jnp.float32)
        adapter_idx = jax.random.randint(k_idx, (B,), 0, N_ADAPTERS, dtype=jnp.int32)
        return {'x': x, 'W': W, 'A': A, 'Bm': Bm, 'scalings': scalings, 'adapter_idx': adapter_idx}
    _L1_cond_all = _L1_cond_setup()
    _L1_cond_in = {k: v for k, v in _L1_cond_all.items() if k in ('W', 'A', 'Bm', 'scalings')}
    del _L1_cond_all

    def _L1_ffn_setup():
        import jax, jax.numpy as jnp
        import numpy as np
        FP8_MAX = 448.0
        GLOBAL_DIV = 448.0 * 6.0

        def _fp8(x):
            return x.astype(jnp.float8_e4m3fn).astype(jnp.float32)

        def _reorder_quantize_x(x, idx):
            scale = jnp.max(jnp.abs(x)) / GLOBAL_DIV
            xr = (x / scale)[:, idx]
            scale_x = jnp.max(jnp.abs(xr), axis=1, keepdims=True) / FP8_MAX
            qx = _fp8(xr / scale_x)
            return (qx, scale_x, scale)

        def _qlinear(qx, scale_x, scale, W, idx, out_idx=None):
            Wr = W[:, idx]
            w_scale = jnp.max(jnp.abs(Wr), axis=1, keepdims=True) / FP8_MAX
            qw = _fp8(Wr / w_scale)
            y = qx * scale_x @ (qw * w_scale).T * scale
            if out_idx is not None:
                y = y[:, out_idx]
            return y
        key = jax.random.key(seed)
        ks = jax.random.split(key, 6)
        B, S, H, I = (2, 256, 512, 1408)
        return {'x': jax.random.normal(ks[0], (B, S, H), jnp.float32), 'w_gate': jax.random.normal(ks[1], (I, H), jnp.float32) * 0.02, 'w_up': jax.random.normal(ks[2], (I, H), jnp.float32) * 0.02, 'w_down': jax.random.normal(ks[3], (H, I), jnp.float32) * 0.02, 'up_reorder_index': jax.random.permutation(ks[4], jnp.arange(H, dtype=jnp.int64)), 'down_reorder_index': jax.random.permutation(ks[5], jnp.arange(I, dtype=jnp.int64))}
    _L1_ffn_all = _L1_ffn_setup()
    _L1_ffn_in = {k: v for k, v in _L1_ffn_all.items() if k in ('w_gate', 'w_up', 'w_down', 'up_reorder_index', 'down_reorder_index')}
    del _L1_ffn_all
    return {'x': x, 'cond_1': cond_1, 'itok_B_0_6': itok_B_0_6, 'L0_cond_Wq': _L0_cond_in['Wq'], 'L0_cond_Wk': _L0_cond_in['Wk'], 'L0_cond_Wv': _L0_cond_in['Wv'], 'L0_cond_Wo': _L0_cond_in['Wo'], 'L0_ffn_gate_weight': _L0_ffn_in['gate_weight'], 'L0_ffn_inv_mapping': _L0_ffn_in['inv_mapping'], 'L0_ffn_mask_up_W': _L0_ffn_in['mask_up_W'], 'L0_ffn_gate_W': _L0_ffn_in['gate_W'], 'L0_ffn_gate_qa': _L0_ffn_in['gate_qa'], 'L0_ffn_gate_qb': _L0_ffn_in['gate_qb'], 'L0_ffn_gate_scale': _L0_ffn_in['gate_scale'], 'L0_ffn_up_W': _L0_ffn_in['up_W'], 'L0_ffn_up_qa': _L0_ffn_in['up_qa'], 'L0_ffn_up_qb': _L0_ffn_in['up_qb'], 'L0_ffn_up_scale': _L0_ffn_in['up_scale'], 'L0_ffn_down_W': _L0_ffn_in['down_W'], 'L0_ffn_down_qa': _L0_ffn_in['down_qa'], 'L0_ffn_down_qb': _L0_ffn_in['down_qb'], 'L0_ffn_down_scale': _L0_ffn_in['down_scale'], 'L0_ffn_sh_gate_W': _L0_ffn_in['sh_gate_W'], 'L0_ffn_sh_up_W': _L0_ffn_in['sh_up_W'], 'L0_ffn_sh_down_W': _L0_ffn_in['sh_down_W'], 'L1_cond_W': _L1_cond_in['W'], 'L1_cond_A': _L1_cond_in['A'], 'L1_cond_Bm': _L1_cond_in['Bm'], 'L1_cond_scalings': _L1_cond_in['scalings'], 'L1_ffn_w_gate': _L1_ffn_in['w_gate'], 'L1_ffn_w_up': _L1_ffn_in['w_up'], 'L1_ffn_w_down': _L1_ffn_in['w_down'], 'L1_ffn_up_reorder_index': _L1_ffn_in['up_reorder_index'], 'L1_ffn_down_reorder_index': _L1_ffn_in['down_reorder_index']}

def reference(x, cond_1, itok_B_0_6, L0_cond_Wq, L0_cond_Wk, L0_cond_Wv, L0_cond_Wo, L0_ffn_gate_weight, L0_ffn_inv_mapping, L0_ffn_mask_up_W, L0_ffn_gate_W, L0_ffn_gate_qa, L0_ffn_gate_qb, L0_ffn_gate_scale, L0_ffn_up_W, L0_ffn_up_qa, L0_ffn_up_qb, L0_ffn_up_scale, L0_ffn_down_W, L0_ffn_down_qa, L0_ffn_down_qb, L0_ffn_down_scale, L0_ffn_sh_gate_W, L0_ffn_sh_up_W, L0_ffn_sh_down_W, L1_cond_W, L1_cond_A, L1_cond_Bm, L1_cond_scalings, L1_ffn_w_gate, L1_ffn_w_up, L1_ffn_w_down, L1_ffn_up_reorder_index, L1_ffn_down_reorder_index):
    import jax
    import jax.numpy as jnp

    def _L0_cond_ref(hidden_states, attention_precision, Wq, Wk, Wv, Wo):
        import jax, jax.numpy as jnp
        import numpy as np
        B, S, D_MODEL, NHEAD = (4, 512, 512, 16)
        HEAD_DIM = D_MODEL // NHEAD
        b, s, _ = hidden_states.shape

        def proj(x, W):
            y = jnp.einsum('bsd,ed->bse', x, W)
            return y.reshape(b, s, NHEAD, HEAD_DIM).transpose(0, 2, 1, 3)
        q = proj(hidden_states, Wq)
        k = proj(hidden_states, Wk)
        v = proj(hidden_states, Wv)
        beta = jnp.minimum(attention_precision, 4.0)[:, None]
        q = q * beta
        scores = jnp.einsum('bhqd,bhkd->bhqk', q, k) / np.sqrt(HEAD_DIM)
        causal = jnp.tril(jnp.ones((s, s), dtype=bool))
        scores = jnp.where(causal, scores, jnp.finfo(scores.dtype).min)
        attn = jax.nn.softmax(scores, axis=-1)
        out = jnp.einsum('bhqk,bhkd->bhqd', attn, v)
        out = out.transpose(0, 2, 1, 3).reshape(b, s, D_MODEL)
        return jnp.einsum('bsd,ed->bse', out, Wo)

    def _L0_ffn_ref(hidden_states, gate_weight, inv_mapping, mask_up_W, gate_W, gate_qa, gate_qb, gate_scale, up_W, up_qa, up_qb, up_scale, down_W, down_qa, down_qb, down_scale, sh_gate_W, sh_up_W, sh_down_W):
        import jax, jax.numpy as jnp
        import numpy as np
        B, S, H, I, E, F, K, R, TOPK = (1, 256, 512, 352, 64, 8, 8, 8, 6)
        ISH = 2 * I

        def _fused_linear(x, W, qa, qb, scale, w):
            out = x @ W.T
            a = jnp.einsum('th,krh->tkr', x, qa)
            b = jnp.einsum('tkr,khr->tkh', a, qb)
            mix = jnp.einsum('tkh,tk->th', b, w)
            return out + scale[None, :] * mix

        def _moe_forward(hidden_states, gate_weight, inv_mapping, mask_up_W, gate_W, gate_qa, gate_qb, gate_scale, up_W, up_qa, up_qb, up_scale, down_W, down_qa, down_qb, down_scale, sh_gate_W, sh_up_W, sh_down_W):
            b, s, h = hidden_states.shape
            x = hidden_states.reshape(-1, h)
            T = x.shape[0]
            scores = jax.nn.softmax(x @ gate_weight.T, axis=-1)
            topk_w, topk_idx = jax.lax.top_k(scores, TOPK)
            w_dense = jnp.zeros((T, E), x.dtype).at[jnp.arange(T)[:, None], topk_idx].add(topk_w)
            flat = w_dense[:, inv_mapping]
            scalar = flat.sum(-1)
            soft = jax.nn.softmax(jnp.where(flat == 0, -1000000000.0, flat), axis=-1)

            def expert(muW, gW, gqa, gqb, gs, uW, uqa, uqb, us, dW, dqa, dqb, ds, w):
                xe = x + w @ muW.T
                gate = jax.nn.silu(_fused_linear(xe, gW, gqa, gqb, gs, w))
                up = _fused_linear(xe, uW, uqa, uqb, us, w)
                return _fused_linear(gate * up, dW, dqa, dqb, ds, w)
            outs = jax.vmap(expert, in_axes=(0,) * 13 + (1,))(mask_up_W, gate_W, gate_qa, gate_qb, gate_scale, up_W, up_qa, up_qb, up_scale, down_W, down_qa, down_qb, down_scale, soft)
            y = jnp.einsum('fth,tf->th', outs, scalar).reshape(b, s, h)
            sh = jax.nn.silu(hidden_states @ sh_gate_W.T) * (hidden_states @ sh_up_W.T) @ sh_down_W.T
            return y + sh
        return _moe_forward(hidden_states, gate_weight, inv_mapping, mask_up_W, gate_W, gate_qa, gate_qb, gate_scale, up_W, up_qa, up_qb, up_scale, down_W, down_qa, down_qb, down_scale, sh_gate_W, sh_up_W, sh_down_W)

    def _L1_cond_ref(x, W, A, Bm, scalings, adapter_idx):
        import jax, jax.numpy as jnp
        import numpy as np
        B, T, D_IN, D_OUT = (16, 512, 512, 512)
        N_ADAPTERS, RANK = (8, 16)
        H = jnp.einsum('btd,od->bto', x, W)
        A_b = A[adapter_idx]
        B_b = Bm[adapter_idx]
        s_b = scalings[adapter_idx]
        xa = jnp.einsum('btd,brd->btr', x, A_b)
        delta = jnp.einsum('btr,bor->bto', xa, B_b)
        delta = jax.lax.stop_gradient(delta * s_b[:, None, None])
        return H + delta

    def _L1_ffn_ref(x, w_gate, w_up, w_down, up_reorder_index, down_reorder_index):
        import jax, jax.numpy as jnp
        import numpy as np
        FP8_MAX = 448.0
        GLOBAL_DIV = 448.0 * 6.0

        def _fp8(x):
            return x.astype(jnp.float8_e4m3fn).astype(jnp.float32)

        def _reorder_quantize_x(x, idx):
            scale = jnp.max(jnp.abs(x)) / GLOBAL_DIV
            xr = (x / scale)[:, idx]
            scale_x = jnp.max(jnp.abs(xr), axis=1, keepdims=True) / FP8_MAX
            qx = _fp8(xr / scale_x)
            return (qx, scale_x, scale)

        def _qlinear(qx, scale_x, scale, W, idx, out_idx=None):
            Wr = W[:, idx]
            w_scale = jnp.max(jnp.abs(Wr), axis=1, keepdims=True) / FP8_MAX
            qw = _fp8(Wr / w_scale)
            y = qx * scale_x @ (qw * w_scale).T * scale
            if out_idx is not None:
                y = y[:, out_idx]
            return y
        B, S, H = x.shape
        xf = x.reshape(B * S, H)
        qx, sx, sc = _reorder_quantize_x(xf, up_reorder_index)
        g = _qlinear(qx, sx, sc, w_gate, up_reorder_index, out_idx=down_reorder_index)
        u = _qlinear(qx, sx, sc, w_up, up_reorder_index, out_idx=down_reorder_index)
        t = jax.nn.silu(g) * u
        qt, st, sct = _reorder_quantize_x(t, down_reorder_index)
        y = _qlinear(qt, st, sct, w_down, down_reorder_index)
        return y.reshape(B, S, H)
    x = x + _L0_ffn_ref(_L0_cond_ref(x, cond_1[:, None, :], L0_cond_Wq, L0_cond_Wk, L0_cond_Wv, L0_cond_Wo), L0_ffn_gate_weight, L0_ffn_inv_mapping, L0_ffn_mask_up_W, L0_ffn_gate_W, L0_ffn_gate_qa, L0_ffn_gate_qb, L0_ffn_gate_scale, L0_ffn_up_W, L0_ffn_up_qa, L0_ffn_up_qb, L0_ffn_up_scale, L0_ffn_down_W, L0_ffn_down_qa, L0_ffn_down_qb, L0_ffn_down_scale, L0_ffn_sh_gate_W, L0_ffn_sh_up_W, L0_ffn_sh_down_W)
    x = x + _L1_ffn_ref(_L1_cond_ref(x, L1_cond_W, L1_cond_A, L1_cond_Bm, L1_cond_scalings, itok_B_0_6), L1_ffn_w_gate, L1_ffn_w_up, L1_ffn_w_down, L1_ffn_up_reorder_index, L1_ffn_down_reorder_index)
    return x

_drawn_inputs = setup_inputs


def setup_inputs(seed=0):
    import zlib

    import numpy as np

    out = dict(_drawn_inputs(seed))
    spreads = {'L0_ffn_gate_scale': (0.10000000149011612, 0.2),
     'L0_ffn_up_scale': (0.10000000149011612, 0.2),
     'L0_ffn_down_scale': (0.10000000149011612, 0.2),
     'L1_cond_scalings': (1.0, 0.2)}
    factors = {}
    for name, (base, spread) in spreads.items():
        noise = np.random.default_rng([zlib.crc32(name.encode()), seed]).standard_normal(out[name].shape)
        drawn = base * np.exp(spread * noise) if base else spread * noise
        out[name] = jnp.asarray(drawn.astype(out[name].dtype))
    for name, factor in factors.items():
        out[name] = (out[name] * factor).astype(out[name].dtype)
    return out
```

```python
from contextlib import ExitStack

import concourse.bass as bass
from concourse import mybir

F32 = mybir.dt.float32
BF16 = mybir.dt.bfloat16
U32 = mybir.dt.uint32
I32 = mybir.dt.int32
ALU = mybir.AluOpType
ACT = mybir.ActivationFunctionType
AX = mybir.AxisListType

P = 128
B, S, D = 4, 512, 512
T = B * S
KD = D // P
ST = S // P
HEADS, HD = 16, 32
HPT = P // HD
F, KR, R, I = 8, 8, 8, 352
LR = KR * R
E = F * KR
TOPK = 6
IT = [(0, 128), (128, 128), (256, 96)]
NEG = -1.0e30
L1I = 1408
L1T = L1I // P
NA, RANK = 8, 16
FP8_MAX = 448.0
CH = 4
CW = 512

SHARED_COLS = [("gate", KD * I), ("up", KD * I), ("down", 3 * D)]
ROUTED_COLS = SHARED_COLS + [("qa", KD * 2 * LR), ("dqa", 3 * LR), ("qb", I), ("qscale", I),
                             ("mu", D), ("dqb", D), ("dscale", D)]


def columns(cols):
    at, out = 0, {}
    for name, n in cols:
        out[name] = (at, at + n)
        at += n
    return out, at


RC, RCOLS = columns(ROUTED_COLS)
SC, SCOLS = columns(SHARED_COLS)


def attend(nc, d, g):
    UNITS = ST * HEADS
    FRONT, QT, PTB, PSB, OB = 4, 4, 2, 4, 2
    LAG_T, LAG_V = 2, 3

    front = [("q", m) for m in range(KD)] + [("k", m) for m in range(KD)] + [("v", m) for m in range(ST)]
    steps = []
    for i in range(UNITS + LAG_V):
        turn = None
        j = i - LAG_V - 2
        if i < UNITS and j >= 0 and j % HEADS == HEADS - 1:
            turn = j // HEADS
        steps.append((i if i < UNITS else None, i - LAG_T if 0 <= i - LAG_T < UNITS else None,
                      i - LAG_V if i >= LAG_V else None, turn))
    for u, _, _, turn in steps:
        if u is not None:
            front.append(("s", u))
        if turn is not None:
            front.append(("t", turn))
    front.append(("t", ST - 1))
    front += [("o", m) for m in range(KD)]
    at = {item: n for n, item in enumerate(front)}
    NF = len(front)
    assert NF % FRONT == 0

    with ExitStack() as ctx:
        def sb(name, shape, dt):
            return ctx.enter_context(nc.sbuf_tensor(name, shape, dt))

        def sem(name):
            return ctx.enter_context(nc.semaphore(name))

        w = {n: sb("w_" + n, [P, KD, D], F32) for n in "qkvo"}
        xT = sb("xT", [P, KD, S], F32)
        qT = sb("qT", [P, KD, S], F32)
        kT = sb("kT", [P, KD, S], F32)
        v = sb("v", [P, ST, D], F32)
        probs = sb("probs", [P, PSB, S], F32)
        probsT = sb("probsT", [P, PTB, ST, P], F32)
        attn = sb("attn", [P, 2, D], F32)
        attnT = sb("attnT", [P, KD, S], F32)
        negmax = sb("negmax", [P, 4], F32)
        rowsum = sb("rowsum", [P, 2, HEADS], F32)
        rinv = sb("rinv", [P, 2, HEADS], F32)
        cond = sb("cond", [P, 1], F32)
        beta = sb("beta", [P, 1], F32)
        front_ps = ctx.enter_context(nc.psum_tensor("front_ps", [P, FRONT, 512], F32))
        turned_ps = ctx.enter_context(nc.psum_tensor("turned_ps", [P, PTB, ST, P], F32))
        out_ps = ctx.enter_context(nc.psum_tensor("out_ps", [P, OB, D], F32))

        attn_w_in = sem("attn_w_in")
        x_in = sem("x_in")
        beta_in = sem("beta_in")
        beta_done = sem("beta_done")
        front_full = sem("front_full")
        front_done = sem("front_done")
        negmax_done = sem("negmax_done")
        turned_full = sem("turned_full")
        turned_copied = sem("turned_copied")
        value_done = sem("value_done")
        rinv_done = sem("rinv_done")
        out_done = sem("out_done")

        block = ctx.enter_context(nc.Block())

        @block.sync
        def _(sp):
            for n in "qkvo":
                sp.dma_start(w[n][:, :, :], d["W" + n].rearrange("(k p) n -> p k n", p=P)).then_inc(attn_w_in, 16)
            sp.dma_start(cond[:, :], d["cond"][0:1, :].to_broadcast([P, 1])).then_inc(beta_in, 16)
            sp.dma_start(xT[:, :, :], d["xT"][0, :, :].rearrange("(k p) n -> p k n", p=P)).then_inc(x_in, 16)
            with sp.Fori(0, B - 1) as b:
                sp.wait_ge(front_done, b * NF + FRONT + at["v", ST - 1] + 1)
                sp.dma_start(cond[:, :], d["cond"][bass.ds(b + 1, 1), :].to_broadcast([P, 1])).then_inc(beta_in, 16)
                sp.dma_start(xT[:, :, :], d["xT"][bass.ds(b + 1, 1), :, :].rearrange("a (k p) n -> p (a k) n", p=P)
                             ).then_inc(x_in, 16)

        @block.tensor
        def _(pe):
            pe.wait_ge(g["ident_done"], 4)
            pe.wait_ge(attn_w_in, 64)
            with pe.Fori(0, B) as b:
                def bank(item):
                    pe.wait_ge(front_done, b * NF + at[item] + 1)
                    return front_ps[:, at[item] % FRONT, :]

                pe.wait_ge(x_in, b * 16 + 16)
                for n in "qk":
                    for m in range(KD):
                        out = bank((n, m))
                        for k in range(KD):
                            last = nc.tensor.matmul(out, w[n][:, k, m * P:(m + 1) * P], xT[:, k, :],
                                                    start=k == 0, stop=k == KD - 1)
                        last.then_inc(front_full, 1)
                for m in range(ST):
                    out = bank(("v", m))
                    for k in range(KD):
                        last = nc.tensor.matmul(out, xT[:, k, m * P:(m + 1) * P], w["v"][:, k, :],
                                                start=k == 0, stop=k == KD - 1)
                    last.then_inc(front_full, 1)
                pe.wait_ge(front_done, b * NF + FRONT + at["v", ST - 1] + 1)

                def turn(qt):
                    out = bank(("t", qt))
                    pe.wait_ge(out_done, b * ST + qt + 1 + OB)
                    for k in range(KD):
                        last = nc.tensor.transpose(out[:, k * P:(k + 1) * P],
                                                   attn[:, qt % 2, k * P:(k + 1) * P], g["ident"][:, :])
                    last.then_inc(front_full, 1)

                for u, ut, uv, ot in steps:
                    if u is not None:
                        qt, h = divmod(u, HEADS)
                        r, c, n = HD * (h % HPT), h // HPT, P * (qt + 1)
                        out = bank(("s", u))
                        nc.tensor.matmul(out[:, 0:n], qT[r:r + HD, c, qt * P:(qt + 1) * P],
                                         kT[r:r + HD, c, 0:n], start=True, stop=False)
                        nc.tensor.matmul(out[:, n - P:n], g["identb"][:, :], g["mask"][:, :],
                                         start=False, stop=True).then_inc(front_full, 1)
                    if ut is not None:
                        qt = ut // HEADS
                        pe.wait_ge(front_done, b * NF + FRONT + at["s", ut] + 1)
                        pe.wait_ge(turned_copied, b * UNITS + ut + 1)
                        for k in range(qt + 1):
                            last = nc.tensor.transpose(turned_ps[:, ut % PTB, k, :],
                                                       probs[:, ut % PSB, k * P:(k + 1) * P], g["ident"][:, :])
                        last.then_inc(turned_full, 1)
                    if uv is not None:
                        qt, h = divmod(uv, HEADS)
                        pe.wait_ge(turned_copied, b * UNITS + uv + 1 + PTB)
                        if h == 0:
                            pe.wait_ge(out_done, b * ST + qt + 1)
                        for k in range(qt + 1):
                            last = nc.tensor.matmul(out_ps[:, qt % OB, h * HD:(h + 1) * HD],
                                                    probsT[:, uv % PTB, k, :], v[:, k, h * HD:(h + 1) * HD],
                                                    start=k == 0, stop=k == qt)
                        last.then_inc(value_done, 1)
                    if ot is not None:
                        turn(ot)
                turn(ST - 1)
                pe.wait_ge(front_done, b * NF + FRONT + at["t", ST - 1] + 1)
                for m in range(KD):
                    out = bank(("o", m))
                    for k in range(KD):
                        last = nc.tensor.matmul(out, w["o"][:, k, m * P:(m + 1) * P], attnT[:, k, :],
                                                start=k == 0, stop=k == KD - 1)
                    last.then_inc(front_full, 1)

        @block.scalar
        def _(act):
            act.sem_inc(front_done, FRONT)
            with act.Fori(0, B) as b:
                for n, (kind, m) in enumerate(front):
                    bank = front_ps[:, n % FRONT, :]
                    act.wait_ge(front_full, b * NF + n + 1)
                    if kind == "q":
                        if m == 0:
                            act.wait_ge(beta_done, b + 1)
                        op = nc.scalar.activation(qT[:, m, :], bank, ACT.Copy, scale=beta[:, 0:1])
                    elif kind == "k":
                        op = nc.scalar.activation(kT[:, m, :], bank, ACT.Copy)
                    elif kind == "v":
                        op = nc.scalar.activation(v[:, m, :], bank, ACT.Copy)
                    elif kind == "s":
                        qt, h = divmod(m, HEADS)
                        act.wait_ge(negmax_done, b * UNITS + m + 1)
                        act.wait_ge(turned_full, b * UNITS + m + 1)
                        op = nc.scalar.activation(probs[:, m % PSB, 0:P * (qt + 1)], bank[:, 0:P * (qt + 1)],
                                                  ACT.Exp, bias=negmax[:, m % 4:m % 4 + 1],
                                                  accum_out=rowsum[:, qt % 2, h:h + 1])
                    elif kind == "t":
                        op = nc.scalar.activation(attnT[:, :, m * P:(m + 1) * P],
                                                  bank.rearrange("p (k n) -> p k n", k=KD), ACT.Copy)
                    else:
                        op = nc.scalar.activation(g["condT"][:, m, bass.ds(b * S, S)], bank, ACT.Copy)
                    op.then_inc(front_done, 1)

        @block.vector
        def _(dve):
            dve.sem_inc(turned_copied, PTB)
            dve.sem_inc(turned_full, PSB)
            dve.sem_inc(value_done, PTB)
            dve.sem_inc(out_done, OB)
            with dve.Fori(0, B) as b:
                dve.wait_ge(beta_in, b * 16 + 16)
                nc.vector.tensor_scalar(beta[:, :], cond[:, :], 4.0, float(HD) ** -0.5, ALU.min, ALU.mult
                                        ).then_inc(beta_done, 1)
                for u, ut, uv, _ in steps:
                    if u is not None:
                        n = P * (u // HEADS + 1)
                        dve.wait_ge(front_full, b * NF + at["s", u] + 1)
                        nc.vector.tensor_reduce(negmax[:, u % 4:u % 4 + 1], front_ps[:, at["s", u] % FRONT, 0:n],
                                                AX.X, ALU.max, negate=True).then_inc(negmax_done, 1)
                    if ut is not None:
                        n = ut // HEADS + 1
                        dve.wait_ge(turned_full, b * UNITS + ut + 1 + PSB)
                        dve.wait_ge(value_done, b * UNITS + ut + 1)
                        nc.vector.tensor_copy(probsT[:, ut % PTB, 0:n, :], turned_ps[:, ut % PTB, 0:n, :]
                                              ).then_inc(turned_copied, 1)
                    if uv is not None and uv % HEADS == HEADS - 1:
                        qt = uv // HEADS
                        dve.wait_ge(front_done, b * NF + FRONT + at["s", uv] + 1)
                        nc.vector.reciprocal(rinv[:, qt % 2, :], rowsum[:, qt % 2, :]).then_inc(rinv_done, 1)
                        dve.wait_ge(rinv_done, b * ST + qt + 1)
                        dve.wait_ge(value_done, b * UNITS + uv + 1 + PTB)
                        nc.vector.tensor_tensor(attn[:, qt % 2, :].rearrange("p (h d) -> p h d", h=HEADS),
                                                out_ps[:, qt % OB, :].rearrange("p (h d) -> p h d", h=HEADS),
                                                rinv[:, qt % 2, :].unsqueeze(2).to_broadcast([P, HEADS, HD]),
                                                ALU.mult).then_inc(out_done, 1)

        @block.gpsimd
        def _(pool):
            make_constants(nc, pool, g)


def make_constants(nc, pool, g):
    tiles = (g["ident"], g["identb"], g["mask"])
    for m in tiles:
        nc.gpsimd.memset(m[:, :], 0.0).then_inc(g["blank_done"], 1)
    pool.wait_ge(g["blank_done"], len(tiles))
    for m in tiles[:2]:
        nc.gpsimd.affine_select(out=m[:, :], in_=m[:, :], compare_op=ALU.not_equal, fill=1.0, base=0,
                                pattern=[[-1, P]], channel_multiplier=1).then_inc(g["ident_done"], 1)
    nc.gpsimd.affine_select(out=g["mask"][:, :], in_=g["mask"][:, :], compare_op=ALU.is_ge, fill=NEG, base=0,
                            pattern=[[-1, P]], channel_multiplier=1).then_inc(g["ident_done"], 2)


def experts(nc, d, g):
    STEP = 5
    SHARED = 2
    NS = SHARED * CH
    with ExitStack() as ctx:
        def sb(name, shape, dt):
            return ctx.enter_context(nc.sbuf_tensor(name, shape, dt))

        def sem(name):
            return ctx.enter_context(nc.semaphore(name))

        condT, x1T = g["condT"], g["x1T"]
        W = [sb(f"W{s}", [P, RCOLS], F32) for s in range(2)]
        slot_w = [sb(f"slot_w{s}", [P, T], F32) for s in range(2)]
        gate_w = [sb(f"gate_w{s}", [P, T], F32) for s in range(2)]
        xe = sb("xe", [P, 2, KD, CW], F32)
        sg = sb("sg", [P, 2, CW], F32)
        hu = sb("hu", [P, 3, CW], F32)
        hid = sb("hid", [P, 3, CW], F32)
        low = sb("low", [P, CW], F32)
        dlow = sb("dlow", [LR, CW], F32)
        wide = ctx.enter_context(nc.psum_tensor("wide", [P, 2, 2, CW], F32))
        xe_ps = ctx.enter_context(nc.psum_tensor("xe_ps", [P, 2, CW], F32))
        low_ps = ctx.enter_context(nc.psum_tensor("low_ps", [P, CW], F32))
        dlow_ps = ctx.enter_context(nc.psum_tensor("dlow_ps", [P, CW], F32))

        x_res_in = sem("x_res_in")
        w_in = [sem(f"w_in{s}") for s in range(2)]
        route_in = [sem(f"route_in{s}") for s in range(2)]
        scaled = sem("scaled")
        wide_full = sem("wide_full")
        wide_done = sem("wide_done")
        silu_done = sem("silu_done")
        hid_done = sem("hid_done")
        xe_full = sem("xe_full")
        xe_done = sem("xe_done")
        low_full = sem("low_full")
        low_done = sem("low_done")
        dlow_full = sem("dlow_full")
        dlow_done = sem("dlow_done")
        logits_full = sem("logits_full")
        routed_done = sem("routed_done")
        route_exp = sem("route_exp")
        route_ready = sem("route_ready")
        turned = sem("turned")
        turned_out = sem("turned_out")
        route_out = sem("route_out")
        inv_in = sem("inv_in")

        NT = T // P
        area = gate_w[1][:, :]
        area2 = gate_w[0][:, :]
        area3 = slot_w[1][:, :]
        score = area[:, 0:NT * E].rearrange("p (t e) -> p t e", t=NT)
        work = area[:, NT * E:2 * NT * E].rearrange("p (t e) -> p t e", t=NT)
        flat = area2[:, 0:NT * E].rearrange("p (t e) -> p t e", t=NT)
        eq = area2[:, NT * E:2 * NT * E].rearrange("p (t e) -> p t e", t=NT)
        soft = area3[:, 0:NT * (E + F)].rearrange("p (t e) -> p t e", t=NT)
        o = NT * (E + F)
        top = area3[:, o:o + NT * 8].rearrange("p (t e) -> p t e", t=NT)
        topi = area3[:, o + NT * 8:o + NT * 16].bitcast(U32).rearrange("p (t e) -> p t e", t=NT)
        topf = area3[:, o + NT * 16:o + NT * 24].rearrange("p (t e) -> p t e", t=NT)
        stat = area3[:, o + NT * 24:o + NT * 24 + NT * F]
        inv = area3[:, o + NT * 32:o + NT * 32 + E]
        routeT = slot_w[0][0:E + F, :]
        inv_i = hid[:, 0, 0:E].bitcast(I32)
        router_w = xe[:, 0, 0, 0:KD * E].rearrange("p (k e) -> p k e", k=KD)

        def wt(s, name, kt=None, cols=RC):
            a, z = cols[name]
            t = W[s][:, a:z]
            return t if kt is None else t.rearrange("p (k n) -> p k n", k=kt)

        block = ctx.enter_context(nc.Block())

        @block.sync
        def _(sp):
            for b in range(B):
                sp.dma_start(x1T[:, :, b * S:(b + 1) * S],
                             d["xT"][b, :, :].rearrange("(k p) s -> p k s", p=P)).then_inc(x_res_in, 16)
            for s in range(SHARED):
                sp.dma_start(W[s][:, 0:SCOLS], d["shared"][s, :, :]).then_inc(w_in[s], 16)
            sp.dma_start(router_w, d["router"].rearrange("(k p) e -> p k e", p=P)).then_inc(inv_in, 16)
            sp.dma_start(inv_i, d["inv"].to_broadcast([P, E])).then_inc(inv_in, 16)

            sp.wait_ge(turned_out, 4)
            sp.dma_start(d["route"], routeT).then_inc(route_out, 16)
            sp.wait_ge(route_out, 16)

            def load(f, s):
                if isinstance(f, int):
                    sp.dma_start(W[s][:, :], d["expert"][f, :, :]).then_inc(w_in[s], 16)
                    rows = d["route"][f * KR:(f + 1) * KR, :]
                    scalar = d["route"][E + f:E + f + 1, :]
                else:
                    sp.dma_start(W[s][:, :], d["expert"][bass.ds(f, 1), :, :].rearrange("a p n -> p (a n)")
                                 ).then_inc(w_in[s], 16)
                    rows = d["route"][bass.ds(f * KR, KR), :]
                    scalar = d["route"][bass.ds(f + E, 1), :]
                for half in range(2):
                    sp.dma_start(slot_w[s][half * LR:(half + 1) * LR, :],
                                 rows.unsqueeze(1).to_broadcast([KR, R, T])).then_inc(route_in[s], 16)
                sp.dma_start(gate_w[s][:, :], scalar.to_broadcast([P, T])).then_inc(route_in[s], 16)

            for s in range(2):
                sp.wait_ge(wide_done, 2 + STEP * CH * (s + 1))
                load(s, s)
            with sp.Fori(0, F // 2 - 1) as it:
                for s in range(2):
                    sp.wait_ge(wide_done, it * (2 * CH * STEP) + 2 + STEP * (NS + CH * (s + 1)))
                    load(it * 2 + 2 + s, s)

        def ring_of(c, m):
            return (c * STEP + m) % 2

        def shared_steps():
            return [(i, i // CH, i % CH) for i in range(NS)]

        def pair_steps():
            return [(i, i // CH, i % CH) for i in range(2 * CH)]

        @block.tensor
        def _(pe):
            pe.wait_ge(inv_in, 32)
            for t in range(NT):
                for k in range(KD):
                    last = nc.tensor.matmul(xe_ps[:, t // 8, (t % 8) * E:(t % 8 + 1) * E],
                                            condT[:, k, t * P:(t + 1) * P], router_w[:, k, :],
                                            start=k == 0, stop=k == KD - 1)
            last.then_inc(logits_full, 1)

            def gate_up(n, s, c, m, routed):
                i0, rows = IT[m]
                item = n * STEP + m
                pe.wait_ge(wide_done, item + 1)
                cols = RC if routed else SC
                x = xe[:, c % 2, :, :] if routed else condT[:, :, c * CW:(c + 1) * CW]
                ring = ring_of(c, m)
                for j, name in enumerate(("gate", "up")):
                    for k in range(KD):
                        last = nc.tensor.matmul(wide[0:rows, ring, j, :], wt(s, name, KD, cols)[:, k, i0:i0 + rows],
                                                x[:, k, :], start=k == 0, stop=not routed and k == KD - 1)
                if routed:
                    for j in range(2):
                        last = nc.tensor.matmul(wide[0:rows, ring, j, :],
                                                wt(s, "qb")[j * LR:(j + 1) * LR, i0:i0 + rows],
                                                low[j * LR:(j + 1) * LR, :], start=False, stop=True)
                last.then_inc(wide_full, 1)

            def project_slots(n, s, c):
                for m in range(KD):
                    pe.wait_ge(xe_done, (n - NS) * KD + m + 1)
                    nc.tensor.matmul(xe_ps[:, m % 2, :], wt(s, "mu")[0:LR, m * P:(m + 1) * P],
                                     slot_w[s][0:LR, c * CW:(c + 1) * CW], start=True, stop=True
                                     ).then_inc(xe_full, 1)

            def low_rank(n, s, c):
                pe.wait_ge(xe_done, (n - NS) * KD + KD + 2)
                for k in range(KD):
                    last = nc.tensor.matmul(low_ps[:, :], wt(s, "qa", KD)[:, k, :], xe[:, c % 2, k, :],
                                            start=k == 0, stop=k == KD - 1)
                last.then_inc(low_full, 1)

            def down(n, s, c, routed):
                cols = RC if routed else SC
                if routed:
                    pe.wait_ge(hid_done, (n - NS) * 3 + 3)
                    for m, (_, rows) in enumerate(IT):
                        last = nc.tensor.matmul(dlow_ps[0:LR, :], wt(s, "dqa", 3)[0:rows, m, :], hid[0:rows, m, :],
                                                start=m == 0, stop=m == 2)
                    last.then_inc(dlow_full, 1)
                else:
                    pe.wait_ge(wide_done, n * STEP + 3 + 2)
                for pair in range(2):
                    item = n * STEP + 3 + pair
                    pe.wait_ge(wide_done, item + 1)
                    ring = ring_of(c, 3 + pair)
                    for j in range(2):
                        h0 = (2 * pair + j) * P
                        for m, (_, rows) in enumerate(IT):
                            last = nc.tensor.matmul(wide[:, ring, j, :], wt(s, "down", 3, cols)[0:rows, m, h0:h0 + P],
                                                    hid[0:rows, m, :], start=m == 0, stop=not routed and m == 2)
                    if routed:
                        pe.wait_ge(dlow_done, n - NS + 1)
                        for j in range(2):
                            h0 = (2 * pair + j) * P
                            last = nc.tensor.matmul(wide[:, ring, j, :], wt(s, "dqb")[0:LR, h0:h0 + P], dlow[:, :],
                                                    start=False, stop=True)
                    last.then_inc(wide_full, 1)

            for n, s, c in shared_steps():
                if c == 0:
                    pe.wait_ge(w_in[s], 16)
                for m in range(3):
                    gate_up(n, s, c, m, False)
                if n == 1:
                    pe.wait_ge(route_ready, 1)
                    for q in range(4):
                        if q >= 2:
                            pe.wait_ge(turned_out, q - 1)
                        for t in range(4):
                            last = nc.tensor.transpose(xe_ps[0:E + F, q % 2, t * P:(t + 1) * P], soft[:, 4 * q + t, :],
                                                       g["ident"][:, :])
                        last.then_inc(turned, 1)
                if n == NS - 1:
                    pe.wait_ge(route_in[0], 48)
                    pe.wait_ge(w_in[0], 32)
                    project_slots(NS, 0, 0)
                    low_rank(NS, 0, 0)
                down(n, s, c, False)

            def pair(it, final):
                for i, s, c in pair_steps():
                    n = it * (2 * CH) + (NS + i)
                    gate_ready = it * 2 + (s + 1)
                    if c == 0:
                        pe.wait_ge(scaled, gate_ready)
                    pe.wait_ge(low_done, n - NS + 1)
                    gate_up(n, s, c, 0, True)
                    gate_up(n, s, c, 1, True)
                    following = not (final and i == 2 * CH - 1)
                    ns, ncx = ((i + 1) // CH) % 2, (i + 1) % CH
                    if following:
                        if ncx == 0:
                            loads = it + (1 if i + 1 < 2 * CH else 2)
                            pe.wait_ge(w_in[ns], loads * 16 + 16)
                            pe.wait_ge(route_in[ns], loads * 48)
                        project_slots(n + 1, ns, ncx)
                    gate_up(n, s, c, 2, True)
                    if following:
                        low_rank(n + 1, ns, ncx)
                    down(n, s, c, True)

            with pe.Fori(0, F // 2 - 1) as it:
                pair(it, False)
            pair(F // 2 - 1, True)

        @block.scalar
        def _(act):
            act.wait_ge(routed_done, 2)
            nc.scalar.activation(score, work, ACT.Exp).then_inc(route_exp, 1)

            def silus(n, c):
                for m, (_, rows) in enumerate(IT):
                    act.wait_ge(wide_full, n * STEP + m + 1)
                    nc.scalar.activation(sg[0:rows, ring_of(c, m), :], wide[0:rows, ring_of(c, m), 0, :], ACT.Silu
                                         ).then_inc(silu_done, 1)

            for n, s, c in shared_steps():
                if n == 1:
                    act.wait_ge(routed_done, g["second_exp_after"])
                    nc.scalar.activation(work, eq, ACT.Exp).then_inc(route_exp, 1)
                silus(n, c)
                if n == 1:
                    for q in range(4):
                        act.wait_ge(turned, q + 1)
                        nc.scalar.activation(routeT[:, q * CW:(q + 1) * CW], xe_ps[0:E + F, q % 2, :], ACT.Copy
                                             ).then_inc(turned_out, 1)

            def pair(it):
                for i, s, c in pair_steps():
                    silus(it * (2 * CH) + (NS + i), c)

            with act.Fori(0, F // 2) as it:
                pair(it)

        @block.gpsimd
        def _(pool):
            def scale_low_rank(s, loads):
                pool.wait_ge(w_in[s], loads * 16 + 16)
                nc.gpsimd.tensor_tensor(wt(s, "qb"), wt(s, "qb"), wt(s, "qscale"), ALU.mult)
                nc.gpsimd.tensor_tensor(wt(s, "dqb")[0:LR, :], wt(s, "dqb")[0:LR, :], wt(s, "dscale")[0:LR, :],
                                        ALU.mult).then_inc(scaled, 1)

            scale_low_rank(0, 1)

            def pair(it, final):
                for i, s, c in pair_steps():
                    n = it * (2 * CH) + (NS + i)
                    if c == 0:
                        pool.wait_ge(route_in[s], it * 48 + 48)
                    for m, (_, rows) in enumerate(IT):
                        pool.wait_ge(wide_done, n * STEP + m + 3)
                        nc.gpsimd.tensor_tensor(hid[0:rows, m, :], hu[0:rows, m, :],
                                                gate_w[s][0:rows, c * CW:(c + 1) * CW], ALU.mult
                                                ).then_inc(hid_done, 1)
                    if c == CH - 2:
                        if s == 0:
                            scale_low_rank(1, it + 1)
                        elif not final:
                            scale_low_rank(0, it + 2)

            with pool.Fori(0, F // 2 - 1) as it:
                pair(it, False)
            pair(F // 2 - 1, True)

        @block.vector
        def _(dve):
            dve.sem_inc(wide_done, 2)
            dve.sem_inc(xe_done, 2)
            done = [0]

            def link(op):
                done[0] += 1
                op.then_inc(routed_done, 1)
                dve.wait_ge(routed_done, done[0])

            def over(x, n):
                return x.unsqueeze(2).to_broadcast([P, x.shape[1], n])

            dve.wait_ge(inv_in, 32)
            dve.wait_ge(logits_full, 1)
            logits = xe_ps[:, :, :].rearrange("p b (t e) -> p (b t) e", e=E)
            link(nc.vector.tensor_reduce(stat[:, 0:NT], logits, AX.X, ALU.max))
            link(nc.vector.tensor_tensor(work, logits, over(stat[:, 0:NT], E), ALU.subtract))
            dve.wait_ge(route_exp, 1)
            link(nc.vector.tensor_reduce(stat[:, NT:2 * NT], score, AX.X, ALU.add))
            link(nc.vector.reciprocal(stat[:, 0:NT], stat[:, NT:2 * NT]))
            link(nc.vector.tensor_tensor(score, score, over(stat[:, 0:NT], E), ALU.mult))
            for t in range(NT):
                link(nc.vector.max(top[:, t, :], score[:, t, :]))
                link(nc.vector.max_index(topi[:, t, :], top[:, t, :], score[:, t, :]))
            link(nc.vector.tensor_copy(topf, topi))
            link(nc.vector.tensor_copy(inv, inv_i))
            inv_b = inv.unsqueeze(1).to_broadcast([P, NT, E])
            for j in range(TOPK):
                dst = flat if j == 0 else work
                link(nc.vector.tensor_tensor(eq, inv_b, topf[:, :, j:j + 1].to_broadcast([P, NT, E]), ALU.is_equal))
                link(nc.vector.tensor_tensor(dst, eq, top[:, :, j:j + 1].to_broadcast([P, NT, E]), ALU.mult))
                if j:
                    link(nc.vector.tensor_tensor(flat, flat, work, ALU.add))
            by_expert = "p t (f k) -> p (t f) k"
            link(nc.vector.tensor_reduce(soft[:, :, E:E + F], flat.rearrange("p t (f k) -> p t f k", k=KR), AX.X, ALU.add))
            link(nc.vector.tensor_scalar(eq, flat, 0.0, -1.0e9, ALU.is_equal, ALU.mult))
            link(nc.vector.tensor_tensor(eq, eq, flat, ALU.add))
            link(nc.vector.tensor_reduce(stat, eq.rearrange(by_expert, k=KR), AX.X, ALU.max))
            link(nc.vector.tensor_tensor(eq.rearrange(by_expert, k=KR), eq.rearrange(by_expert, k=KR), over(stat, KR),
                                         ALU.subtract))
            assert done[0] == g["second_exp_after"], done[0]

            def second_half():
                dve.wait_ge(route_exp, 2)
                link(nc.vector.tensor_reduce(stat, work.rearrange(by_expert, k=KR), AX.X, ALU.add))
                link(nc.vector.reciprocal(topf.rearrange("p t e -> p (t e)"), stat))
                nc.vector.tensor_tensor(soft[:, :, 0:E].rearrange("p t (f k) -> p t f k", k=KR),
                                        work.rearrange("p t (f k) -> p t f k", k=KR),
                                        topf.unsqueeze(3).to_broadcast([P, NT, F, KR]),
                                        ALU.mult).then_inc(route_ready, 1)

            def hidden(n, c, m, routed):
                rows = IT[m][1]
                ring = ring_of(c, m)
                dve.wait_ge(silu_done, n * 3 + m + 1)
                out = hu if routed else hid
                nc.vector.tensor_tensor(out[0:rows, m, :], wide[0:rows, ring, 1, :], sg[0:rows, ring, :], ALU.mult
                                        ).then_inc(wide_done, 1)

            def add_out(n, c):
                for pair in range(2):
                    dve.wait_ge(wide_full, n * STEP + 3 + pair + 1)
                    acc = x1T[:, 2 * pair:2 * pair + 2, c * CW:(c + 1) * CW]
                    nc.vector.tensor_tensor(acc, wide[:, ring_of(c, 3 + pair), :, :], acc, ALU.add
                                            ).then_inc(wide_done, 1)

            def add_x(n, c):
                for m in range(KD):
                    dve.wait_ge(xe_full, (n - NS) * KD + m + 1)
                    nc.vector.tensor_tensor(xe[:, c % 2, m, :], xe_ps[:, m % 2, :], condT[:, m, c * CW:(c + 1) * CW],
                                            ALU.add).then_inc(xe_done, 1)

            def weigh_low(n, s, c):
                dve.wait_ge(low_full, n - NS + 1)
                nc.vector.tensor_tensor(low[:, :], low_ps[:, :], slot_w[s][:, c * CW:(c + 1) * CW], ALU.mult
                                        ).then_inc(low_done, 1)

            def weigh_dlow(n, s, c):
                dve.wait_ge(dlow_full, n - NS + 1)
                nc.vector.tensor_tensor(dlow[:, :], dlow_ps[0:LR, :], slot_w[s][0:LR, c * CW:(c + 1) * CW], ALU.mult
                                        ).then_inc(dlow_done, 1)

            for n, s, c in shared_steps():
                if n == 0:
                    dve.wait_ge(x_res_in, 16 * B)
                if n == 1:
                    second_half()
                for m in range(3):
                    hidden(n, c, m, False)
                if n == NS - 1:
                    dve.wait_ge(route_in[0], 48)
                    add_x(NS, 0)
                    weigh_low(NS, 0, 0)
                add_out(n, c)

            def pair(it, final):
                for i, s, c in pair_steps():
                    n = it * (2 * CH) + (NS + i)
                    following = not (final and i == 2 * CH - 1)
                    ns, ncx = ((i + 1) // CH) % 2, (i + 1) % CH
                    hidden(n, c, 0, True)
                    hidden(n, c, 1, True)
                    if following:
                        add_x(n + 1, ncx)
                    hidden(n, c, 2, True)
                    if following:
                        if ncx == 0:
                            loads = it + (1 if i + 1 < 2 * CH else 2)
                            dve.wait_ge(route_in[ns], loads * 48)
                        weigh_low(n + 1, ns, ncx)
                    weigh_dlow(n, s, c)
                    add_out(n, c)

            with dve.Fori(0, F // 2 - 1) as it:
                pair(it, False)
            pair(F // 2 - 1, True)


def ffn(nc, d, g):
    NT = T // P
    GC = 4
    GW = L1I // GC
    with ExitStack() as ctx:
        def sb(name, shape, dt):
            return ctx.enter_context(nc.sbuf_tensor(name, shape, dt))

        def sem(name):
            return ctx.enter_context(nc.semaphore(name))

        x1T = g["x1T"]
        wgT = sb("wgT", [P, KD, L1I], BF16)
        wuT = sb("wuT", [P, KD, L1I], BF16)
        wdT = sb("wdT", [P, L1T, D], BF16)
        gscale = sb("gscale", [P, L1I], F32)
        uscale = sb("uscale", [P, L1I], F32)
        dscale = sb("dscale", [P, D], F32)
        idx = sb("idx", [P, L1T], I32)
        spare = g["condT"][:, :, :].rearrange("p k n -> p (k n)")
        raw = spare[:, 0:2 * L1I].rearrange("p (a n) -> p a n", a=2)
        scaled = sb("scaled_rows", [P, L1I], F32)
        step_of = sb("step_of", [P, L1I], F32)
        rowq = sb("rowq", [P, 2, L1I], BF16)
        colscale = sb("colscale", [P, 2 * L1T + KD], F32)
        amax = sb("amax", [P, 4], F32)
        rcp = sb("rcp", [P, 4], F32)
        condW = sb("condW", [P, KD, D], F32)
        condWb = sb("condWb", [P, 2, KD, D], F32)
        adA = sb("adA", [RANK, 2, D], F32)
        adB = sb("adB", [RANK, 2, D], F32)
        adS = sb("adS", [RANK, 2], F32)
        adBs = sb("adBs", [RANK, 2, D], F32)
        itok = sb("itok", [1, B], I32)
        xq = sb("xq", [P, D], BF16)
        xqT = sb("xqT", [P, KD, P], BF16)
        xs = sb("xs", [P, 4], F32)
        xr = sb("xr", [P, 2], F32)
        x1 = sb("x1", [P, 3, D], F32)
        zg = sb("zg", [P, 2, GW], F32)
        sg = sb("sg_l1", [P, 2, GW], F32)
        hid = spare[:, 2 * L1I:4 * L1I].rearrange("p (a n) -> p a n", a=2)
        hs = sb("hs", [P, 4], F32)
        hr = sb("hr", [P, 2], F32)
        hq = sb("hq", [P, L1I], BF16)
        hqT = sb("hqT", [P, L1T, P], BF16)
        fin = sb("fin", [P, 2, D], F32)

        xc_ps = ctx.enter_context(nc.psum_tensor("xc_ps", [P, D], F32))
        misc = ctx.enter_context(nc.psum_tensor("misc", [P, 2, 512], F32))
        gu = ctx.enter_context(nc.psum_tensor("gu", [P, 2, 2, 512], F32))
        out_ps = ctx.enter_context(nc.psum_tensor("out_ps_l1", [P, D], F32))

        idx_in = sem("idx_in")
        itok_in = sem("itok_in")
        condW_in = sem("condW_in")
        ad_in = [sem(f"ad_in{s}") for s in range(2)]
        row_in = [sem(f"row_in{s}") for s in range(2)]
        down_in = [sem(f"down_in{s}") for s in range(2)]
        dve_step = sem("dve_step")
        row_q = sem("row_q")
        misc_full = sem("misc_full")
        misc_done = sem("misc_done")
        scales_done = sem("scales_done")
        scales_out = sem("scales_out")
        scales_in = sem("scales_in")
        adb_done = sem("adb_done")
        wb_full = sem("wb_full")
        wb_done = sem("wb_done")
        xc_full = sem("xc_full")
        xq_done = sem("xq_done")
        gu_full = sem("gu_full")
        zg_done = sem("zg_done")
        silu_done = sem("silu_done_l1")
        gu_done = sem("gu_done")
        hq_done = sem("hq_done")
        out_full = sem("out_full")
        fin_done = sem("fin_done")
        stored = [sem(f"stored{s}") for s in range(2)]

        rows = [("gate", j) for j in range(L1T)] + [("up", j) for j in range(L1T)] + [("down", j) for j in range(KD)]
        fills = []
        for n, (kind, j) in enumerate(rows):
            nb = KD if kind != "down" else L1T
            for b0 in range(0, nb, 8):
                fills.append((n, b0, min(8, nb - b0)))
        NFILL = len(fills)
        def step_fills(i):
            out = []
            if i < NT:
                out.append(("x1", i))
            if 0 <= i - 1 < NT:
                out.append(("xq", i - 1))
            if 0 <= i - 2 < NT:
                out += [("hqa", i - 2), ("hqb", i - 2)]
            return out
        order = [f for i in range(NT + 2) for f in step_fills(i)]
        fill_at = {f: NFILL + n for n, f in enumerate(order)}

        block = ctx.enter_context(nc.Block())

        def bankb(n):
            return misc[:, n % 2, :].bitcast(BF16).rearrange("p (k n) -> p k n", n=P)

        @block.sync
        def _(sp):
            sp.dma_start(idx[:, :], d["didx"]).then_inc(idx_in, 16)
            sp.dma_start(itok[:, :], d["itok"]).then_inc(itok_in, 16)
            sp.dma_start(condW[:, :, :], d["condW"].rearrange("(k p) n -> p k n", p=P)).then_inc(condW_in, 16)
            sp.wait_ge(itok_in, 16)
            for b in range(B):
                s = b % 2
                if b >= 2:
                    sp.wait_ge(wb_done, 4 * (b - 1) + 2)
                a = sp.value_load(itok[0:1, b:b + 1], min_val=0, max_val=NA - 1)
                sp.dma_start(adA[:, s, :], d["adA"][bass.ds(a, 1), :, :].rearrange("a r n -> (a r) n")).then_inc(ad_in[s], 16)
                sp.dma_start(adB[:, s, :], d["adB"][bass.ds(a, 1), :, :].rearrange("a r n -> (a r) n")).then_inc(ad_in[s], 16)
                sp.dma_start(adS[:, s:s + 1], d["adS"][bass.ds(a, 1), :].to_broadcast([RANK, 1])).then_inc(ad_in[s], 16)
                if b == 1:
                    for n, (kind, j) in enumerate(rows):
                        if kind == "down":
                            sp.wait_ge(row_q, n - 1)
                            sp.dma_start(raw[:, n % 2, :], d["wdown"][j * P:(j + 1) * P, :]
                                         ).then_inc(down_in[j % 2], 16)
                    sp.wait_ge(row_q, len(rows))
                    sp.dma_start(d["scales"].rearrange("j p -> p j"), colscale[:, :],
                                 allow_slow_non_contiguous=True).then_inc(scales_out, 16)
                    sp.wait_ge(scales_out, 16)
                    flat = d["scales"].rearrange("j p -> (j p)").unsqueeze(0)
                    sp.dma_start(gscale[:, :], flat[:, 0:L1I].to_broadcast([P, L1I])).then_inc(scales_in, 16)
                    sp.dma_start(uscale[:, :], flat[:, L1I:2 * L1I].to_broadcast([P, L1I])).then_inc(scales_in, 16)
                    sp.dma_start(dscale[:, :], flat[:, 2 * L1I:2 * L1I + D].to_broadcast([P, D])).then_inc(scales_in, 16)
            for t in range(NT):
                sp.wait_ge(fin_done, t + 1)
                sp.dma_start(d["out"][t * P:(t + 1) * P, :], fin[:, t % 2, :]).then_inc(stored[t % 2], 16)
            for s in range(2):
                sp.wait_ge(stored[s], 16 * (NT // 2))

        @block.gpsimd
        def _(pool):
            pool.wait_ge(idx_in, 16)
            for n, (kind, j) in enumerate(rows):
                if kind == "down":
                    break
                if n >= 2:
                    pool.wait_ge(row_q, n - 1)
                nc.gpsimd.indirect_dma_start(
                    raw[:, n % 2, 0:D], None, d["w" + kind],
                    bass.IndirectOffsetOnAxis(ap=idx[:, j:j + 1].bitcast(U32), axis=0)).then_inc(row_in[n % 2], 16)

        @block.vector
        def _(dve):
            count = [0]

            def link(op):
                count[0] += 1
                op.then_inc(dve_step, 1)
                dve.wait_ge(dve_step, count[0])

            dve.sem_inc(misc_done, 2)
            dve.sem_inc(wb_done, 2)

            def scale_of(src, scale, r, j):
                link(nc.vector.tensor_reduce(amax[:, j:j + 1], src, AX.X, ALU.max, apply_absolute_value=True))
                link(nc.vector.tensor_scalar(scale, amax[:, j:j + 1], 1.0 / FP8_MAX, None, ALU.mult))
                link(nc.vector.reciprocal(r, scale))

            def round_fp8(out, src, r, n):
                y, st = scaled[:, 0:n], step_of[:, 0:n]
                link(nc.vector.tensor_scalar(y, src, r, None, ALU.mult))
                link(nc.vector.tensor_scalar(st.bitcast(U32), y.bitcast(U32), 0x7F800000, None, ALU.bitwise_and))
                link(nc.vector.tensor_scalar(st, st, 2.0 ** -6, 1.5 * 2.0 ** 20, ALU.max, ALU.mult))
                link(nc.vector.tensor_tensor(y, y, st, ALU.add))
                return nc.vector.tensor_tensor(out, y, st, ALU.subtract)

            for n, (kind, j) in enumerate(rows):
                s = n % 2
                wd = L1I if kind == "down" else D
                if kind == "down":
                    dve.wait_ge(down_in[s], 16 * (j // 2 + 1))
                else:
                    dve.wait_ge(row_in[s], 16 * (n // 2 + 1))
                scale_of(raw[:, s, 0:wd], colscale[:, n:n + 1], rcp[:, 0:1], 0)
                if n >= 2:
                    dve.wait_ge(misc_full, max(f for f, (m, _, _) in enumerate(fills) if m == n - 2) + 1)
                round_fp8(rowq[:, s, 0:wd], raw[:, s, 0:wd], rcp[:, 0:1], wd).then_inc(row_q, 1)

            def conditioned(b):
                s = b % 2
                dve.wait_ge(ad_in[s], 48 * (b // 2 + 1))
                nc.vector.tensor_scalar(adBs[:, s, :], adB[:, s, :], adS[:, s:s + 1], None, ALU.mult
                                        ).then_inc(adb_done, 1)
                if b == 0:
                    dve.wait_ge(condW_in, 16)
                for k in range(KD):
                    dve.wait_ge(wb_full, 4 * b + k + 1)
                    nc.vector.tensor_tensor(condWb[:, s, k, :], gu[:, k % 2, 0, :], condW[:, k, :], ALU.add
                                            ).then_inc(wb_done, 1)

            def quantise_x(t):
                dve.wait_ge(xc_full, t + 1)
                scale_of(xc_ps[:, :], xs[:, t % 4:t % 4 + 1], xr[:, t % 2:t % 2 + 1], 1)
                if t >= 1:
                    dve.wait_ge(misc_full, fill_at["xq", t - 1] + 1)
                round_fp8(xq[:, :], xc_ps[:, :], xr[:, t % 2:t % 2 + 1], D).then_inc(xq_done, 1)

            def gate_up(t):
                for c in range(GC):
                    n = t * GC + c
                    cols = slice(c * GW, (c + 1) * GW)
                    dve.wait_ge(gu_full, n + 1)
                    nc.vector.tensor_tensor(zg[:, n % 2, :], gu[:, n % 2, 0, 0:GW], gscale[:, cols], ALU.mult
                                            ).then_inc(zg_done, 1)
                    link(nc.vector.scalar_tensor_tensor(hid[:, t % 2, cols], gu[:, n % 2, 1, 0:GW],
                                                        xs[:, t % 4:t % 4 + 1], uscale[:, cols], ALU.mult, ALU.mult))
                    dve.wait_ge(silu_done, n + 1)
                    nc.vector.tensor_tensor(hid[:, t % 2, cols], hid[:, t % 2, cols], sg[:, n % 2, :], ALU.mult
                                            ).then_inc(gu_done, 1)
                dve.wait_ge(gu_done, 2 + t * GC + GC)

            def quantise_hidden(t):
                scale_of(hid[:, t % 2, :], hs[:, t % 4:t % 4 + 1], hr[:, t % 2:t % 2 + 1], 2)
                if t >= 1:
                    dve.wait_ge(misc_full, fill_at["hqb", t - 1] + 1)
                round_fp8(hq[:, :], hid[:, t % 2, :], hr[:, t % 2:t % 2 + 1], L1I).then_inc(hq_done, 1)

            def finish(t):
                dve.wait_ge(out_full, t + 1)
                if t >= 2:
                    dve.wait_ge(stored[t % 2], 16 * (t // 2))
                link(nc.vector.scalar_tensor_tensor(fin[:, t % 2, :], out_ps[:, :], hs[:, t % 4:t % 4 + 1],
                                                    dscale[:, :], ALU.mult, ALU.mult))
                dve.wait_ge(misc_done, 2 + fill_at["x1", t] + 1)
                nc.vector.tensor_tensor(fin[:, t % 2, :], fin[:, t % 2, :], x1[:, t % 3, :], ALU.add
                                        ).then_inc(fin_done, 1)

            dve.sem_inc(gu_done, 2)
            conditioned(0)
            dve.wait_ge(scales_in, 48)
            for i in range(NT + 2):
                if i < NT:
                    if i % ST == 0 and i:
                        conditioned(i // ST)
                    quantise_x(i)
                if 0 <= i - 1 < NT:
                    gate_up(i - 1)
                    quantise_hidden(i - 1)
                if 0 <= i - 2 < NT:
                    finish(i - 2)

        @block.scalar
        def _(act):
            def take(n):
                act.wait_ge(misc_full, n + 1)

            for n, (m, b0, nb) in enumerate(fills):
                kind, j = rows[m]
                take(n)
                dst = {"gate": wgT, "up": wuT, "down": wdT}[kind]
                nc.scalar.activation(dst[:, b0:b0 + nb, j * P:(j + 1) * P], bankb(n)[:, 0:nb, :], ACT.Copy
                                     ).then_inc(misc_done, 1)

            def silus(t):
                for c in range(GC):
                    n = t * GC + c
                    act.wait_ge(zg_done, n + 1)
                    act.wait_ge(gu_done, n + 1)
                    nc.scalar.activation(sg[:, n % 2, :], zg[:, n % 2, :], ACT.Silu, scale=xs[:, t % 4:t % 4 + 1]
                                         ).then_inc(silu_done, 1)

            for i in range(NT + 2):
                for f in step_fills(i):
                    n = fill_at[f]
                    take(n)
                    kind, t = f
                    if kind == "x1":
                        if t >= 3:
                            act.wait_ge(fin_done, t - 2)
                        op = nc.scalar.activation(x1[:, t % 3, :], misc[:, n % 2, :], ACT.Copy)
                    elif kind == "xq":
                        op = nc.scalar.activation(xqT[:, :, :], bankb(n)[:, 0:KD, :], ACT.Copy)
                    elif kind == "hqa":
                        op = nc.scalar.activation(hqT[:, 0:8, :], bankb(n), ACT.Copy)
                    else:
                        op = nc.scalar.activation(hqT[:, 8:L1T, :], bankb(n)[:, 0:L1T - 8, :], ACT.Copy)
                    op.then_inc(misc_done, 1)
                    if kind == "xq":
                        silus(t)

        @block.tensor
        def _(pe):
            def bank_free(n):
                pe.wait_ge(misc_done, n + 1)

            for n, (m, b0, nb) in enumerate(fills):
                bank_free(n)
                pe.wait_ge(row_q, m + 1)
                for k in range(nb):
                    last = nc.tensor.transpose(bankb(n)[:, k, :], rowq[:, m % 2, (b0 + k) * P:(b0 + k + 1) * P],
                                               g["identb"][:, :])
                last.then_inc(misc_full, 1)

            def conditioned(b):
                s = b % 2
                pe.wait_ge(adb_done, b + 1)
                for k in range(KD):
                    pe.wait_ge(wb_done, 4 * b + k + 1)
                    nc.tensor.matmul(gu[:, k % 2, 0, :], adA[:, s, k * P:(k + 1) * P], adBs[:, s, :],
                                     start=True, stop=True).then_inc(wb_full, 1)
                pe.wait_ge(wb_done, 4 * b + 4 + 2)

            def project(t):
                if t >= 1:
                    pe.wait_ge(xq_done, t)
                for k in range(KD):
                    last = nc.tensor.matmul(xc_ps[:, :], x1T[:, k, t * P:(t + 1) * P], condWb[:, (t // ST) % 2, k, :],
                                            start=k == 0, stop=k == KD - 1)
                last.then_inc(xc_full, 1)
                n = fill_at["x1", t]
                bank_free(n)
                for k in range(KD):
                    last = nc.tensor.transpose(misc[:, n % 2, k * P:(k + 1) * P], x1T[:, k, t * P:(t + 1) * P],
                                               g["ident"][:, :])
                last.then_inc(misc_full, 1)

            def gate_up(t):
                n = fill_at["xq", t]
                bank_free(n)
                pe.wait_ge(xq_done, t + 1)
                for k in range(KD):
                    last = nc.tensor.transpose(bankb(n)[:, k, :], xq[:, k * P:(k + 1) * P], g["identb"][:, :])
                last.then_inc(misc_full, 1)
                pe.wait_ge(misc_done, 2 + n + 1)
                for c in range(GC):
                    m = t * GC + c
                    pe.wait_ge(gu_done, m + 1)
                    for j, wT in enumerate((wgT, wuT)):
                        for k in range(KD):
                            last = nc.tensor.matmul(gu[:, m % 2, j, 0:GW], xqT[:, k, :], wT[:, k, c * GW:(c + 1) * GW],
                                                    start=k == 0, stop=k == KD - 1)
                    last.then_inc(gu_full, 1)

            def down(t):
                pe.wait_ge(hq_done, t + 1)
                for kind, k0, nb in (("hqa", 0, 8), ("hqb", 8, L1T - 8)):
                    n = fill_at[kind, t]
                    bank_free(n)
                    for k in range(nb):
                        last = nc.tensor.transpose(bankb(n)[:, k, :], hq[:, (k0 + k) * P:(k0 + k + 1) * P],
                                                   g["identb"][:, :])
                    last.then_inc(misc_full, 1)
                pe.wait_ge(misc_done, 2 + fill_at["hqb", t] + 1)
                if t >= 1:
                    pe.wait_ge(fin_done, t)
                for k in range(L1T):
                    last = nc.tensor.matmul(out_ps[:, :], hqT[:, k, :], wdT[:, k, :], start=k == 0, stop=k == L1T - 1)
                last.then_inc(out_full, 1)

            conditioned(0)
            for i in range(NT + 2):
                if i < NT:
                    if i % ST == 0 and i:
                        pe.wait_ge(gu_done, 2 + (i - 1) * GC)
                        conditioned(i // ST)
                    project(i)
                if 0 <= i - 1 < NT:
                    gate_up(i - 1)
                if 0 <= i - 2 < NT:
                    down(i - 2)


def build(nc, d):
    with ExitStack() as ctx:
        g = {
            "ident": ctx.enter_context(nc.sbuf_tensor("ident", [P, P], F32)),
            "identb": ctx.enter_context(nc.sbuf_tensor("identb", [P, P], BF16)),
            "mask": ctx.enter_context(nc.sbuf_tensor("mask", [P, P], BF16)),
            "condT": ctx.enter_context(nc.sbuf_tensor("condT", [P, KD, T], F32)),
            "blank_done": ctx.enter_context(nc.semaphore("blank_done")),
            "ident_done": ctx.enter_context(nc.semaphore("ident_done")),
            "second_exp_after": 5 + 2 * (T // P) + 2 + 3 * TOPK - 1 + 5,
        }
        attend(nc, d, g)
        g["x1T"] = ctx.enter_context(nc.sbuf_tensor("x1T", [P, KD, T], F32))
        experts(nc, d, g)
        ffn(nc, d, g)


def kernel(**x):
    import numpy as np
    import concourse.bacc as bacc
    from concourse.bass_utils import run_bass_kernel_spmd

    a = {k: np.asarray(v) for k, v in x.items()}

    def tiles(w, rows):
        full = np.zeros((rows * P,) + w.shape[1:], w.dtype)
        full[:w.shape[0]] = w
        return full.reshape(rows, P, -1).transpose(1, 0, 2).reshape(P, -1)

    def spread(w):
        full = np.zeros((P, w.shape[1]), w.dtype)
        full[:w.shape[0]] = w
        return full

    def repeated(row, n):
        return np.broadcast_to(row[None, :], (n, row.shape[0]))

    def low_rows(w):
        return w.transpose(0, 2, 1).reshape(LR, -1)

    packed = []
    for f in range(F):
        q = "L0_ffn_"
        mu = np.zeros((LR, D), np.float32)
        mu[::R] = a[q + "mask_up_W"][f].T
        qa = np.concatenate([a[q + n + "_qa"][f].reshape(LR, D) for n in ("gate", "up")]).T
        packed.append(np.concatenate([
            tiles(a[q + "gate_W"][f].T, KD), tiles(a[q + "up_W"][f].T, KD), tiles(a[q + "down_W"][f].T, 3),
            tiles(qa, KD), tiles(a[q + "down_qa"][f].reshape(LR, I).T, 3),
            np.concatenate([low_rows(a[q + n + "_qb"][f]) for n in ("gate", "up")]),
            np.concatenate([repeated(a[q + n + "_scale"][f], LR) for n in ("gate", "up")]),
            spread(mu), spread(low_rows(a[q + "down_qb"][f])), spread(repeated(a[q + "down_scale"][f], LR)),
        ], axis=1))
    shared = []
    for s in range(2):
        i = slice(s * I, (s + 1) * I)
        shared.append(np.concatenate([
            tiles(a["L0_ffn_sh_gate_W"][i].T, KD), tiles(a["L0_ffn_sh_up_W"][i].T, KD),
            tiles(a["L0_ffn_sh_down_W"][:, i].T, 3)], axis=1))
    arrays = {
        "xT": a["x"].transpose(0, 2, 1),
        "cond": a["cond_1"].reshape(B, 1),
        "Wq": a["L0_cond_Wq"].T, "Wk": a["L0_cond_Wk"].T, "Wv": a["L0_cond_Wv"].T, "Wo": a["L0_cond_Wo"].T,
        "router": a["L0_ffn_gate_weight"].T,
        "inv": a["L0_ffn_inv_mapping"].reshape(1, E),
        "expert": np.stack(packed),
        "shared": np.stack(shared),
        "didx": a["L1_ffn_down_reorder_index"].reshape(L1T, P).T,
        "itok": a["itok_B_0_6"].reshape(1, B),
        "condW": a["L1_cond_W"].T,
        "adA": a["L1_cond_A"],
        "adB": a["L1_cond_Bm"].transpose(0, 2, 1),
        "adS": a["L1_cond_scalings"].reshape(NA, 1),
        "wgate": a["L1_ffn_w_gate"], "wup": a["L1_ffn_w_up"], "wdown": a["L1_ffn_w_down"],
    }
    arrays = {"in_" + k: np.ascontiguousarray(v) for k, v in arrays.items()}
    nc = bacc.Bacc("TRN2", target_bir_lowering=False, num_devices=1)
    d = {k[3:]: nc.dram_tensor(k, v.shape, mybir.dt.from_np(v.dtype), kind="ExternalInput").ap()
         for k, v in arrays.items()}
    d["route"] = nc.dram_tensor("route", [E + F, T], F32, kind="Internal").ap()
    d["scales"] = nc.dram_tensor("scales", [2 * L1T + KD, P], F32, kind="Internal").ap()
    d["out"] = nc.dram_tensor("out", [T, D], F32, kind="ExternalOutput").ap()
    build(nc, d)
    got = run_bass_kernel_spmd(nc, [arrays], core_ids=[0])
    return got.results[0]["out"].reshape(B, S, D)
```

```python
from contextlib import ExitStack

import concourse.bass as bass
from concourse import mybir

F32 = mybir.dt.float32
F32R = mybir.dt.float32r
BF16 = mybir.dt.bfloat16
U32 = mybir.dt.uint32
I32 = mybir.dt.int32
ALU = mybir.AluOpType
ACT = mybir.ActivationFunctionType
AX = mybir.AxisListType

P = 128
B, S, D = 4, 512, 512
T = B * S
KD = D // P
ST = S // P
HEADS, HD = 16, 32
HPT = P // HD
F, KR, R, I = 8, 8, 8, 352
LR = KR * R
E = F * KR
TOPK = 6
IT = [(0, 128), (128, 128), (256, 96)]
NEG = -1.0e30
L1I = 1408
L1T = L1I // P
NA, RANK = 8, 16
FP8_MAX = 448.0
CH = 4
CW = 512

def columns(cols):
    at, out = 0, {}
    for name, n in cols:
        out[name] = (at, at + n)
        at += n
    return out, at


AC, ACOLS = columns([("gate", KD * I), ("up", KD * I), ("qb", 2 * I), ("qscale", 2 * I)])
BC, BCOLS = columns([("down", 3 * D), ("dqa", 3 * 2 * LR), ("dqb", D), ("dscale", D)])
CC, CCOLS = columns([("mu", D), ("qa", KD * 2 * LR)])


def attend(nc, d, g):
    UNITS = ST * HEADS
    FRONT, QT, PTB, PSB, OB = 4, 4, 2, 4, 2
    LAG_T, LAG_V = 2, 3

    front = [("q", m) for m in range(KD)] + [("k", m) for m in range(KD)] + [("v", m) for m in range(ST)]
    steps = []
    for i in range(UNITS + LAG_V):
        turn = None
        j = i - LAG_V - 2
        if i < UNITS and j >= 0 and j % HEADS == HEADS - 1:
            turn = j // HEADS
        steps.append((i if i < UNITS else None, i - LAG_T if 0 <= i - LAG_T < UNITS else None,
                      i - LAG_V if i >= LAG_V else None, turn))
    for u, _, _, turn in steps:
        if u is not None:
            front.append(("s", u))
        if turn is not None:
            front.append(("t", turn))
    front.append(("t", ST - 1))
    front += [("o", m) for m in range(KD)]
    at = {item: n for n, item in enumerate(front)}
    NF = len(front)
    assert NF % FRONT == 0

    with ExitStack() as ctx:
        def sb(name, shape, dt):
            return ctx.enter_context(nc.sbuf_tensor(name, shape, dt))

        def sem(name):
            return ctx.enter_context(nc.semaphore(name))

        g["mask"] = sb("mask", [P, P], BF16)
        w = {n: sb("w_" + n, [P, KD, D], F32) for n in "qkvo"}
        xT = sb("xT", [P, KD, S], F32)
        qT = sb("qT", [P, KD, S], F32)
        kT = sb("kT", [P, KD, S], F32)
        v = sb("v", [P, ST, D], F32)
        probs = sb("probs", [P, PSB, S], F32)
        probsT = sb("probsT", [P, PTB, ST, P], F32)
        attn = sb("attn", [P, 2, D], F32)
        attnT = sb("attnT", [P, KD, S], F32)
        negmax = sb("negmax", [P, 4], F32)
        rowsum = sb("rowsum", [P, 2, HEADS], F32)
        rinv = sb("rinv", [P, 2, HEADS], F32)
        cond = sb("cond", [P, 1], F32)
        beta = sb("beta", [P, 1], F32)
        front_ps = ctx.enter_context(nc.psum_tensor("front_ps", [P, FRONT, 512], F32))
        turned_ps = ctx.enter_context(nc.psum_tensor("turned_ps", [P, PTB, ST, P], F32))
        out_ps = ctx.enter_context(nc.psum_tensor("out_ps", [P, OB, D], F32))

        attn_w_in = sem("attn_w_in")
        x_in = sem("x_in")
        beta_in = sem("beta_in")
        beta_done = sem("beta_done")
        front_full = sem("front_full")
        front_done = sem("front_done")
        negmax_done = sem("negmax_done")
        turned_full = sem("turned_full")
        turned_copied = sem("turned_copied")
        value_done = sem("value_done")
        rinv_done = sem("rinv_done")
        out_done = sem("out_done")

        block = ctx.enter_context(nc.Block())

        @block.sync
        def _(sp):
            for n in "qkvo":
                sp.dma_start(w[n][:, :, :], d["W" + n].rearrange("(k p) n -> p k n", p=P)).then_inc(attn_w_in, 16)
            sp.dma_start(cond[:, :], d["cond"][0:1, :].to_broadcast([P, 1])).then_inc(beta_in, 16)
            sp.dma_start(xT[:, :, :], d["xT"][0, :, :].rearrange("(k p) n -> p k n", p=P)).then_inc(x_in, 16)
            with sp.Fori(0, B - 1) as b:
                sp.wait_ge(front_done, b * NF + FRONT + at["v", ST - 1] + 1)
                sp.dma_start(cond[:, :], d["cond"][bass.ds(b + 1, 1), :].to_broadcast([P, 1])).then_inc(beta_in, 16)
                sp.dma_start(xT[:, :, :], d["xT"][bass.ds(b + 1, 1), :, :].rearrange("a (k p) n -> p (a k) n", p=P)
                             ).then_inc(x_in, 16)

        @block.tensor
        def _(pe):
            pe.wait_ge(g["ident_done"], 4)
            pe.wait_ge(attn_w_in, 64)
            with pe.Fori(0, B) as b:
                def bank(item):
                    pe.wait_ge(front_done, b * NF + at[item] + 1)
                    return front_ps[:, at[item] % FRONT, :]

                pe.wait_ge(x_in, b * 16 + 16)
                for n in "qk":
                    for m in range(KD):
                        out = bank((n, m))
                        for k in range(KD):
                            last = nc.tensor.matmul(out, w[n][:, k, m * P:(m + 1) * P], xT[:, k, :],
                                                    start=k == 0, stop=k == KD - 1)
                        last.then_inc(front_full, 1)
                for m in range(ST):
                    out = bank(("v", m))
                    for k in range(KD):
                        last = nc.tensor.matmul(out, xT[:, k, m * P:(m + 1) * P], w["v"][:, k, :],
                                                start=k == 0, stop=k == KD - 1)
                    last.then_inc(front_full, 1)
                pe.wait_ge(front_done, b * NF + FRONT + at["v", ST - 1] + 1)

                def turn(qt):
                    out = bank(("t", qt))
                    pe.wait_ge(out_done, b * ST + qt + 1 + OB)
                    for k in range(KD):
                        last = nc.tensor.transpose(out[:, k * P:(k + 1) * P],
                                                   attn[:, qt % 2, k * P:(k + 1) * P], g["ident"][:, :])
                    last.then_inc(front_full, 1)

                for u, ut, uv, ot in steps:
                    if u is not None:
                        qt, h = divmod(u, HEADS)
                        r, c, n = HD * (h % HPT), h // HPT, P * (qt + 1)
                        out = bank(("s", u))
                        nc.tensor.matmul(out[:, 0:n], qT[r:r + HD, c, qt * P:(qt + 1) * P],
                                         kT[r:r + HD, c, 0:n], start=True, stop=False)
                        nc.tensor.matmul(out[:, n - P:n], g["identb"][:, :], g["mask"][:, :],
                                         start=False, stop=True).then_inc(front_full, 1)
                    if ut is not None:
                        qt = ut // HEADS
                        pe.wait_ge(front_done, b * NF + FRONT + at["s", ut] + 1)
                        pe.wait_ge(turned_copied, b * UNITS + ut + 1)
                        for k in range(qt + 1):
                            last = nc.tensor.transpose(turned_ps[:, ut % PTB, k, :],
                                                       probs[:, ut % PSB, k * P:(k + 1) * P], g["ident"][:, :])
                        last.then_inc(turned_full, 1)
                    if uv is not None:
                        qt, h = divmod(uv, HEADS)
                        pe.wait_ge(turned_copied, b * UNITS + uv + 1 + PTB)
                        if h == 0:
                            pe.wait_ge(out_done, b * ST + qt + 1)
                        for k in range(qt + 1):
                            last = nc.tensor.matmul(out_ps[:, qt % OB, h * HD:(h + 1) * HD],
                                                    probsT[:, uv % PTB, k, :], v[:, k, h * HD:(h + 1) * HD],
                                                    start=k == 0, stop=k == qt)
                        last.then_inc(value_done, 1)
                    if ot is not None:
                        turn(ot)
                turn(ST - 1)
                pe.wait_ge(front_done, b * NF + FRONT + at["t", ST - 1] + 1)
                for m in range(KD):
                    out = bank(("o", m))
                    for k in range(KD):
                        last = nc.tensor.matmul(out, w["o"][:, k, m * P:(m + 1) * P], attnT[:, k, :],
                                                start=k == 0, stop=k == KD - 1)
                    last.then_inc(front_full, 1)

        @block.scalar
        def _(act):
            act.sem_inc(front_done, FRONT)
            with act.Fori(0, B) as b:
                for n, (kind, m) in enumerate(front):
                    bank = front_ps[:, n % FRONT, :]
                    act.wait_ge(front_full, b * NF + n + 1)
                    if kind == "q":
                        if m == 0:
                            act.wait_ge(beta_done, b + 1)
                        op = nc.scalar.activation(qT[:, m, :], bank, ACT.Copy, scale=beta[:, 0:1])
                    elif kind == "k":
                        op = nc.scalar.activation(kT[:, m, :], bank, ACT.Copy)
                    elif kind == "v":
                        op = nc.scalar.activation(v[:, m, :], bank, ACT.Copy)
                    elif kind == "s":
                        qt, h = divmod(m, HEADS)
                        act.wait_ge(negmax_done, b * UNITS + m + 1)
                        act.wait_ge(turned_full, b * UNITS + m + 1)
                        op = nc.scalar.activation(probs[:, m % PSB, 0:P * (qt + 1)], bank[:, 0:P * (qt + 1)],
                                                  ACT.Exp, bias=negmax[:, m % 4:m % 4 + 1],
                                                  accum_out=rowsum[:, qt % 2, h:h + 1])
                    elif kind == "t":
                        op = nc.scalar.activation(attnT[:, :, m * P:(m + 1) * P],
                                                  bank.rearrange("p (k n) -> p k n", k=KD), ACT.Copy)
                    else:
                        op = nc.scalar.activation(g["condT"][:, m, bass.ds(b * S, S)], bank, ACT.Copy)
                    op.then_inc(front_done, 1)

        @block.vector
        def _(dve):
            dve.sem_inc(turned_copied, PTB)
            dve.sem_inc(turned_full, PSB)
            dve.sem_inc(value_done, PTB)
            dve.sem_inc(out_done, OB)
            with dve.Fori(0, B) as b:
                dve.wait_ge(beta_in, b * 16 + 16)
                nc.vector.tensor_scalar(beta[:, :], cond[:, :], 4.0, float(HD) ** -0.5, ALU.min, ALU.mult
                                        ).then_inc(beta_done, 1)
                for u, ut, uv, _ in steps:
                    if u is not None:
                        n = P * (u // HEADS + 1)
                        dve.wait_ge(front_full, b * NF + at["s", u] + 1)
                        nc.vector.tensor_reduce(negmax[:, u % 4:u % 4 + 1], front_ps[:, at["s", u] % FRONT, 0:n],
                                                AX.X, ALU.max, negate=True).then_inc(negmax_done, 1)
                    if ut is not None:
                        n = ut // HEADS + 1
                        dve.wait_ge(turned_full, b * UNITS + ut + 1 + PSB)
                        dve.wait_ge(value_done, b * UNITS + ut + 1)
                        nc.vector.tensor_copy(probsT[:, ut % PTB, 0:n, :], turned_ps[:, ut % PTB, 0:n, :]
                                              ).then_inc(turned_copied, 1)
                    if uv is not None and uv % HEADS == HEADS - 1:
                        qt = uv // HEADS
                        dve.wait_ge(front_done, b * NF + FRONT + at["s", uv] + 1)
                        nc.vector.reciprocal(rinv[:, qt % 2, :], rowsum[:, qt % 2, :]).then_inc(rinv_done, 1)
                        dve.wait_ge(rinv_done, b * ST + qt + 1)
                        dve.wait_ge(value_done, b * UNITS + uv + 1 + PTB)
                        nc.vector.tensor_tensor(attn[:, qt % 2, :].rearrange("p (h d) -> p h d", h=HEADS),
                                                out_ps[:, qt % OB, :].rearrange("p (h d) -> p h d", h=HEADS),
                                                rinv[:, qt % 2, :].unsqueeze(2).to_broadcast([P, HEADS, HD]),
                                                ALU.mult).then_inc(out_done, 1)

        @block.gpsimd
        def _(pool):
            make_constants(nc, pool, g)


def make_constants(nc, pool, g):
    tiles = (g["ident"], g["identb"], g["mask"])
    for m in tiles:
        nc.gpsimd.memset(m[:, :], 0.0).then_inc(g["blank_done"], 1)
    pool.wait_ge(g["blank_done"], len(tiles))
    for m in tiles[:2]:
        nc.gpsimd.affine_select(out=m[:, :], in_=m[:, :], compare_op=ALU.not_equal, fill=1.0, base=0,
                                pattern=[[-1, P]], channel_multiplier=1).then_inc(g["ident_done"], 1)
    nc.gpsimd.affine_select(out=g["mask"][:, :], in_=g["mask"][:, :], compare_op=ALU.is_ge, fill=NEG, base=0,
                            pattern=[[-1, P]], channel_multiplier=1).then_inc(g["ident_done"], 2)


def experts(nc, d, g):
    STEP = 5
    SHARED = 2
    NS = SHARED * CH
    GT = CW // P
    with ExitStack() as ctx:
        def sb(name, shape, dt):
            return ctx.enter_context(nc.sbuf_tensor(name, shape, dt))

        def sem(name):
            return ctx.enter_context(nc.semaphore(name))

        condT, x1T = g["condT"], g["x1T"]
        raw_ab = sb("raw_ab", [P, ACOLS], F32)
        raw_c = sb("raw_c", [P, CCOLS], F32)
        gate2 = sb("gate2", [P, 2, KD, I], F32R)
        up2 = sb("up2", [P, 2, KD, I], F32R)
        down2 = sb("down2", [P, 2, 3, D], F32R)
        mu2 = sb("mu2", [P, D], F32R)
        qa2 = sb("qa2", [P, 2, KD, 2 * LR], F32R)
        qb2 = sb("qb2", [P, 2, 2, I], F32R)
        dqa2 = sb("dqa2", [P, 2, 3, 2 * LR], F32R)
        dqb2 = sb("dqb2", [P, 2, D], F32R)
        mu_mask = sb("mu_mask", [P, 2], F32)
        mult_w = sb("mult_w", [P, 4, CW], F32)
        slot_w = mult_w[:, 0:2, :]
        gate_w = mult_w[:, 2:4, :]
        slot2 = sb("slot2", [P, CW], F32R)
        xe32 = sb("xe32", [P, 2, CW], F32)
        xe2 = sb("xe2", [P, 2, 2, KD, CW], F32R)
        sg = sb("sg", [P, 2, CW], F32)
        hid2 = sb("hid2", [P, 2, 3, CW], F32R)
        low32 = sb("low32", [P, CW], F32)
        lowg = sb("lowg", [P, CW], F32R)
        lowu = sb("lowu", [P, CW], F32R)
        dlow2 = sb("dlow2", [P, CW], F32R)
        wide = ctx.enter_context(nc.psum_tensor("wide", [P, 2, 2, CW], F32))
        xe_ps = ctx.enter_context(nc.psum_tensor("xe_ps", [P, 2, CW], F32))
        low_ps = ctx.enter_context(nc.psum_tensor("low_ps", [P, CW], F32))
        dlow_ps = ctx.enter_context(nc.psum_tensor("dlow_ps", [P, CW], F32))

        x_res_in = sem("x_res_in")
        router_in = sem("router_in")
        wa_in = sem("wa_in")
        wb_in = sem("wb_in")
        wc_in = sem("wc_in")
        slot_in = [sem(f"slot_in{s}") for s in range(2)]
        gu_hi = sem("gu_hi")
        gu_split = sem("gu_split")
        qb_scaled = sem("qb_scaled")
        qb_hi = sem("qb_hi")
        qb_split = sem("qb_split")
        dn_hi = sem("dn_hi")
        dn_split = sem("dn_split")
        dqb_scaled = sem("dqb_scaled")
        dl_hi = sem("dl_hi")
        dl_split = sem("dl_split")
        early_hi = sem("early_hi")
        qa_split = sem("qa_split")
        mu_rest = sem("mu_rest")
        mu_split = sem("mu_split")
        slot_hi = sem("slot_hi")
        slot_split = sem("slot_split")
        xe_full = sem("xe_full")
        xe_sum = sem("xe_sum")
        xe_hi = sem("xe_hi")
        xe_split = sem("xe_split")
        low_full = sem("low_full")
        low_sum = sem("low_sum")
        low_hi = sem("low_hi")
        low_split = sem("low_split")
        dlow_full = sem("dlow_full")
        dlow_sum = sem("dlow_sum")
        dlow_hi = sem("dlow_hi")
        dlow_split = sem("dlow_split")
        wide_full = sem("wide_full")
        wide_done = sem("wide_done")
        silu_done = sem("silu_done")
        up_weighed = sem("up_weighed")
        hid_hi = sem("hid_hi")
        hid_split = sem("hid_split")
        logits_full = sem("logits_full")
        rstep = sem("rstep")
        r_exp = sem("r_exp")
        route_ready = sem("route_ready")
        turned = sem("turned")
        turned_out = sem("turned_out")
        route_out = sem("route_out")

        area = mult_w[:, :, :].rearrange("p a n -> p (a n)")
        place = [0]

        def routing_tile(n):
            a = place[0]
            place[0] += GT * n
            return area[:, a:a + GT * n].rearrange("p (t e) -> p t e", t=GT)

        score, work, flat, eq = (routing_tile(E) for _ in range(4))
        soft = routing_tile(E + F)
        top, topi, topf, stat, stat2 = (routing_tile(F) for _ in range(5))
        inv = area[:, place[0]:place[0] + E]
        inv_i = area[:, place[0] + E:place[0] + 2 * E].bitcast(I32)
        router_w = xe32[:, 0, 0:KD * E].rearrange("p (k e) -> p k e", k=KD)
        routeT = low32[0:E + F, :]

        def a_of(name, kt=None, cols=AC):
            a, z = cols[name]
            t = (raw_c if cols is CC else raw_ab)[:, a:z]
            return t if kt is None else t.rearrange("p (k n) -> p k n", k=kt)

        def parity(c, m):
            return (c * STEP + m) % 2

        def chunk(c):
            return slice(c * CW, (c + 1) * CW)

        def slot_loads(n, c):
            return (n - NS - c) * (96 // CH) + 48 * (c // 2 + 1)

        block = ctx.enter_context(nc.Block())


        @block.sync
        def _(sp):
            def pick(name, e):
                f = e - SHARED
                if isinstance(f, int):
                    return d[name][f, :, :]
                return d[name][bass.ds(f, 1), :, :].rearrange("a p n -> p (a n)")

            def load_a(e, shared=False):
                if shared:
                    sp.dma_start(raw_ab[:, 0:2 * KD * I], d["shared_a"][e, :, :]).then_inc(wa_in, 16)
                else:
                    sp.dma_start(raw_ab[:, 0:ACOLS], pick("expert_a", e)).then_inc(wa_in, 16)

            def load_b(e, shared=False):
                if not shared:
                    sp.wait_ge(qb_split, e - SHARED + 1)
                sp.wait_ge(gu_split, e * 2 + 2)
                if shared:
                    sp.dma_start(raw_ab[:, 0:3 * D], d["shared_b"][e, :, :]).then_inc(wb_in, 16)
                else:
                    sp.dma_start(raw_ab[:, 0:BCOLS], pick("expert_b", e)).then_inc(wb_in, 16)

            def load_c(e):
                sp.dma_start(raw_c[:, :], pick("expert_c", e)).then_inc(wc_in, 16)

            def load_slots(e, c, s):
                f = e - SHARED
                if isinstance(f, int):
                    rows, scalar = d["route"][f * KR:(f + 1) * KR, chunk(c)], d["route"][E + f:E + f + 1, chunk(c)]
                else:
                    rows = d["route"][bass.ds(f * KR, KR), chunk(c)]
                    scalar = d["route"][bass.ds(f + E, 1), chunk(c)]
                for half in range(2):
                    sp.dma_start(slot_w[half * LR:(half + 1) * LR, s, :],
                                 rows.unsqueeze(1).to_broadcast([KR, R, CW])).then_inc(slot_in[s], 16)
                sp.dma_start(gate_w[:, s, :], scalar.to_broadcast([P, CW])).then_inc(slot_in[s], 16)

            load_a(0, True)
            sp.dma_start(router_w, d["router"].rearrange("(k p) e -> p k e", p=P)).then_inc(router_in, 16)
            sp.dma_start(inv_i, d["inv"].to_broadcast([P, E])).then_inc(router_in, 16)
            sp.dma_start(mu_mask[:, :], d["mu_mask"]).then_inc(router_in, 16)
            load_b(0, True)
            for b in range(B):
                sp.dma_start(x1T[:, :, b * S:(b + 1) * S],
                             d["xT"][b, :, :].rearrange("(k p) s -> p k s", p=P)).then_inc(x_res_in, 16)
            load_c(SHARED)
            sp.wait_ge(dn_split, 1)
            load_a(1, True)
            for q in range(CH):
                sp.wait_ge(turned_out, q + 1)
                sp.dma_start(d["route"][:, chunk(q)], routeT).then_inc(route_out, 16)
                if q == CH - 2:
                    load_b(1, True)
            sp.wait_ge(route_out, 16 * CH)
            sp.wait_ge(dn_split, 2)
            load_a(SHARED)
            load_slots(SHARED, 0, 0)

            def expert(it, last):
                e = it + SHARED
                for c in range(CH):
                    if c == 0:
                        sp.wait_ge(low_sum, it * CH + 1)
                    else:
                        sp.wait_ge(dlow_sum, it * CH + c)
                    if c < CH - 1:
                        load_slots(e, c + 1, (c + 1) % 2)
                    elif not last:
                        load_slots(e + 1, 0, 0)
                    if c == 1 and not last:
                        sp.wait_ge(dn_split, e + 1)
                        sp.wait_ge(dl_split, it * 2 + 2)
                        load_a(e + 1)
                        sp.wait_ge(qa_split, it + 1)
                        sp.wait_ge(mu_split, it + 1)
                        load_c(e + 1)
                    if c == CH - 1 and not last:
                        load_b(e + 1)

            load_b(SHARED)
            with sp.Fori(0, F - 1) as it:
                expert(it, False)
            expert(F - 1, True)

        @block.tensor
        def _(pe):
            def products(out, lhs, rhs, start, stop):
                for k, (a, b) in enumerate(zip(lhs, rhs)):
                    nc.tensor.matmul(out, a[0], b[0], start=start and k == 0, stop=False)
                    nc.tensor.matmul(out, a[0], b[1], start=False, stop=False)
                    last = nc.tensor.matmul(out, a[1], b[0], start=False, stop=stop and k == len(lhs) - 1)
                return last

            def gate_up(n, c, m, routed):
                i0, rows = IT[m]
                cols = slice(i0, i0 + rows)
                pe.wait_ge(wide_done, n * STEP + (m + 1))
                x = [(xe2[:, c % 2, 0, k, :], xe2[:, c % 2, 1, k, :]) for k in range(KD)]
                for j, w in enumerate((gate2, up2)):
                    last = products(wide[0:rows, parity(c, m), j, :],
                                    [(w[:, 0, k, cols], w[:, 1, k, cols]) for k in range(KD)], x, True, not routed)
                if routed:
                    if m == 0:
                        pe.wait_ge(low_split, (n - NS) * 2 + 2)
                    for j, low in enumerate((lowg, lowu)):
                        out = wide[0:rows, parity(c, m), j, :]
                        nc.tensor.matmul(out, qb2[:, 0, j, cols], low[:, :], start=False, stop=False)
                        last = nc.tensor.matmul(out, qb2[:, 1, j, cols], low[:, :], start=False, stop=True)
                last.then_inc(wide_full, 1)

            def project_slots(n, half):
                pe.wait_ge(xe_sum, (n - NS) * 2 + (half + 1))
                if half == 0:
                    pe.wait_ge(slot_split, n - NS + 1)
                for j in range(2):
                    m = 2 * half + j
                    last = nc.tensor.matmul(xe_ps[:, j, :], mu2[:, m * P:(m + 1) * P], slot2[:, :],
                                            start=True, stop=True)
                last.then_inc(xe_full, 1)

            def low_rank(n, c):
                pe.wait_ge(xe_split, n * 2 + 2)
                products(low_ps[:, :], [(qa2[:, 0, k, :], qa2[:, 1, k, :]) for k in range(KD)],
                         [(xe2[:, c % 2, 0, k, :], xe2[:, c % 2, 1, k, :]) for k in range(KD)], True, True
                         ).then_inc(low_full, 1)

            def down(n, c, e, routed):
                if c == 0:
                    pe.wait_ge(dn_split, e + 1)
                    if routed:
                        pe.wait_ge(dl_split, (e - SHARED) * 2 + 2)
                h = [(hid2[0:rows, 0, m, :], hid2[0:rows, 1, m, :]) for m, (_, rows) in enumerate(IT)]
                if routed:
                    pe.wait_ge(hid_split, n * 3 + 2)
                    products(dlow_ps[:, :], [(dqa2[:, 0, m, :], dqa2[:, 1, m, :]) for m in range(2)], h[:2], True, False)
                    pe.wait_ge(hid_split, n * 3 + 3)
                    rows = IT[2][1]
                    products(dlow_ps[:, :], [(dqa2[0:rows, 0, 2, :], dqa2[0:rows, 1, 2, :])], h[2:], False, True
                             ).then_inc(dlow_full, 1)
                else:
                    pe.wait_ge(hid_split, n * 3 + 3)
                for pair in range(2):
                    pe.wait_ge(wide_done, n * STEP + (3 + pair + 1))
                    for j in range(2):
                        h0 = (2 * pair + j) * P
                        w = [(down2[0:rows, 0, m, h0:h0 + P], down2[0:rows, 1, m, h0:h0 + P])
                             for m, (_, rows) in enumerate(IT)]
                        last = products(wide[:, parity(c, 3 + pair), j, :], w, h, True, not routed)
                    if routed:
                        if pair == 0:
                            pe.wait_ge(dlow_split, n - NS + 2)
                        for j in range(2):
                            h0 = (2 * pair + j) * P
                            out = wide[:, parity(c, 3 + pair), j, :]
                            nc.tensor.matmul(out, dqb2[:, 0, h0:h0 + P], dlow2[:, :], start=False, stop=False)
                            last = nc.tensor.matmul(out, dqb2[:, 1, h0:h0 + P], dlow2[:, :], start=False, stop=True)
                    last.then_inc(wide_full, 1)

            def turn(q):
                pe.wait_ge(route_ready, q + 1)
                if q >= 1:
                    pe.wait_ge(turned_out, q)
                for t in range(GT):
                    last = nc.tensor.transpose(xe_ps[0:E + F, 1, t * P:(t + 1) * P], soft[:, t, :], g["ident"][:, :])
                last.then_inc(turned, 1)

            for n in range(NS):
                e, c = divmod(n, CH)
                if n < CH:
                    if n == 0:
                        pe.wait_ge(router_in, 48)
                    else:
                        pe.wait_ge(r_exp, 2 * n - 1)
                    for t in range(GT):
                        for k in range(KD):
                            tok = (n * GT + t) * P
                            last = nc.tensor.matmul(xe_ps[:, 0, t * E:(t + 1) * E], condT[:, k, tok:tok + P],
                                                    router_w[:, k, :], start=k == 0, stop=k == KD - 1)
                    last.then_inc(logits_full, 1)
                if c == 0:
                    pe.wait_ge(gu_split, e * 2 + 2)
                pe.wait_ge(xe_split, n * 2 + 2)
                gate_up(n, c, 0, False)
                if n == NS - 1:
                    pe.wait_ge(mu_split, 1)
                    project_slots(NS, 0)
                gate_up(n, c, 1, False)
                if 1 <= n <= CH:
                    turn(n - 1)
                if n == NS - 1:
                    project_slots(NS, 1)
                gate_up(n, c, 2, False)
                if n == NS - 1:
                    pe.wait_ge(qa_split, 1)
                    low_rank(NS, 0)
                down(n, c, e, False)

            def expert(it, last):
                e = it + SHARED
                for c in range(CH):
                    n = it * CH + (NS + c)
                    following = not (last and c == CH - 1)
                    if c == 0:
                        pe.wait_ge(gu_split, e * 2 + 2)
                        pe.wait_ge(qb_split, it + 1)
                    gate_up(n, c, 0, True)
                    if following:
                        if c == CH - 1:
                            pe.wait_ge(mu_split, it + 2)
                        project_slots(n + 1, 0)
                    gate_up(n, c, 1, True)
                    if following:
                        project_slots(n + 1, 1)
                    gate_up(n, c, 2, True)
                    if following:
                        if c == CH - 1:
                            pe.wait_ge(qa_split, it + 2)
                        low_rank(n + 1, (c + 1) % CH)
                    down(n, c, e, True)

            with pe.Fori(0, F - 1) as it:
                expert(it, False)
            expert(F - 1, True)

        @block.scalar
        def _(act):
            copy = nc.scalar.activation

            def split_gate_up(e, routed):
                act.wait_ge(wa_in, e * 16 + 16)
                copy(gate2[:, 0, :, :], a_of("gate", KD), ACT.Copy).then_inc(gu_hi, 1)
                copy(up2[:, 0, :, :], a_of("up", KD), ACT.Copy).then_inc(gu_hi, 1)
                if routed:
                    act.wait_ge(qb_scaled, e - SHARED + 1)
                    copy(qb2[:, 0, :, :], a_of("qb", 2), ACT.Copy).then_inc(qb_hi, 1)

            def split_down(e, routed):
                act.wait_ge(wb_in, e * 16 + 16)
                copy(down2[:, 0, :, :], a_of("down", 3, BC), ACT.Copy).then_inc(dn_hi, 1)
                if routed:
                    copy(dqa2[:, 0, :, :], a_of("dqa", 3, BC), ACT.Copy).then_inc(dl_hi, 1)
                    act.wait_ge(dqb_scaled, e - SHARED + 1)
                    copy(dqb2[:, 0, :], a_of("dqb", None, BC), ACT.Copy).then_inc(dl_hi, 1)

            def split_early(f):
                act.wait_ge(wc_in, f * 16 + 16)
                copy(mu2[:, :], a_of("mu", None, CC), ACT.Copy).then_inc(early_hi, 1)
                copy(qa2[:, 0, :, :], a_of("qa", KD, CC), ACT.Copy).then_inc(early_hi, 1)

            def input_half(n, c, half, routed):
                m = slice(2 * half, 2 * half + 2)
                if routed:
                    act.wait_ge(xe_sum, (n - NS) * 2 + (half + 2))
                    src = xe32[:, :, :]
                else:
                    src = condT[:, m, chunk(c)]
                copy(xe2[:, c % 2, 0, m, :], src, ACT.Copy).then_inc(xe_hi, 1)

            def slots(n, c):
                act.wait_ge(slot_in[c % 2], slot_loads(n, c))
                copy(slot2[:, :], slot_w[:, c % 2, :], ACT.Copy).then_inc(slot_hi, 1)

            def silu(n, c, m):
                rows = IT[m][1]
                act.wait_ge(wide_full, n * STEP + (m + 1))
                if m == 2:
                    act.wait_ge(hid_split, n * 3 + 1)
                copy(sg[0:rows, parity(c, m), :], wide[0:rows, parity(c, m), 0, :], ACT.Silu).then_inc(silu_done, 1)

            def hidden_hi(n, c, m):
                rows = IT[m][1]
                act.wait_ge(wide_done, n * STEP + (m + 3))
                copy(hid2[0:rows, 0, m, :], sg[0:rows, parity(c, m), :], ACT.Copy).then_inc(hid_hi, 1)

            def low_rank_hi(n):
                act.wait_ge(low_sum, n - NS + 1)
                copy(lowg[0:LR, :], low32[0:LR, :], ACT.Copy).then_inc(low_hi, 1)
                copy(lowu[LR:2 * LR, :], low32[LR:2 * LR, :], ACT.Copy).then_inc(low_hi, 1)

            def dlow_rank_hi(n):
                act.wait_ge(dlow_sum, n - NS + 1)
                copy(dlow2[:, :], low32[:, :], ACT.Copy).then_inc(dlow_hi, 1)

            split_gate_up(0, False)
            input_half(0, 0, 0, False)
            input_half(0, 0, 1, False)
            for n in range(NS):
                e, c = divmod(n, CH)
                nxt = (n + 1, (c + 1) % CH)
                routed = n == NS - 1
                if n < CH:
                    act.wait_ge(rstep, g["r_first"] + n * g["r_all"])
                    copy(score, work, ACT.Exp).then_inc(r_exp, 1)
                if routed:
                    split_early(0)
                    slots(*nxt)
                silu(n, c, 0)
                if c == 0:
                    split_down(e, False)
                input_half(*nxt, 0, routed)
                silu(n, c, 1)
                hidden_hi(n, c, 0)
                input_half(*nxt, 1, routed)
                if 1 <= n <= CH:
                    act.wait_ge(turned, n)
                    if n >= 2:
                        act.wait_ge(route_out, 16 * (n - 1))
                    copy(routeT, xe_ps[0:E + F, 1, :], ACT.Copy).then_inc(turned_out, 1)
                silu(n, c, 2)
                hidden_hi(n, c, 1)
                hidden_hi(n, c, 2)
                if n < CH:
                    act.wait_ge(rstep, g["r_second"] + n * g["r_all"])
                    copy(work, eq, ACT.Exp).then_inc(r_exp, 1)
                if c == CH - 1:
                    split_gate_up(e + 1, n == NS - 1)
                if routed:
                    low_rank_hi(NS)

            def expert(it, last):
                e = it + SHARED
                for c in range(CH):
                    n = it * CH + (NS + c)
                    following = not (last and c == CH - 1)
                    nxt = (n + 1, (c + 1) % CH)
                    if following:
                        if c == CH - 1:
                            split_early(it + 1)
                        slots(*nxt)
                    silu(n, c, 0)
                    if c == 0:
                        split_down(e, True)
                    if following:
                        input_half(*nxt, 0, True)
                    silu(n, c, 1)
                    hidden_hi(n, c, 0)
                    if following:
                        input_half(*nxt, 1, True)
                    silu(n, c, 2)
                    hidden_hi(n, c, 1)
                    hidden_hi(n, c, 2)
                    if following:
                        low_rank_hi(n + 1)
                    dlow_rank_hi(n)
                    if c == CH - 1 and not last:
                        split_gate_up(e + 1, True)

            with act.Fori(0, F - 1) as it:
                expert(it, False)
            expert(F - 1, True)

        @block.gpsimd
        def _(pool):
            sub = nc.gpsimd.tensor_tensor

            def input_half(n, c, half, routed):
                m = slice(2 * half, 2 * half + 2)
                pool.wait_ge(xe_hi, n * 2 + (half + 1))
                src = xe32[:, :, :] if routed else condT[:, m, chunk(c)]
                sub(xe2[:, c % 2, 1, m, :], src, xe2[:, c % 2, 0, m, :].bitcast(F32), ALU.subtract).then_inc(xe_split, 1)

            def scale_qb(e):
                pool.wait_ge(wa_in, e * 16 + 16)
                sub(a_of("qb"), a_of("qb"), a_of("qscale"), ALU.mult).then_inc(qb_scaled, 1)

            def qb_low(e):
                pool.wait_ge(qb_hi, e - SHARED + 1)
                sub(qb2[:, 1, :, :], a_of("qb", 2), qb2[:, 0, :, :].bitcast(F32), ALU.subtract).then_inc(qb_split, 1)

            def down_low(e):
                pool.wait_ge(wb_in, e * 16 + 16)
                sub(a_of("dqb", None, BC), a_of("dqb", None, BC), a_of("dscale", None, BC), ALU.mult
                    ).then_inc(dqb_scaled, 1)
                pool.wait_ge(dl_hi, (e - SHARED) * 2 + 1)
                sub(dqa2[:, 1, :, :], a_of("dqa", 3, BC), dqa2[:, 0, :, :].bitcast(F32), ALU.subtract
                    ).then_inc(dl_split, 1)
                pool.wait_ge(dl_hi, (e - SHARED) * 2 + 2)
                sub(dqb2[:, 1, :], a_of("dqb", None, BC), dqb2[:, 0, :].bitcast(F32), ALU.subtract
                    ).then_inc(dl_split, 1)

            def early_low(f):
                pool.wait_ge(early_hi, f * 2 + 2)
                sub(qa2[:, 1, :, :], a_of("qa", KD, CC), qa2[:, 0, :, :].bitcast(F32), ALU.subtract).then_inc(qa_split, 1)

            input_half(0, 0, 0, False)
            input_half(0, 0, 1, False)
            for n in range(NS):
                c = n % CH
                routed = n == NS - 1
                if routed:
                    early_low(0)
                input_half(n + 1, (c + 1) % CH, 0, routed)
                input_half(n + 1, (c + 1) % CH, 1, routed)
                if routed:
                    scale_qb(SHARED)
                    qb_low(SHARED)

            def expert(it, last):
                e = it + SHARED
                for c in range(CH):
                    n = it * CH + (NS + c)
                    following = not (last and c == CH - 1)
                    if c == CH - 1 and following:
                        early_low(it + 1)
                    if c == 0:
                        down_low(e)
                    if following:
                        input_half(n + 1, (c + 1) % CH, 0, True)
                        input_half(n + 1, (c + 1) % CH, 1, True)
                    if c == CH - 2 and not last:
                        scale_qb(e + 1)
                    if c == CH - 1 and not last:
                        qb_low(e + 1)

            with pool.Fori(0, F - 1) as it:
                expert(it, False)
            expert(F - 1, True)

        @block.vector
        def _(dve):
            tt = nc.vector.tensor_tensor
            dve.sem_inc(wide_done, 2)
            dve.sem_inc(xe_sum, 1)
            dve.sem_inc(dlow_split, 1)
            done = [0]

            def link(op):
                done[0] += 1
                op.then_inc(rstep, 1)
                dve.wait_ge(rstep, done[0])

            def over(x, n):
                return x.unsqueeze(3).to_broadcast([P, x.shape[1], x.shape[2], n])

            def column(x, j, n):
                return x[:, :, j:j + 1].to_broadcast([P, GT, n])

            def by_expert(x):
                return x.rearrange("p t (f k) -> p t f k", k=KR)

            def route_1(q):
                dve.wait_ge(logits_full, q + 1)
                logits = xe_ps[:, 0, 0:GT * E].rearrange("p (t e) -> p t e", e=E)
                link(nc.vector.tensor_reduce(stat[:, :, 0], logits, AX.X, ALU.max))
                link(tt(work, logits, column(stat, 0, E), ALU.subtract))

            def route_2(q):
                dve.wait_ge(r_exp, 2 * q + 1)
                link(nc.vector.tensor_reduce(stat[:, :, 1], score, AX.X, ALU.add))
                link(nc.vector.reciprocal(stat[:, :, 2], stat[:, :, 1]))
                link(tt(score, score, column(stat, 2, E), ALU.mult))
                for t in range(GT):
                    link(nc.vector.max(top[:, t, :], score[:, t, :]))
                    link(nc.vector.max_index(topi[:, t, :].bitcast(U32), top[:, t, :], score[:, t, :]))
                link(nc.vector.tensor_copy(topf, topi.bitcast(U32)))

            def route_3(q):
                inv_b = inv.unsqueeze(1).to_broadcast([P, GT, E])
                for j in range(TOPK):
                    link(tt(eq, inv_b, column(topf, j, E), ALU.is_equal))
                    link(tt(work if j else flat, eq, column(top, j, E), ALU.mult))
                    if j:
                        link(tt(flat, flat, work, ALU.add))

            def route_4(q):
                link(nc.vector.tensor_reduce(soft[:, :, E:E + F], by_expert(flat), AX.X, ALU.add))
                link(nc.vector.tensor_scalar(eq, flat, 0.0, -1.0e9, ALU.is_equal, ALU.mult))
                link(tt(eq, eq, flat, ALU.add))
                link(nc.vector.tensor_reduce(stat, by_expert(eq), AX.X, ALU.max))
                link(tt(by_expert(eq), by_expert(eq), over(stat, KR), ALU.subtract))

            def route_5(q):
                dve.wait_ge(r_exp, 2 * q + 2)
                link(nc.vector.tensor_reduce(stat, by_expert(work), AX.X, ALU.add))
                link(nc.vector.reciprocal(stat2, stat))
                tt(by_expert(soft[:, :, 0:E]), by_expert(work), over(stat2, KR), ALU.mult).then_inc(route_ready, 1)
                dve.wait_ge(route_ready, q + 1)

            def hidden(n, c, m, routed):
                rows = IT[m][1]
                slot = parity(c, m)
                if routed:
                    dve.wait_ge(wide_full, n * STEP + (m + 1))
                    if m == 0:
                        dve.wait_ge(slot_in[c % 2], slot_loads(n, c))
                    tt(wide[0:rows, slot, 1, :], wide[0:rows, slot, 1, :], gate_w[0:rows, c % 2, :], ALU.mult
                       ).then_inc(up_weighed, 1)
                    dve.wait_ge(up_weighed, (n - NS) * 3 + (m + 1))
                dve.wait_ge(silu_done, n * 3 + (m + 1))
                tt(sg[0:rows, slot, :], wide[0:rows, slot, 1, :], sg[0:rows, slot, :], ALU.mult).then_inc(wide_done, 1)

            def hidden_low(n, c, m):
                rows = IT[m][1]
                dve.wait_ge(hid_hi, n * 3 + (m + 1))
                tt(hid2[0:rows, 1, m, :], sg[0:rows, parity(c, m), :], hid2[0:rows, 0, m, :].bitcast(F32), ALU.subtract
                   ).then_inc(hid_split, 1)

            def slots_low(n, c):
                dve.wait_ge(slot_hi, n - NS + 1)
                tt(slot2[LR:2 * LR, :], slot_w[LR:2 * LR, c % 2, :], slot2[LR:2 * LR, :].bitcast(F32), ALU.subtract
                   ).then_inc(slot_split, 1)

            def add_x(n, c, half):
                dve.wait_ge(xe_full, (n - NS) * 2 + (half + 1))
                dve.wait_ge(xe_split, n * 2 + half)
                tt(xe32[:, :, :], xe_ps[:, :, :], condT[:, 2 * half:2 * half + 2, chunk(c)], ALU.add
                   ).then_inc(xe_sum, 1)

            def weigh_low(n, c, after):
                dve.wait_ge(low_full, n - NS + 1)
                if after:
                    dve.wait_ge(low_split, (n - NS) * 2)
                    dve.wait_ge(dlow_split, n - NS)
                tt(low32[:, :], low_ps[:, :], slot_w[:, c % 2, :], ALU.mult).then_inc(low_sum, 1)

            def low_low(n):
                dve.wait_ge(low_hi, (n - NS) * 2 + 1)
                tt(lowg[LR:2 * LR, :], low32[0:LR, :], lowg[0:LR, :].bitcast(F32), ALU.subtract).then_inc(low_split, 1)
                dve.wait_ge(low_hi, (n - NS) * 2 + 2)
                tt(lowu[0:LR, :], low32[LR:2 * LR, :], lowu[LR:2 * LR, :].bitcast(F32), ALU.subtract
                   ).then_inc(low_split, 1)

            def weigh_dlow(n, c, following):
                dve.wait_ge(dlow_full, n - NS + 1)
                dve.wait_ge(low_split, (n - NS + following) * 2 + 2)
                tt(low32[:, :], dlow_ps[:, :], slot_w[:, c % 2, :], ALU.mult).then_inc(dlow_sum, 1)

            def dlow_low(n):
                dve.wait_ge(dlow_hi, n - NS + 1)
                tt(dlow2[LR:2 * LR, :], low32[LR:2 * LR, :], dlow2[LR:2 * LR, :].bitcast(F32), ALU.subtract
                   ).then_inc(dlow_split, 1)

            def add_out(n, c, pair):
                dve.wait_ge(wide_full, n * STEP + (3 + pair + 1))
                acc = x1T[:, 2 * pair:2 * pair + 2, chunk(c)]
                tt(acc, wide[:, parity(c, 3 + pair), :, :], acc, ALU.add).then_inc(wide_done, 1)

            def gate_up_low(e, j):
                dve.wait_ge(gu_hi, e * 2 + (j + 1))
                w, name = ((gate2, "gate"), (up2, "up"))[j]
                tt(w[:, 1, :, :], a_of(name, KD), w[:, 0, :, :].bitcast(F32), ALU.subtract).then_inc(gu_split, 1)

            def down_low(e):
                dve.wait_ge(dn_hi, e + 1)
                tt(down2[:, 1, :, :], a_of("down", 3, BC), down2[:, 0, :, :].bitcast(F32), ALU.subtract
                   ).then_inc(dn_split, 1)

            def mu_low(f):
                dve.wait_ge(early_hi, f * 2 + 1)
                raw = a_of("mu", None, CC)
                tt(raw, raw, mu2[:, :].bitcast(F32), ALU.subtract).then_inc(mu_rest, 1)
                dve.wait_ge(mu_rest, f * 2 + 1)
                nc.vector.tensor_scalar(raw, raw, mu_mask[:, 1:2], None, ALU.mult).then_inc(mu_rest, 1)
                dve.wait_ge(mu_rest, f * 2 + 2)
                nc.vector.scalar_tensor_tensor(mu2[:, :], mu2[:, :].bitcast(F32), mu_mask[:, 0:1], raw,
                                               ALU.mult, ALU.add).then_inc(mu_split, 1)

            gate_up_low(0, 0)
            gate_up_low(0, 1)
            dve.wait_ge(router_in, 48)
            link(nc.vector.tensor_copy(inv, inv_i))
            for n in range(NS):
                e, c = divmod(n, CH)
                if n < CH:
                    route_1(n)
                    assert done[0] == g["r_first"] + n * g["r_all"], done
                if n == NS - 1:
                    mu_low(0)
                    slots_low(NS, 0)
                hidden(n, c, 0, False)
                if c == 0:
                    down_low(e)
                if n == 0:
                    dve.wait_ge(x_res_in, 16 * B)
                if n < CH:
                    route_2(n)
                if n == NS - 1:
                    add_x(NS, 0, 0)
                hidden(n, c, 1, False)
                hidden_low(n, c, 0)
                if n < CH:
                    route_3(n)
                if n == NS - 1:
                    add_x(NS, 0, 1)
                hidden(n, c, 2, False)
                hidden_low(n, c, 1)
                hidden_low(n, c, 2)
                if n < CH:
                    route_4(n)
                    assert done[0] == g["r_second"] + n * g["r_all"], done
                    route_5(n)
                if c == CH - 1:
                    gate_up_low(e + 1, 0)
                    gate_up_low(e + 1, 1)
                if n == NS - 1:
                    weigh_low(NS, 0, False)
                    low_low(NS)
                add_out(n, c, 0)
                add_out(n, c, 1)

            def expert(it, last):
                e = it + SHARED
                for c in range(CH):
                    n = it * CH + (NS + c)
                    following = not (last and c == CH - 1)
                    nc_ = (c + 1) % CH
                    if following:
                        if c == CH - 1:
                            mu_low(it + 1)
                        slots_low(n + 1, nc_)
                    hidden(n, c, 0, True)
                    if c == 0:
                        down_low(e)
                    if following:
                        add_x(n + 1, nc_, 0)
                    hidden(n, c, 1, True)
                    hidden_low(n, c, 0)
                    if following:
                        add_x(n + 1, nc_, 1)
                    hidden(n, c, 2, True)
                    hidden_low(n, c, 1)
                    hidden_low(n, c, 2)
                    if following:
                        weigh_low(n + 1, nc_, True)
                        low_low(n + 1)
                    weigh_dlow(n, c, following)
                    dlow_low(n)
                    if c == CH - 1 and not last:
                        gate_up_low(e + 1, 0)
                        gate_up_low(e + 1, 1)
                    add_out(n, c, 0)
                    add_out(n, c, 1)

            with dve.Fori(0, F - 1) as it:
                expert(it, False)
            expert(F - 1, True)


def ffn(nc, d, g):
    NT = T // P
    GC = 4
    GW = L1I // GC
    RING = 3
    with ExitStack() as ctx:
        def sb(name, shape, dt):
            return ctx.enter_context(nc.sbuf_tensor(name, shape, dt))

        def sem(name):
            return ctx.enter_context(nc.semaphore(name))

        x1T = g["x1T"]
        wgT = sb("wgT", [P, KD, L1I], BF16)
        wuT = sb("wuT", [P, KD, L1I], BF16)
        wdT = sb("wdT", [P, L1T, D], BF16)
        gscale = sb("gscale", [P, L1I], F32)
        uscale = sb("uscale", [P, L1I], F32)
        dscale = sb("dscale", [P, D], F32)
        idx = sb("idx", [P, L1T], I32)
        spare = g["condT"][:, :, :].rearrange("p k n -> p (k n)")
        raw = spare[:, 0:RING * L1I].rearrange("p (a n) -> p a n", a=RING)
        fin = spare[:, RING * L1I:RING * L1I + 3 * D].rearrange("p (a n) -> p a n", a=3)
        x1 = spare[:, RING * L1I + 3 * D:RING * L1I + 7 * D].rearrange("p (a n) -> p a n", a=4)
        wy = sb("wy", [P, RING, L1I], F32)
        wgrid = sb("wgrid", [P, RING, L1I], F32)
        rowq = sb("rowq", [P, 2, L1I], BF16)
        hid = wy[:, 0:2, :]
        hy = wy[:, 2, :]
        hgrid = wgrid[:, 0, :]
        xy = wgrid[:, 1, 0:D]
        xgrid = wgrid[:, 1, D:2 * D]
        colscale = sb("colscale", [P, 2 * L1T + KD], F32)
        amax = sb("amax", [P, 4], F32)
        rcp = sb("rcp", [P, RING], F32)
        condW = sb("condW", [P, KD, D], F32)
        condWb = sb("condWb", [P, 2, KD, D], F32)
        adA = sb("adA", [RANK, 2, D], F32)
        adB = sb("adB", [RANK, 2, D], F32)
        adS = sb("adS", [RANK, 2], F32)
        adBs = sb("adBs", [RANK, 2, D], F32)
        itok = sb("itok", [1, B], I32)
        xq = sb("xq", [P, D], BF16)
        xqT = sb("xqT", [P, KD, P], BF16)
        xs = sb("xs", [P, 4], F32)
        xr = sb("xr", [P, 2], F32)
        zg = sb("zg", [P, 2, GW], F32)
        sg = sb("sg_l1", [P, 2, GW], F32)
        hs = sb("hs", [P, 4], F32)
        hr = sb("hr", [P, 2], F32)
        hq = sb("hq", [P, L1I], BF16)
        hqT = sb("hqT", [P, L1T, P], BF16)

        xc_ps = ctx.enter_context(nc.psum_tensor("xc_ps", [P, D], F32))
        misc = ctx.enter_context(nc.psum_tensor("misc", [P, 2, 512], F32))
        gu = ctx.enter_context(nc.psum_tensor("gu", [P, 2, 2, 512], F32))
        out_ps = ctx.enter_context(nc.psum_tensor("out_ps_l1", [P, D], F32))

        idx_in = sem("idx_in")
        itok_in = sem("itok_in")
        condW_in = sem("condW_in")
        ad_in = [sem(f"ad_in{s}") for s in range(2)]
        row_in = [sem(f"row_in{s}") for s in range(RING)]
        down_in = [sem(f"down_in{s}") for s in range(RING)]
        dve_step = sem("dve_step")
        wmax_done = sem("wmax_done")
        wy_done = sem("wy_done")
        wgrid_done = sem("wgrid_done")
        wshift_done = sem("wshift_done")
        row_q = sem("row_q")
        misc_full = sem("misc_full")
        misc_done = sem("misc_done")
        scales_out = sem("scales_out")
        scales_in = sem("scales_in")
        adb_done = sem("adb_done")
        wb_full = sem("wb_full")
        wb_done = sem("wb_done")
        xc_full = sem("xc_full")
        xmax_done = sem("xmax_done")
        xy_done = sem("xy_done")
        xgrid_done = sem("xgrid_done")
        xshift_done = sem("xshift_done")
        xq_done = sem("xq_done")
        gu_full = sem("gu_full")
        zg_done = sem("zg_done")
        silu_done = sem("silu_done_l1")
        gu_done = sem("gu_done")
        hid_done = sem("hid_done_l1")
        hmax_done = sem("hmax_done")
        hy_done = sem("hy_done")
        hgrid_done = sem("hgrid_done")
        hshift_done = sem("hshift_done")
        hq_done = sem("hq_done")
        out_full = sem("out_full")
        outs_done = sem("outs_done")
        fin_done = sem("fin_done")
        stored = [sem(f"stored{s}") for s in range(3)]

        rows = [("gate", j) for j in range(L1T)] + [("up", j) for j in range(L1T)] + [("down", j) for j in range(KD)]
        NR = len(rows)
        width = {"gate": D, "up": D, "down": L1I}
        fills = []
        for n, (kind, j) in enumerate(rows):
            nb = width[kind] // P
            for b0 in range(0, nb, 8):
                fills.append((n, b0, min(8, nb - b0)))
        last_fill = {m: f for f, (m, _, _) in enumerate(fills)}

        def step_fills(i):
            out = []
            if i < NT:
                out.append(("x1", i))
            if 0 <= i - 1 < NT:
                out.append(("xq", i - 1))
            if 0 <= i - 2 < NT:
                out += [("hqa", i - 2), ("hqb", i - 2)]
            return out
        order = [f for i in range(NT + 2) for f in step_fills(i)]
        fill_at = {f: len(fills) + n for n, f in enumerate(order)}

        block = ctx.enter_context(nc.Block())

        def bankb(n):
            return misc[:, n % 2, :].bitcast(BF16).rearrange("p (k n) -> p k n", n=P)

        @block.sync
        def _(sp):
            sp.dma_start(idx[:, :], d["didx"]).then_inc(idx_in, 16)
            sp.dma_start(itok[:, :], d["itok"]).then_inc(itok_in, 16)
            sp.dma_start(condW[:, :, :], d["condW"].rearrange("(k p) n -> p k n", p=P)).then_inc(condW_in, 16)
            sp.wait_ge(itok_in, 16)
            for b in range(B):
                s = b % 2
                if b >= 2:
                    sp.wait_ge(wb_done, 4 * (b - 1) + 2)
                a = sp.value_load(itok[0:1, b:b + 1], min_val=0, max_val=NA - 1)
                sp.dma_start(adA[:, s, :], d["adA"][bass.ds(a, 1), :, :].rearrange("a r n -> (a r) n")
                             ).then_inc(ad_in[s], 16)
                sp.dma_start(adB[:, s, :], d["adB"][bass.ds(a, 1), :, :].rearrange("a r n -> (a r) n")
                             ).then_inc(ad_in[s], 16)
                sp.dma_start(adS[:, s:s + 1], d["adS"][bass.ds(a, 1), :].to_broadcast([RANK, 1])
                             ).then_inc(ad_in[s], 16)
                if b == 1:
                    for n, (kind, j) in enumerate(rows):
                        if kind == "down":
                            sp.wait_ge(wy_done, n - RING + 1)
                            sp.dma_start(raw[:, n % RING, :], d["wdown"][j * P:(j + 1) * P, :]
                                         ).then_inc(down_in[n % RING], 16)
                    sp.wait_ge(wmax_done, NR)
                    sp.dma_start(d["scales"].rearrange("j p -> p j"), colscale[:, :],
                                 allow_slow_non_contiguous=True).then_inc(scales_out, 16)
                    sp.wait_ge(scales_out, 16)
                    flat = d["scales"].rearrange("j p -> (j p)").unsqueeze(0)
                    sp.dma_start(gscale[:, :], flat[:, 0:L1I].to_broadcast([P, L1I])).then_inc(scales_in, 16)
                    sp.dma_start(uscale[:, :], flat[:, L1I:2 * L1I].to_broadcast([P, L1I])).then_inc(scales_in, 16)
                    sp.dma_start(dscale[:, :], flat[:, 2 * L1I:2 * L1I + D].to_broadcast([P, D])).then_inc(scales_in, 16)
            for t in range(NT):
                sp.wait_ge(fin_done, t + 1)
                sp.dma_start(d["out"][t * P:(t + 1) * P, :], fin[:, t % 3, :]).then_inc(stored[t % 3], 16)
            for s in range(3):
                sp.wait_ge(stored[s], 16 * len(range(s, NT, 3)))

        @block.gpsimd
        def _(pool):
            def gather(n):
                kind, j = rows[n]
                if kind == "down":
                    return
                if n >= RING:
                    pool.wait_ge(wy_done, n - RING + 1)
                nc.gpsimd.indirect_dma_start(
                    raw[:, n % RING, 0:D], None, d["w" + kind],
                    bass.IndirectOffsetOnAxis(ap=idx[:, j:j + 1].bitcast(U32), axis=0)).then_inc(row_in[n % RING], 16)

            pool.wait_ge(idx_in, 16)
            for n in range(RING - 1):
                gather(n)
            for n, (kind, j) in enumerate(rows):
                if n + RING - 1 < NR:
                    gather(n + RING - 1)
                y, wd = n % RING, width[kind]
                pool.wait_ge(wgrid_done, n + 1)
                nc.gpsimd.tensor_tensor(wy[:, y, 0:wd], wy[:, y, 0:wd], wgrid[:, y, 0:wd], ALU.add
                                        ).then_inc(wshift_done, 1)

            def weigh(t, c):
                n = t * GC + c
                cols = slice(c * GW, (c + 1) * GW)
                pool.wait_ge(silu_done, n + 1 + 2)
                pool.wait_ge(gu_done, n + 1 + 2)
                nc.gpsimd.tensor_tensor(hid[:, t % 2, cols], hid[:, t % 2, cols], sg[:, n % 2, :], ALU.mult
                                        ).then_inc(hid_done, 1)

            for i in range(NT + 2):
                if 0 <= i - 1 < NT:
                    weigh(i - 1, 0)
                    weigh(i - 1, 1)
                if i < NT:
                    pool.wait_ge(xgrid_done, i + 1)
                    nc.gpsimd.tensor_tensor(xy, xy, xgrid, ALU.add).then_inc(xshift_done, 1)
                if 0 <= i - 1 < NT:
                    weigh(i - 1, 2)
                    weigh(i - 1, 3)
                if 0 <= i - 2 < NT:
                    t = i - 2
                    pool.wait_ge(outs_done, t + 1)
                    nc.gpsimd.tensor_tensor(fin[:, t % 3, :], fin[:, t % 3, :], x1[:, t % 4, :], ALU.add
                                            ).then_inc(fin_done, 1)
                if 0 <= i - 1 < NT:
                    pool.wait_ge(hgrid_done, i)
                    nc.gpsimd.tensor_tensor(hy, hy, hgrid, ALU.add).then_inc(hshift_done, 1)

        @block.vector
        def _(dve):
            count = [0]

            def link(op):
                count[0] += 1
                op.then_inc(dve_step, 1)
                dve.wait_ge(dve_step, count[0])

            def scale_of(src, scale, r, j):
                link(nc.vector.tensor_reduce(amax[:, j:j + 1], src, AX.X, ALU.max, apply_absolute_value=True))
                link(nc.vector.tensor_scalar(scale, amax[:, j:j + 1], 1.0 / FP8_MAX, None, ALU.mult))
                return nc.vector.reciprocal(r, scale)

            def grid_of(st, y):
                link(nc.vector.tensor_scalar(st.bitcast(U32), y.bitcast(U32), 0x7F800000, None, ALU.bitwise_and))
                return nc.vector.tensor_scalar(st, st, 2.0 ** -6, 1.5 * 2.0 ** 20, ALU.max, ALU.mult)

            dve.sem_inc(misc_done, 2)
            dve.sem_inc(wb_done, 2)
            dve.sem_inc(gu_done, 2)
            dve.sem_inc(silu_done, 2)
            dve.sem_inc(hid_done, 2)

            for i in range(NR + 2):
                if i < NR:
                    kind, j = rows[i]
                    s = i % RING
                    if kind == "down":
                        dve.wait_ge(down_in[s], 16 * len([m for m in range(i + 1) if rows[m][0] == "down"
                                                          and m % RING == s]))
                    else:
                        dve.wait_ge(row_in[s], 16 * (i // RING + 1))
                    scale_of(raw[:, s, 0:width[kind]], colscale[:, i:i + 1], rcp[:, s:s + 1], 0).then_inc(wmax_done, 1)
                if 0 <= i - 1 < NR:
                    m = i - 1
                    wd = width[rows[m][0]]
                    dve.wait_ge(wy_done, m + 1)
                    grid_of(wgrid[:, m % RING, 0:wd], wy[:, m % RING, 0:wd]).then_inc(wgrid_done, 1)
                if i - 2 >= 0:
                    m = i - 2
                    wd = width[rows[m][0]]
                    dve.wait_ge(wshift_done, m + 1)
                    if m >= 2:
                        dve.wait_ge(misc_full, last_fill[m - 2] + 1)
                    nc.vector.tensor_tensor(rowq[:, m % 2, 0:wd], wy[:, m % RING, 0:wd], wgrid[:, m % RING, 0:wd],
                                            ALU.subtract).then_inc(row_q, 1)
            dve.wait_ge(row_q, NR)

            def conditioned(b):
                s = b % 2
                dve.wait_ge(ad_in[s], 48 * (b // 2 + 1))
                nc.vector.tensor_scalar(adBs[:, s, :], adB[:, s, :], adS[:, s:s + 1], None, ALU.mult
                                        ).then_inc(adb_done, 1)
                if b == 0:
                    dve.wait_ge(condW_in, 16)
                for k in range(KD):
                    dve.wait_ge(wb_full, 4 * b + k + 1)
                    nc.vector.tensor_tensor(condWb[:, s, k, :], gu[:, k % 2, 0, :], condW[:, k, :], ALU.add
                                            ).then_inc(wb_done, 1)

            def gate_up(t, c):
                n = t * GC + c
                cols = slice(c * GW, (c + 1) * GW)
                dve.wait_ge(gu_full, n + 1)
                dve.wait_ge(silu_done, n + 1)
                nc.vector.tensor_tensor(zg[:, n % 2, :], gu[:, n % 2, 0, 0:GW], gscale[:, cols], ALU.mult
                                        ).then_inc(zg_done, 1)
                nc.vector.scalar_tensor_tensor(hid[:, t % 2, cols], gu[:, n % 2, 1, 0:GW], xs[:, t % 4:t % 4 + 1],
                                               uscale[:, cols], ALU.mult, ALU.mult).then_inc(gu_done, 1)

            conditioned(0)
            dve.wait_ge(scales_in, 48)
            for i in range(NT + 2):
                x, h, o = i, i - 1, i - 2
                if x < NT:
                    if x % ST == 0 and x:
                        conditioned(x // ST)
                    dve.wait_ge(xc_full, x + 1)
                    scale_of(xc_ps[:, :], xs[:, x % 4:x % 4 + 1], xr[:, x % 2:x % 2 + 1], 1).then_inc(xmax_done, 1)
                if 0 <= o < NT:
                    dve.wait_ge(hshift_done, o + 1)
                    if o >= 1:
                        dve.wait_ge(misc_full, fill_at["hqb", o - 1] + 1)
                    nc.vector.tensor_tensor(hq[:, :], hy, hgrid, ALU.subtract).then_inc(hq_done, 1)
                if 0 <= h < NT:
                    gate_up(h, 0)
                    gate_up(h, 1)
                if x < NT:
                    dve.wait_ge(xy_done, x + 1)
                    grid_of(xgrid, xy).then_inc(xgrid_done, 1)
                if 0 <= h < NT:
                    gate_up(h, 2)
                    gate_up(h, 3)
                if x < NT:
                    dve.wait_ge(xshift_done, x + 1)
                    if x >= 1:
                        dve.wait_ge(misc_full, fill_at["xq", x - 1] + 1)
                    nc.vector.tensor_tensor(xq[:, :], xy, xgrid, ALU.subtract).then_inc(xq_done, 1)
                if 0 <= h < NT:
                    dve.wait_ge(hid_done, 2 + h * GC + GC)
                    scale_of(hid[:, h % 2, :], hs[:, h % 4:h % 4 + 1], hr[:, h % 2:h % 2 + 1], 2).then_inc(hmax_done, 1)
                if 0 <= o < NT:
                    dve.wait_ge(out_full, o + 1)
                    if o >= 3:
                        dve.wait_ge(stored[o % 3], 16 * (o // 3))
                    nc.vector.scalar_tensor_tensor(fin[:, o % 3, :], out_ps[:, :], hs[:, o % 4:o % 4 + 1],
                                                   dscale[:, :], ALU.mult, ALU.mult).then_inc(outs_done, 1)
                if 0 <= h < NT:
                    dve.wait_ge(hy_done, h + 1)
                    grid_of(hgrid, hy).then_inc(hgrid_done, 1)

        @block.scalar
        def _(act):
            def turned_weights(n):
                m, b0, nb = fills[n]
                kind, j = rows[m]
                act.wait_ge(misc_full, n + 1)
                dst = {"gate": wgT, "up": wuT, "down": wdT}[kind]
                nc.scalar.activation(dst[:, b0:b0 + nb, j * P:(j + 1) * P], bankb(n)[:, 0:nb, :], ACT.Copy
                                     ).then_inc(misc_done, 1)

            n = 0
            for m, (kind, j) in enumerate(rows):
                wd = width[kind]
                act.wait_ge(wmax_done, m + 1)
                if m >= RING:
                    act.wait_ge(row_q, m - RING + 1)
                nc.scalar.activation(wy[:, m % RING, 0:wd], raw[:, m % RING, 0:wd], ACT.Copy,
                                     scale=rcp[:, m % RING:m % RING + 1]).then_inc(wy_done, 1)
                while n < len(fills) and fills[n][0] <= m - RING:
                    turned_weights(n)
                    n += 1
            while n < len(fills):
                turned_weights(n)
                n += 1

            def take(f):
                n = fill_at[f]
                act.wait_ge(misc_full, n + 1)
                kind, t = f
                if kind == "x1":
                    if t >= 4:
                        act.wait_ge(fin_done, t - 3)
                    op = nc.scalar.activation(x1[:, t % 4, :], misc[:, n % 2, :], ACT.Copy)
                elif kind == "xq":
                    op = nc.scalar.activation(xqT[:, :, :], bankb(n)[:, 0:KD, :], ACT.Copy)
                elif kind == "hqa":
                    op = nc.scalar.activation(hqT[:, 0:8, :], bankb(n), ACT.Copy)
                else:
                    op = nc.scalar.activation(hqT[:, 8:L1T, :], bankb(n)[:, 0:L1T - 8, :], ACT.Copy)
                op.then_inc(misc_done, 1)

            for i in range(NT + 2):
                x, h, o = i, i - 1, i - 2
                if x < NT:
                    take(("x1", x))
                if 0 <= h < NT:
                    take(("xq", h))
                if x < NT:
                    act.wait_ge(xmax_done, x + 1)
                    if x >= 1:
                        act.wait_ge(xq_done, x)
                    else:
                        act.wait_ge(row_q, NR)
                    nc.scalar.activation(xy, xc_ps[:, :], ACT.Copy, scale=xr[:, x % 2:x % 2 + 1]).then_inc(xy_done, 1)
                if 0 <= h < NT:
                    for c in range(GC):
                        n = h * GC + c
                        act.wait_ge(zg_done, n + 1)
                        act.wait_ge(hid_done, n + 1)
                        nc.scalar.activation(sg[:, n % 2, :], zg[:, n % 2, :], ACT.Silu, scale=xs[:, h % 4:h % 4 + 1]
                                             ).then_inc(silu_done, 1)
                if 0 <= o < NT:
                    take(("hqa", o))
                    take(("hqb", o))
                if 0 <= h < NT:
                    act.wait_ge(hmax_done, h + 1)
                    if h >= 1:
                        act.wait_ge(hq_done, h)
                    nc.scalar.activation(hy, hid[:, h % 2, :], ACT.Copy, scale=hr[:, h % 2:h % 2 + 1]
                                         ).then_inc(hy_done, 1)

        @block.tensor
        def _(pe):
            for n, (m, b0, nb) in enumerate(fills):
                pe.wait_ge(misc_done, n + 1)
                pe.wait_ge(row_q, m + 1)
                for k in range(nb):
                    last = nc.tensor.transpose(bankb(n)[:, k, :], rowq[:, m % 2, (b0 + k) * P:(b0 + k + 1) * P],
                                               g["identb"][:, :])
                last.then_inc(misc_full, 1)

            def conditioned(b):
                s = b % 2
                pe.wait_ge(adb_done, b + 1)
                for k in range(KD):
                    pe.wait_ge(wb_done, 4 * b + k + 1)
                    nc.tensor.matmul(gu[:, k % 2, 0, :], adA[:, s, k * P:(k + 1) * P], adBs[:, s, :],
                                     start=True, stop=True).then_inc(wb_full, 1)
                pe.wait_ge(wb_done, 4 * b + 4 + 2)

            def project(t):
                if t >= 1:
                    pe.wait_ge(xy_done, t)
                for k in range(KD):
                    last = nc.tensor.matmul(xc_ps[:, :], x1T[:, k, t * P:(t + 1) * P], condWb[:, (t // ST) % 2, k, :],
                                            start=k == 0, stop=k == KD - 1)
                last.then_inc(xc_full, 1)
                n = fill_at["x1", t]
                pe.wait_ge(misc_done, n + 1)
                for k in range(KD):
                    last = nc.tensor.transpose(misc[:, n % 2, k * P:(k + 1) * P], x1T[:, k, t * P:(t + 1) * P],
                                               g["ident"][:, :])
                last.then_inc(misc_full, 1)

            def gate_up(t):
                n = fill_at["xq", t]
                pe.wait_ge(misc_done, n + 1)
                pe.wait_ge(xq_done, t + 1)
                for k in range(KD):
                    last = nc.tensor.transpose(bankb(n)[:, k, :], xq[:, k * P:(k + 1) * P], g["identb"][:, :])
                last.then_inc(misc_full, 1)
                pe.wait_ge(misc_done, 2 + n + 1)
                for c in range(GC):
                    m = t * GC + c
                    pe.wait_ge(gu_done, m + 1)
                    for j, wT in enumerate((wgT, wuT)):
                        for k in range(KD):
                            last = nc.tensor.matmul(gu[:, m % 2, j, 0:GW], xqT[:, k, :], wT[:, k, c * GW:(c + 1) * GW],
                                                    start=k == 0, stop=k == KD - 1)
                    last.then_inc(gu_full, 1)

            def down(t):
                pe.wait_ge(hq_done, t + 1)
                for kind, k0, nb in (("hqa", 0, 8), ("hqb", 8, L1T - 8)):
                    n = fill_at[kind, t]
                    pe.wait_ge(misc_done, n + 1)
                    for k in range(nb):
                        last = nc.tensor.transpose(bankb(n)[:, k, :], hq[:, (k0 + k) * P:(k0 + k + 1) * P],
                                                   g["identb"][:, :])
                    last.then_inc(misc_full, 1)
                pe.wait_ge(misc_done, 2 + fill_at["hqb", t] + 1)
                if t >= 1:
                    pe.wait_ge(outs_done, t)
                for k in range(L1T):
                    last = nc.tensor.matmul(out_ps[:, :], hqT[:, k, :], wdT[:, k, :], start=k == 0, stop=k == L1T - 1)
                last.then_inc(out_full, 1)

            conditioned(0)
            for i in range(NT + 2):
                if i < NT:
                    if i % ST == 0 and i:
                        pe.wait_ge(gu_done, 2 + (i - 1) * GC)
                        conditioned(i // ST)
                    project(i)
                if 0 <= i - 1 < NT:
                    gate_up(i - 1)
                if 0 <= i - 2 < NT:
                    down(i - 2)


def build(nc, d):
    with ExitStack() as ctx:
        g = {
            "ident": ctx.enter_context(nc.sbuf_tensor("ident", [P, P], F32)),
            "identb": ctx.enter_context(nc.sbuf_tensor("identb", [P, P], BF16)),
            "condT": ctx.enter_context(nc.sbuf_tensor("condT", [P, KD, T], F32)),
            "blank_done": ctx.enter_context(nc.semaphore("blank_done")),
            "ident_done": ctx.enter_context(nc.semaphore("ident_done")),
            "r_first": 1 + 2,
            "r_second": 1 + 2 + 3 + 2 * (CW // P) + 1 + 3 * TOPK - 1 + 5,
            "r_all": 2 + 3 + 2 * (CW // P) + 1 + 3 * TOPK - 1 + 5 + 2,
        }
        attend(nc, d, g)
        g["x1T"] = ctx.enter_context(nc.sbuf_tensor("x1T", [P, KD, T], F32))
        experts(nc, d, g)
        ffn(nc, d, g)


def kernel(**x):
    import numpy as np
    import concourse.bacc as bacc
    from concourse.bass_utils import run_bass_kernel_spmd

    a = {k: np.asarray(v) for k, v in x.items()}

    def tiles(w, rows):
        full = np.zeros((rows * P,) + w.shape[1:], w.dtype)
        full[:w.shape[0]] = w
        return full.reshape(rows, P, -1).transpose(1, 0, 2).reshape(P, -1)

    def repeated(row, n):
        return np.broadcast_to(row[None, :], (n, row.shape[0]))

    def low_rows(w):
        return w.transpose(0, 2, 1).reshape(LR, -1)

    def twice(w):
        return np.concatenate([w, w])

    q = "L0_ffn_"
    part_a, part_b, part_c = [], [], []
    for f in range(F):
        part_a.append(np.concatenate(
            [tiles(a[q + n + "_W"][f].T, KD) for n in ("gate", "up")]
            + [twice(low_rows(a[q + n + "_qb"][f])) for n in ("gate", "up")]
            + [repeated(a[q + n + "_scale"][f], P) for n in ("gate", "up")], axis=1))
        dqa = a[q + "down_qa"][f].reshape(LR, I).T
        part_b.append(np.concatenate([
            tiles(a[q + "down_W"][f].T, 3), tiles(np.concatenate([dqa, dqa], axis=1), 3),
            twice(low_rows(a[q + "down_qb"][f])), repeated(a[q + "down_scale"][f], P)], axis=1))
        mu = np.zeros((2, KR, R, D), np.float32)
        mu[:, :, 0:2] = a[q + "mask_up_W"][f].T[None, :, None, :]
        qa = np.concatenate([a[q + n + "_qa"][f].reshape(LR, D) for n in ("gate", "up")]).T
        part_c.append(np.concatenate([mu.reshape(P, D), tiles(qa, KD)], axis=1))
    shared_a, shared_b = [], []
    for s in range(2):
        i = slice(s * I, (s + 1) * I)
        shared_a.append(np.concatenate([tiles(a[q + "sh_gate_W"][i].T, KD), tiles(a[q + "sh_up_W"][i].T, KD)], axis=1))
        shared_b.append(tiles(a[q + "sh_down_W"][:, i].T, 3))
    rows = np.arange(P) % R
    mu_mask = np.stack([rows == 0, rows == 1], axis=1).astype(np.float32)
    arrays = {
        "xT": a["x"].transpose(0, 2, 1),
        "cond": a["cond_1"].reshape(B, 1),
        "Wq": a["L0_cond_Wq"].T, "Wk": a["L0_cond_Wk"].T, "Wv": a["L0_cond_Wv"].T, "Wo": a["L0_cond_Wo"].T,
        "router": a["L0_ffn_gate_weight"].T,
        "inv": a["L0_ffn_inv_mapping"].reshape(1, E),
        "expert_a": np.stack(part_a), "expert_b": np.stack(part_b), "expert_c": np.stack(part_c),
        "shared_a": np.stack(shared_a), "shared_b": np.stack(shared_b),
        "mu_mask": mu_mask,
        "didx": a["L1_ffn_down_reorder_index"].reshape(L1T, P).T,
        "itok": a["itok_B_0_6"].reshape(1, B),
        "condW": a["L1_cond_W"].T,
        "adA": a["L1_cond_A"],
        "adB": a["L1_cond_Bm"].transpose(0, 2, 1),
        "adS": a["L1_cond_scalings"].reshape(NA, 1),
        "wgate": a["L1_ffn_w_gate"], "wup": a["L1_ffn_w_up"], "wdown": a["L1_ffn_w_down"],
    }
    arrays = {"in_" + k: np.ascontiguousarray(v) for k, v in arrays.items()}
    nc = bacc.Bacc("TRN2", target_bir_lowering=False, num_devices=1)
    d = {k[3:]: nc.dram_tensor(k, v.shape, mybir.dt.from_np(v.dtype), kind="ExternalInput").ap()
         for k, v in arrays.items()}
    d["route"] = nc.dram_tensor("route", [E + F, T], F32, kind="Internal").ap()
    d["scales"] = nc.dram_tensor("scales", [2 * L1T + KD, P], F32, kind="Internal").ap()
    d["out"] = nc.dram_tensor("out", [T, D], F32, kind="ExternalOutput").ap()
    build(nc, d)
    got = run_bass_kernel_spmd(nc, [arrays], core_ids=[0])
    return got.results[0]["out"].reshape(B, S, D)
```

```python
from contextlib import ExitStack

import concourse.bass as bass
from concourse import mybir

F32 = mybir.dt.float32
F32R = mybir.dt.float32r
BF16 = mybir.dt.bfloat16
U32 = mybir.dt.uint32
I32 = mybir.dt.int32
ALU = mybir.AluOpType
ACT = mybir.ActivationFunctionType
AX = mybir.AxisListType

P = 128
B, S, D = 4, 512, 512
T = B * S
KD = D // P
ST = S // P
HEADS, HD = 16, 32
HPT = P // HD
F, KR, R, I = 8, 8, 8, 352
LR = KR * R
E = F * KR
TOPK = 6
IT = [(0, 128), (128, 128), (256, 96)]
NEG = -1.0e30
L1I = 1408
L1T = L1I // P
NA, RANK = 8, 16
FP8_MAX = 448.0
CH = 4
CW = 512

def columns(cols):
    at, out = 0, {}
    for name, n in cols:
        out[name] = (at, at + n)
        at += n
    return out, at


AC, ACOLS = columns([("gate", KD * I), ("up", KD * I), ("qb", 2 * I), ("qscale", 2 * I)])
BC, BCOLS = columns([("down", 3 * D), ("dqa", 3 * 2 * LR), ("dqb", D), ("dscale", D)])
CC, CCOLS = columns([("mu", D), ("qa", KD * 2 * LR)])


def attend(nc, d, g):
    GU = ST * HPT
    UNITS = KD * GU
    LAG_H = 1
    LAG_T, LAG_L, LAG_V = 2, 3, 4
    STACKED = 3 * HPT * 16
    PB = 4

    ITEMS = ST + 2 * KD + KD + KD
    at = {"first": {("q", 0): 0, ("k", 0): 1}, "middle": {}, "end": {}}
    ending = [("t", -1)] + [("o", m) for m in range(KD)]
    rest = []
    for m in range(KD):
        rest += [("q", m + 1), ("k", m + 1)] if m < KD - 1 else []
        rest += [("t", m - 1)] if m else []
    rest += [("q", KD), ("k", KD)]
    own_values = [("v", m) for m in range(ST)]
    for stage, base, order in (("first", 2, own_values + rest), ("middle", 2 - len(ending), own_values + ending + rest),
                               ("end", -len(ending), ending)):
        at[stage].update({item: base + i for i, item in enumerate(order)})
    assert at["first"]["q", KD] == at["middle"]["q", KD] == ITEMS - len(ending) and ITEMS % 2 == 0

    with ExitStack() as ctx:
        def sb(name, shape, dt):
            return ctx.enter_context(nc.sbuf_tensor(name, shape, dt))

        def sem(name):
            return ctx.enter_context(nc.semaphore(name))

        g["mask"] = sb("mask", [P, P], BF16)
        w2 = {n: sb("w2_" + n, [P, 2, KD, D], F32R) for n in "qkvo"}
        xT2 = sb("xT2", [P, 2, KD, S], F32R)
        qk2 = sb("qk2", [P, 4, S], F32R)
        stacks = sb("stacks", [P, 2, 2, HPT, S], F32R)
        v2 = sb("v2", [P, ST, HEADS, 2, HD], F32R)
        probs = sb("probs", [P, PB, S], F32)
        probsT2 = sb("probsT2", [P, 2, 2, ST, P], F32R)
        attn = sb("attn", [P, 2, ST, P], F32)
        attnT2 = sb("attnT2", [P, 2, KD, S], F32R)
        negmax = sb("negmax", [P, 4], F32)
        rowsum = sb("rowsum", [P, 2, 2 * HPT], F32)
        rinv = sb("rinv", [P, 2, 2 * HPT], F32)
        cond = sb("cond", [P, B], F32)
        beta = sb("beta", [P, 1], F32)
        proj_ps = ctx.enter_context(nc.psum_tensor("proj_ps", [P, 2, 512], F32))
        score_ps = ctx.enter_context(nc.psum_tensor("score_ps", [P, 2, S], F32))
        turned_ps = ctx.enter_context(nc.psum_tensor("turned_ps", [P, 2, ST, P], F32))
        out_ps = ctx.enter_context(nc.psum_tensor("out_ps", [P, 2, 2 * HPT, 2, HD], F32))

        w_in = {n: sem("w_in_" + n) for n in "qkvo"}
        w_hi = sem("w_hi")
        w_split = sem("w_split")
        x_in = sem("x_in")
        x_hi = sem("x_hi")
        x_split = sem("x_split")
        cond_in = sem("cond_in")
        beta_done = sem("beta_done")
        stack_in = [sem(f"stack_in{s}") for s in range(2)]
        proj_full = sem("proj_full")
        proj_hi = sem("proj_hi")
        proj_done = sem("proj_done")
        score_full = sem("score_full")
        negmax_done = sem("negmax_done")
        score_done = sem("score_done")
        turned_full = sem("turned_full")
        turned_hi = sem("turned_hi")
        turned_done = sem("turned_done")
        value_done = sem("value_done")
        rinv_done = sem("rinv_done")
        out_sum = sem("out_sum")
        norm_done = sem("norm_done")

        block = ctx.enter_context(nc.Block())
        condT = g["condT"]

        def place(b, stage, item):
            return b * ITEMS + at[stage][item]

        def unit(u):
            m, i = divmod(u, GU)
            qt, j = divmod(i, HPT)
            return qt, m, j

        def pieces(i, last):
            m, r = divmod(i, GU)
            if 0 <= m < KD - 1 and r < 2 * KD:
                return [(("qk"[r // KD], m + 1), r % KD)]
            if m == KD and r < KD and not last:
                return [(("qk"[j // KD], KD), j % KD) for j in (2 * r, 2 * r + 1)]
            return []

        def items(i, last):
            done = [item for item, k in pieces(i, last) if k == KD - 1]
            m, r = divmod(i, GU)
            if 1 <= m < KD and r == 2 * KD + 1:
                done.append(("t", m - 1))
            return done

        STEPS = UNITS + KD + LAG_H + 1
        X_STEPS = [(KD - 2) * GU + 2 * KD + 1 + 2 * k for k in range(KD)]
        w_raw = {n: condT[:, :, s * S:(s + 1) * S] for n, s in (("q", 1), ("k", 2), ("v", 3), ("o", 0))}

        @block.sync
        def _(sp):
            def load_x(b):
                if isinstance(b, int):
                    src = d["xT"][b, :, :].rearrange("(k p) n -> p k n", p=P)
                else:
                    src = d["xT"][bass.ds(b, 1), :, :].rearrange("a (k p) n -> p (a k) n", p=P)
                sp.dma_start(condT[:, :, bass.ds(b * S, S)], src).then_inc(x_in, 16)

            def load_w(n):
                sp.dma_start(w_raw[n], d["W" + n].rearrange("(k p) n -> p k n", p=P)).then_inc(w_in[n], 16)

            def stack(b, stage, m):
                s = m % 2
                sp.wait_ge(proj_done, place(b, stage, ("k", m)) + 3)
                for j in range(HPT):
                    rows = slice(j * HD, (j + 1) * HD)
                    for r, halves in enumerate((slice(0, 4, 2), slice(0, 4, 3), slice(1, 3, 1))):
                        sp.dma_start(stacks[r * HD:(r + 1) * HD, s, :, j, :].bitcast(F32),
                                     qk2[rows, halves, :].bitcast(F32)).then_inc(stack_in[s], 16)

            load_w("q")
            load_x(0)
            load_w("k")
            sp.dma_start(cond[:, :], d["cond"].to_broadcast([P, B])).then_inc(cond_in, 16)
            load_w("v")
            sp.wait_ge(x_split, KD)
            load_w("o")
            stack(0, "first", 0)

            def batch(b, stage, last):
                if not last:
                    if stage == "first":
                        sp.wait_ge(w_split, 3)
                    load_x(b + 1)
                for m in range(1, KD if last else KD + 1):
                    stack(b, stage, m)

            batch(0, "first", False)
            with sp.Fori(1, B - 1) as b:
                batch(b, "middle", False)
            batch(B - 1, "middle", True)

        @block.tensor
        def _(pe):
            def project(n, i, out, k):
                if n == "v":
                    a, x = (xT2[:, j, k, i * P:(i + 1) * P] for j in range(2)), (w2["v"][:, j, k, :] for j in range(2))
                else:
                    src = attnT2 if n == "o" else xT2
                    a = (w2[n][:, j, k, i * P:(i + 1) * P] for j in range(2))
                    x = (src[:, j, k, :] for j in range(2))
                (a_high, a_low), (x_high, x_low) = a, x
                nc.tensor.matmul(out, a_high, x_high, start=k == 0, stop=False)
                nc.tensor.matmul(out, a_high, x_low, start=False, stop=False)
                return nc.tensor.matmul(out, a_low, x_high, start=False, stop=k == KD - 1)

            def bank(b, stage, item):
                pe.wait_ge(proj_done, place(b, stage, item) + 1)
                return proj_ps[:, at[stage][item] % 2, :]

            def whole(b, stage, item):
                n, i = item
                out = bank(b, stage, item)
                for k in range(KD):
                    op = project(n, i, out, k)
                op.then_inc(proj_full, 1)

            def turn(b, stage, m):
                pe.wait_ge(norm_done, (b * KD + (m + 1)) * 2 + 2)
                out = bank(b, stage, ("t", m))
                for q in range(ST):
                    op = nc.tensor.transpose(out[:, q * P:(q + 1) * P], attn[:, m % 2, q, :], g["ident"][:, :])
                op.then_inc(proj_full, 1)

            def outputs(b, stage):
                pe.wait_ge(proj_done, place(b, stage, ("t", -1)) + 3)
                for m in range(KD):
                    whole(b, stage, ("o", m))

            def scores(b, u):
                qt, m, j = unit(u)
                n = P * (qt + 1)
                if u % GU == 0:
                    pe.wait_ge(stack_in[m % 2], (b * (KD // 2) + (m // 2 + 1)) * STACKED)
                pe.wait_ge(score_done, b * UNITS + (u + 1))
                out, s = score_ps[:, u % 2, :], stacks[0:3 * HD, m % 2, :, j, :]
                nc.tensor.matmul(out[:, 0:n], s[:, 0, qt * P:(qt + 1) * P], s[:, 1, 0:n], start=True, stop=False)
                nc.tensor.matmul(out[:, n - P:n], g["identb"][:, :], g["mask"][:, :],
                                 start=False, stop=True).then_inc(score_full, 1)

            def turn_probs(b, u):
                qt = unit(u)[0]
                pe.wait_ge(score_done, b * UNITS + (u + 3))
                pe.wait_ge(turned_done, b * UNITS + (u + 1))
                for k in range(qt + 1):
                    op = nc.tensor.transpose(turned_ps[:, u % 2, k, :], probs[:, u % PB, k * P:(k + 1) * P],
                                             g["ident"][:, :])
                op.then_inc(turned_full, 1)

            def values(b, stage, u):
                qt, m, j = unit(u)
                pe.wait_ge(turned_done, b * UNITS + (u + 3))
                if u == 0:
                    pe.wait_ge(proj_done, place(b, stage, ("v", ST - 1)) + 3)
                if qt % 2 == 0 and j == 0:
                    pe.wait_ge(norm_done, b * (2 * KD) + (2 * m + qt // 2 + 1))
                out, h = out_ps[:, qt // 2, (qt % 2) * HPT + j, :, :], m * HPT + j
                for k in range(qt + 1):
                    hi, lo = (probsT2[:, u % 2, half, k, :] for half in range(2))
                    nc.tensor.matmul(out[:, :, :], hi, v2[:, k, h, :, :], start=k == 0, stop=False)
                    op = nc.tensor.matmul(out[:, 0, :], lo, v2[:, k, h, 0, :], start=False, stop=k == qt)
                op.then_inc(value_done, 1)

            pe.wait_ge(g["ident_done"], 4)
            pe.wait_ge(x_split, KD)
            for i, n in enumerate("qk"):
                pe.wait_ge(w_split, i + 1)
                whole(0, "first", (n, 0))
            pe.wait_ge(w_split, 3)

            def batch(b, stage, last):
                for m in range(ST):
                    whole(b, stage, ("v", m))
                if stage != "first":
                    turn(b, stage, -1)
                    outputs(b, stage)
                for i in range(STEPS):
                    if i < UNITS:
                        scores(b, i)
                    if 0 <= i - LAG_T < UNITS:
                        turn_probs(b, i - LAG_T)
                    if 0 <= i - LAG_V < UNITS:
                        values(b, stage, i - LAG_V)
                    for item, k in pieces(i, last):
                        if k == 0:
                            if item == ("q", KD):
                                pe.wait_ge(x_split, b * KD + 2 * KD)
                            bank(b, stage, item)
                        n, m = item
                        op = project(n, m % KD, proj_ps[:, at[stage][item] % 2, :], k)
                        if k == KD - 1:
                            op.then_inc(proj_full, 1)
                    for item in items(i, last):
                        if item[0] == "t":
                            turn(b, stage, item[1])

            batch(0, "first", False)
            with pe.Fori(1, B - 1) as b:
                batch(b, "middle", False)
            batch(B - 1, "middle", True)
            turn(B, "end", -1)
            outputs(B, "end")

        @block.scalar
        def _(act):
            copy = nc.scalar.activation

            def split_w(n):
                act.wait_ge(w_in[n], 16)
                copy(w2[n][:, 0, :, :], w_raw[n], ACT.Copy).then_inc(w_hi, 1)

            def split_x(b, k):
                act.wait_ge(x_in, b * 16 + 16)
                copy(xT2[:, 0, k, :], condT[:, k, bass.ds(b * S, S)], ACT.Copy).then_inc(x_hi, 1)

            def high(b, stage, item):
                kind, m = item
                bank = proj_ps[:, at[stage][item] % 2, :]
                act.wait_ge(proj_full, place(b, stage, item) + 1)
                if kind in "qk" and m:
                    act.wait_ge(stack_in[(m - 1) % 2], (b * (KD // 2) + (m + 1) // 2) * STACKED)
                if kind == "q":
                    act.wait_ge(beta_done, b + (m // KD + 1))
                    op = copy(qk2[:, 0, :], bank, ACT.Copy, scale=beta[:, 0:1])
                elif kind == "k":
                    op = copy(qk2[:, 2, :], bank, ACT.Copy)
                elif kind == "v":
                    if stage != "first" and m == 0:
                        act.wait_ge(value_done, b * UNITS + 2)
                    op = copy(v2[:, m, :, 0, :], bank.rearrange("p (h d) -> p h d", h=HEADS), ACT.Copy)
                elif kind == "t":
                    op = copy(attnT2[:, 0, m % KD, :], bank, ACT.Copy)
                else:
                    op = copy(condT[:, m, bass.ds(b * S - S, S // 2)], bank[:, 0:S // 2], ACT.Copy)
                op.then_inc(proj_hi, 1)

            def exponentials(b, u):
                qt, m, j = unit(u)
                n, half, i = P * (qt + 1), qt // 2, (qt % 2) * HPT + j
                act.wait_ge(negmax_done, b * UNITS + (u + 1))
                act.wait_ge(turned_full, b * UNITS + (u + 1))
                if i == 0:
                    act.wait_ge(norm_done, b * (2 * KD) + (2 * m + half + 1))
                copy(probs[:, u % PB, 0:n], score_ps[:, u % 2, 0:n], ACT.Exp, bias=negmax[:, u % 4:u % 4 + 1],
                     accum_out=rowsum[:, half, i:i + 1]).then_inc(score_done, 1)

            def turned_high(b, u):
                n = unit(u)[0] + 1
                act.wait_ge(turned_full, b * UNITS + (u + 1 + PB))
                act.wait_ge(value_done, b * UNITS + (u + 1))
                copy(probsT2[:, u % 2, 0, 0:n, :], turned_ps[:, u % 2, 0:n, :], ACT.Copy).then_inc(turned_hi, 1)

            act.sem_inc(score_done, 2)
            split_w("q")
            for k in range(KD):
                split_x(0, k)
            split_w("k")
            high(0, "first", ("q", 0))
            split_w("v")
            high(0, "first", ("k", 0))
            split_w("o")

            def batch(b, stage, last):
                for m in range(ST):
                    high(b, stage, ("v", m))
                if stage != "first":
                    for item in ending:
                        high(b, stage, item)
                for i in range(STEPS):
                    if i < UNITS:
                        exponentials(b, i)
                    for item in items(i - LAG_H, last):
                        high(b, stage, item)
                    if 0 <= i - LAG_T < UNITS:
                        turned_high(b, i - LAG_T)
                    if i in X_STEPS and not last:
                        act.wait_ge(proj_full, place(b, stage, ("k", KD - 1)) + 1)
                        split_x(b + 1, X_STEPS.index(i))

            batch(0, "first", False)
            with act.Fori(1, B - 1) as b:
                batch(b, "middle", False)
            batch(B - 1, "middle", True)
            for item in ending:
                high(B, "end", item)

        @block.gpsimd
        def _(pool):
            def split_x(b):
                for k in range(KD):
                    pool.wait_ge(x_hi, b * KD + (k + 1))
                    nc.gpsimd.tensor_tensor(xT2[:, 1, k, :], condT[:, k, bass.ds(b * S, S)],
                                            xT2[:, 0, k, :].bitcast(F32), ALU.subtract).then_inc(x_split, 1)

            def divide(b, m, half):
                nth = b * (2 * KD) + (2 * m + half + 1)
                pool.wait_ge(rinv_done, nth)
                pool.wait_ge(out_sum, nth)
                dst = attn[:, m % 2, 2 * half:2 * half + 2, :].rearrange("p q (j d) -> p (q j) d", d=HD)
                nc.gpsimd.tensor_tensor(dst, dst, rinv[:, half, :].unsqueeze(2).to_broadcast([P, 2 * HPT, HD]), ALU.mult
                                        ).then_inc(norm_done, 1)

            def batch(b, stage, last):
                for m in range(KD):
                    divide(b, m, 0)
                    if m == KD - 2 and not last:
                        split_x(b + 1)
                    divide(b, m, 1)

            make_constants(nc, pool, g)
            split_x(0)
            batch(0, "first", False)
            with pool.Fori(1, B - 1) as b:
                batch(b, "middle", False)
            batch(B - 1, "middle", True)

        @block.vector
        def _(dve):
            tt = nc.vector.tensor_tensor
            dve.sem_inc(proj_done, 2)
            dve.sem_inc(turned_full, PB)
            dve.sem_inc(turned_done, 2)
            dve.sem_inc(value_done, 2)
            dve.sem_inc(norm_done, 2)

            def split_w(i, n):
                dve.wait_ge(w_hi, i + 1)
                tt(w2[n][:, 1, :, :], w_raw[n], w2[n][:, 0, :, :].bitcast(F32),
                   ALU.subtract).then_inc(w_split, 1)

            def set_beta(b):
                nc.vector.tensor_scalar(beta[:, :], cond[:, bass.ds(b, 1)], 4.0, float(HD) ** -0.5, ALU.min, ALU.mult
                                        ).then_inc(beta_done, 1)

            def low(b, stage, item):
                kind, m = item
                n = place(b, stage, item)
                bank = proj_ps[:, at[stage][item] % 2, :]
                if kind == "q":
                    if m == KD:
                        dve.wait_ge(proj_done, n + 2)
                        set_beta(b + 1)
                    dve.wait_ge(beta_done, b + (m // KD + 1))
                dve.wait_ge(proj_hi, n + 1)
                if kind == "q":
                    op = nc.vector.scalar_tensor_tensor(qk2[:, 1, :], bank, beta[:, 0:1],
                                                        qk2[:, 0, :].bitcast(F32), ALU.mult, ALU.subtract)
                elif kind == "k":
                    op = tt(qk2[:, 3, :], bank, qk2[:, 2, :].bitcast(F32), ALU.subtract)
                elif kind == "v":
                    op = tt(v2[:, m, :, 1, :], bank.rearrange("p (h d) -> p h d", h=HEADS),
                            v2[:, m, :, 0, :].bitcast(F32), ALU.subtract)
                elif kind == "t":
                    op = tt(attnT2[:, 1, m % KD, :], bank, attnT2[:, 0, m % KD, :].bitcast(F32), ALU.subtract)
                else:
                    op = nc.vector.tensor_copy(condT[:, m, bass.ds(b * S - S // 2, S // 2)], bank[:, S // 2:S])
                op.then_inc(proj_done, 1)

            def maxima(b, u):
                n = P * (unit(u)[0] + 1)
                dve.wait_ge(score_full, b * UNITS + (u + 1))
                nc.vector.tensor_reduce(negmax[:, u % 4:u % 4 + 1], score_ps[:, u % 2, 0:n], AX.X, ALU.max, negate=True
                                        ).then_inc(negmax_done, 1)

            def turned_low(b, u):
                n = unit(u)[0] + 1
                dve.wait_ge(turned_hi, b * UNITS + (u + 1))
                tt(probsT2[:, u % 2, 1, 0:n, :], turned_ps[:, u % 2, 0:n, :], probsT2[:, u % 2, 0, 0:n, :].bitcast(F32),
                   ALU.subtract).then_inc(turned_done, 1)

            def normalise(b, u):
                qt, m, _ = unit(u)
                half = qt // 2
                nth = b * (2 * KD) + (2 * m + half + 1)
                dve.wait_ge(norm_done, nth)
                dve.wait_ge(value_done, b * UNITS + (u + 3))
                nc.vector.reciprocal(rinv[:, half, :], rowsum[:, half, :]).then_inc(rinv_done, 1)
                dst = attn[:, m % 2, 2 * half:2 * half + 2, :].rearrange("p q (j d) -> p (q j) d", d=HD)
                nc.vector.tensor_reduce(dst, out_ps[:, half, :, :, :].rearrange("p i v d -> p i d v"), AX.X, ALU.add
                                        ).then_inc(out_sum, 1)

            split_w(0, "q")
            dve.wait_ge(cond_in, 16)
            set_beta(0)
            split_w(1, "k")
            low(0, "first", ("q", 0))
            split_w(2, "v")
            low(0, "first", ("k", 0))
            split_w(3, "o")

            def batch(b, stage, last):
                for m in range(ST):
                    low(b, stage, ("v", m))
                if stage != "first":
                    for item in ending:
                        low(b, stage, item)
                for i in range(STEPS):
                    if i < UNITS:
                        maxima(b, i)
                    for item in items(i - LAG_H - 1, last):
                        low(b, stage, item)
                    if 0 <= i - LAG_L < UNITS:
                        turned_low(b, i - LAG_L)
                    if 0 <= i - LAG_V < UNITS and (i - LAG_V) % (2 * HPT) == 2 * HPT - 1:
                        normalise(b, i - LAG_V)

            batch(0, "first", False)
            with dve.Fori(1, B - 1) as b:
                batch(b, "middle", False)
            batch(B - 1, "middle", True)
            for item in ending:
                low(B, "end", item)


def make_constants(nc, pool, g):
    tiles = (g["ident"], g["identb"], g["mask"])
    for m in tiles:
        nc.gpsimd.memset(m[:, :], 0.0).then_inc(g["blank_done"], 1)
    pool.wait_ge(g["blank_done"], len(tiles))
    for m in tiles[:2]:
        nc.gpsimd.affine_select(out=m[:, :], in_=m[:, :], compare_op=ALU.not_equal, fill=1.0, base=0,
                                pattern=[[-1, P]], channel_multiplier=1).then_inc(g["ident_done"], 1)
    nc.gpsimd.affine_select(out=g["mask"][:, :], in_=g["mask"][:, :], compare_op=ALU.is_ge, fill=NEG, base=0,
                            pattern=[[-1, P]], channel_multiplier=1).then_inc(g["ident_done"], 2)


def experts(nc, d, g):
    STEP = 5
    SHARED = 2
    NS = SHARED * CH
    GT = CW // P
    with ExitStack() as ctx:
        def sb(name, shape, dt):
            return ctx.enter_context(nc.sbuf_tensor(name, shape, dt))

        def sem(name):
            return ctx.enter_context(nc.semaphore(name))

        condT, x1T = g["condT"], g["x1T"]
        raw_ab = sb("raw_ab", [P, ACOLS], F32)
        raw_c = sb("raw_c", [P, CCOLS], F32)
        gate2 = sb("gate2", [P, 2, KD, I], F32R)
        up2 = sb("up2", [P, 2, KD, I], F32R)
        down2 = sb("down2", [P, 2, 3, D], F32R)
        mu2 = sb("mu2", [P, D], F32R)
        qa2 = sb("qa2", [P, 2, KD, 2 * LR], F32R)
        qb2 = sb("qb2", [P, 2, 2, I], F32R)
        dqa2 = sb("dqa2", [P, 2, 3, 2 * LR], F32R)
        dqb2 = sb("dqb2", [P, 2, D], F32R)
        mu_mask = sb("mu_mask", [P, 2], F32)
        mult_w = sb("mult_w", [P, 4, CW], F32)
        slot_w = mult_w[:, 0:2, :]
        gate_w = mult_w[:, 2:4, :]
        slot2 = sb("slot2", [P, CW], F32R)
        xe32 = sb("xe32", [P, 2, CW], F32)
        xe2 = sb("xe2", [P, 2, 2, KD, CW], F32R)
        sg = sb("sg", [P, 2, CW], F32)
        hid2 = sb("hid2", [P, 2, 3, CW], F32R)
        low32 = sb("low32", [P, CW], F32)
        lowg = sb("lowg", [P, CW], F32R)
        lowu = sb("lowu", [P, CW], F32R)
        dlow2 = sb("dlow2", [P, CW], F32R)
        wide = ctx.enter_context(nc.psum_tensor("wide", [P, 2, 2, CW], F32))
        xe_ps = ctx.enter_context(nc.psum_tensor("xe_ps", [P, 2, CW], F32))
        low_ps = ctx.enter_context(nc.psum_tensor("low_ps", [P, CW], F32))
        dlow_ps = ctx.enter_context(nc.psum_tensor("dlow_ps", [P, CW], F32))

        x_res_in = sem("x_res_in")
        router_in = sem("router_in")
        wa_in = sem("wa_in")
        wb_in = sem("wb_in")
        wc_in = sem("wc_in")
        slot_in = [sem(f"slot_in{s}") for s in range(2)]
        gu_hi = sem("gu_hi")
        gu_split = sem("gu_split")
        qb_scaled = sem("qb_scaled")
        qb_hi = sem("qb_hi")
        qb_split = sem("qb_split")
        dn_hi = sem("dn_hi")
        dn_split = sem("dn_split")
        dqb_scaled = sem("dqb_scaled")
        dl_hi = sem("dl_hi")
        dl_split = sem("dl_split")
        early_hi = sem("early_hi")
        qa_split = sem("qa_split")
        mu_rest = sem("mu_rest")
        mu_split = sem("mu_split")
        slot_hi = sem("slot_hi")
        slot_split = sem("slot_split")
        xe_full = sem("xe_full")
        xe_sum = sem("xe_sum")
        xe_hi = sem("xe_hi")
        xe_split = sem("xe_split")
        low_full = sem("low_full")
        low_sum = sem("low_sum")
        low_hi = sem("low_hi")
        low_split = sem("low_split")
        dlow_full = sem("dlow_full")
        dlow_sum = sem("dlow_sum")
        dlow_hi = sem("dlow_hi")
        dlow_split = sem("dlow_split")
        wide_full = sem("wide_full")
        wide_done = sem("wide_done")
        silu_done = sem("silu_done")
        up_weighed = sem("up_weighed")
        hid_hi = sem("hid_hi")
        hid_split = sem("hid_split")
        logits_full = sem("logits_full")
        rstep = sem("rstep")
        r_exp = sem("r_exp")
        route_ready = sem("route_ready")
        turned = sem("turned")
        turned_out = sem("turned_out")
        route_out = sem("route_out")

        area = mult_w[:, :, :].rearrange("p a n -> p (a n)")
        place = [0]

        def routing_tile(n):
            a = place[0]
            place[0] += GT * n
            return area[:, a:a + GT * n].rearrange("p (t e) -> p t e", t=GT)

        score, work, flat, eq = (routing_tile(E) for _ in range(4))
        soft = routing_tile(E + F)
        top, topi, topf, stat, stat2 = (routing_tile(F) for _ in range(5))
        inv = area[:, place[0]:place[0] + E]
        inv_i = area[:, place[0] + E:place[0] + 2 * E].bitcast(I32)
        router_w = xe32[:, 0, 0:KD * E].rearrange("p (k e) -> p k e", k=KD)
        routeT = low32[0:E + F, :]

        def a_of(name, kt=None, cols=AC):
            a, z = cols[name]
            t = (raw_c if cols is CC else raw_ab)[:, a:z]
            return t if kt is None else t.rearrange("p (k n) -> p k n", k=kt)

        def parity(c, m):
            return (c * STEP + m) % 2

        def chunk(c):
            return slice(c * CW, (c + 1) * CW)

        def slot_loads(n, c):
            return (n - NS - c) * (96 // CH) + 48 * (c // 2 + 1)

        block = ctx.enter_context(nc.Block())


        @block.sync
        def _(sp):
            def pick(name, e):
                f = e - SHARED
                if isinstance(f, int):
                    return d[name][f, :, :]
                return d[name][bass.ds(f, 1), :, :].rearrange("a p n -> p (a n)")

            def load_a(e, shared=False):
                if shared:
                    sp.dma_start(raw_ab[:, 0:2 * KD * I], d["shared_a"][e, :, :]).then_inc(wa_in, 16)
                else:
                    sp.dma_start(raw_ab[:, 0:ACOLS], pick("expert_a", e)).then_inc(wa_in, 16)

            def load_b(e, shared=False):
                if not shared:
                    sp.wait_ge(qb_split, e - SHARED + 1)
                sp.wait_ge(gu_split, e * 2 + 2)
                if shared:
                    sp.dma_start(raw_ab[:, 0:3 * D], d["shared_b"][e, :, :]).then_inc(wb_in, 16)
                else:
                    sp.dma_start(raw_ab[:, 0:BCOLS], pick("expert_b", e)).then_inc(wb_in, 16)

            def load_c(e):
                sp.dma_start(raw_c[:, :], pick("expert_c", e)).then_inc(wc_in, 16)

            def load_slots(e, c, s):
                f = e - SHARED
                if isinstance(f, int):
                    rows, scalar = d["route"][f * KR:(f + 1) * KR, chunk(c)], d["route"][E + f:E + f + 1, chunk(c)]
                else:
                    rows = d["route"][bass.ds(f * KR, KR), chunk(c)]
                    scalar = d["route"][bass.ds(f + E, 1), chunk(c)]
                for half in range(2):
                    sp.dma_start(slot_w[half * LR:(half + 1) * LR, s, :],
                                 rows.unsqueeze(1).to_broadcast([KR, R, CW])).then_inc(slot_in[s], 16)
                sp.dma_start(gate_w[:, s, :], scalar.to_broadcast([P, CW])).then_inc(slot_in[s], 16)

            load_a(0, True)
            sp.dma_start(router_w, d["router"].rearrange("(k p) e -> p k e", p=P)).then_inc(router_in, 16)
            sp.dma_start(inv_i, d["inv"].to_broadcast([P, E])).then_inc(router_in, 16)
            sp.dma_start(mu_mask[:, :], d["mu_mask"]).then_inc(router_in, 16)
            load_b(0, True)
            for b in range(B):
                sp.dma_start(x1T[:, :, b * S:(b + 1) * S],
                             d["xT"][b, :, :].rearrange("(k p) s -> p k s", p=P)).then_inc(x_res_in, 16)
            load_c(SHARED)
            sp.wait_ge(dn_split, 1)
            load_a(1, True)
            for q in range(CH):
                sp.wait_ge(turned_out, q + 1)
                sp.dma_start(d["route"][:, chunk(q)], routeT).then_inc(route_out, 16)
                if q == CH - 2:
                    load_b(1, True)
            sp.wait_ge(route_out, 16 * CH)
            sp.wait_ge(dn_split, 2)
            load_a(SHARED)
            load_slots(SHARED, 0, 0)

            def expert(it, last):
                e = it + SHARED
                for c in range(CH):
                    if c == 0:
                        sp.wait_ge(low_sum, it * CH + 1)
                    else:
                        sp.wait_ge(dlow_sum, it * CH + c)
                    if c < CH - 1:
                        load_slots(e, c + 1, (c + 1) % 2)
                    elif not last:
                        load_slots(e + 1, 0, 0)
                    if c == 1 and not last:
                        sp.wait_ge(dn_split, e + 1)
                        sp.wait_ge(dl_split, it * 2 + 2)
                        load_a(e + 1)
                        sp.wait_ge(qa_split, it + 1)
                        sp.wait_ge(mu_split, it + 1)
                        load_c(e + 1)
                    if c == CH - 1 and not last:
                        load_b(e + 1)

            load_b(SHARED)
            with sp.Fori(0, F - 1) as it:
                expert(it, False)
            expert(F - 1, True)

        @block.tensor
        def _(pe):
            def products(out, lhs, rhs, start, stop):
                for k, (a, b) in enumerate(zip(lhs, rhs)):
                    nc.tensor.matmul(out, a[0], b[0], start=start and k == 0, stop=False)
                    nc.tensor.matmul(out, a[0], b[1], start=False, stop=False)
                    last = nc.tensor.matmul(out, a[1], b[0], start=False, stop=stop and k == len(lhs) - 1)
                return last

            def gate_up(n, c, m, routed):
                i0, rows = IT[m]
                cols = slice(i0, i0 + rows)
                pe.wait_ge(wide_done, n * STEP + (m + 1))
                x = [(xe2[:, c % 2, 0, k, :], xe2[:, c % 2, 1, k, :]) for k in range(KD)]
                for j, w in enumerate((gate2, up2)):
                    last = products(wide[0:rows, parity(c, m), j, :],
                                    [(w[:, 0, k, cols], w[:, 1, k, cols]) for k in range(KD)], x, True, not routed)
                if routed:
                    if m == 0:
                        pe.wait_ge(low_split, (n - NS) * 2 + 2)
                    for j, low in enumerate((lowg, lowu)):
                        out = wide[0:rows, parity(c, m), j, :]
                        nc.tensor.matmul(out, qb2[:, 0, j, cols], low[:, :], start=False, stop=False)
                        last = nc.tensor.matmul(out, qb2[:, 1, j, cols], low[:, :], start=False, stop=True)
                last.then_inc(wide_full, 1)

            def project_slots(n, half):
                pe.wait_ge(xe_sum, (n - NS) * 2 + (half + 1))
                if half == 0:
                    pe.wait_ge(slot_split, n - NS + 1)
                for j in range(2):
                    m = 2 * half + j
                    last = nc.tensor.matmul(xe_ps[:, j, :], mu2[:, m * P:(m + 1) * P], slot2[:, :],
                                            start=True, stop=True)
                last.then_inc(xe_full, 1)

            def low_rank(n, c):
                pe.wait_ge(xe_split, n * 2 + 2)
                products(low_ps[:, :], [(qa2[:, 0, k, :], qa2[:, 1, k, :]) for k in range(KD)],
                         [(xe2[:, c % 2, 0, k, :], xe2[:, c % 2, 1, k, :]) for k in range(KD)], True, True
                         ).then_inc(low_full, 1)

            def down(n, c, e, routed):
                if c == 0:
                    pe.wait_ge(dn_split, e + 1)
                    if routed:
                        pe.wait_ge(dl_split, (e - SHARED) * 2 + 2)
                h = [(hid2[0:rows, 0, m, :], hid2[0:rows, 1, m, :]) for m, (_, rows) in enumerate(IT)]
                if routed:
                    pe.wait_ge(hid_split, n * 3 + 2)
                    products(dlow_ps[:, :], [(dqa2[:, 0, m, :], dqa2[:, 1, m, :]) for m in range(2)], h[:2], True, False)
                    pe.wait_ge(hid_split, n * 3 + 3)
                    rows = IT[2][1]
                    products(dlow_ps[:, :], [(dqa2[0:rows, 0, 2, :], dqa2[0:rows, 1, 2, :])], h[2:], False, True
                             ).then_inc(dlow_full, 1)
                else:
                    pe.wait_ge(hid_split, n * 3 + 3)
                for pair in range(2):
                    pe.wait_ge(wide_done, n * STEP + (3 + pair + 1))
                    for j in range(2):
                        h0 = (2 * pair + j) * P
                        w = [(down2[0:rows, 0, m, h0:h0 + P], down2[0:rows, 1, m, h0:h0 + P])
                             for m, (_, rows) in enumerate(IT)]
                        last = products(wide[:, parity(c, 3 + pair), j, :], w, h, True, not routed)
                    if routed:
                        if pair == 0:
                            pe.wait_ge(dlow_split, n - NS + 2)
                        for j in range(2):
                            h0 = (2 * pair + j) * P
                            out = wide[:, parity(c, 3 + pair), j, :]
                            nc.tensor.matmul(out, dqb2[:, 0, h0:h0 + P], dlow2[:, :], start=False, stop=False)
                            last = nc.tensor.matmul(out, dqb2[:, 1, h0:h0 + P], dlow2[:, :], start=False, stop=True)
                    last.then_inc(wide_full, 1)

            def turn(q):
                pe.wait_ge(route_ready, q + 1)
                if q >= 1:
                    pe.wait_ge(turned_out, q)
                for t in range(GT):
                    last = nc.tensor.transpose(xe_ps[0:E + F, 1, t * P:(t + 1) * P], soft[:, t, :], g["ident"][:, :])
                last.then_inc(turned, 1)

            for n in range(NS):
                e, c = divmod(n, CH)
                if n < CH:
                    if n == 0:
                        pe.wait_ge(router_in, 48)
                    else:
                        pe.wait_ge(r_exp, 2 * n - 1)
                    for t in range(GT):
                        for k in range(KD):
                            tok = (n * GT + t) * P
                            last = nc.tensor.matmul(xe_ps[:, 0, t * E:(t + 1) * E], condT[:, k, tok:tok + P],
                                                    router_w[:, k, :], start=k == 0, stop=k == KD - 1)
                    last.then_inc(logits_full, 1)
                if c == 0:
                    pe.wait_ge(gu_split, e * 2 + 2)
                pe.wait_ge(xe_split, n * 2 + 2)
                gate_up(n, c, 0, False)
                if n == NS - 1:
                    pe.wait_ge(mu_split, 1)
                    project_slots(NS, 0)
                gate_up(n, c, 1, False)
                if 1 <= n <= CH:
                    turn(n - 1)
                if n == NS - 1:
                    project_slots(NS, 1)
                gate_up(n, c, 2, False)
                if n == NS - 1:
                    pe.wait_ge(qa_split, 1)
                    low_rank(NS, 0)
                down(n, c, e, False)

            def expert(it, last):
                e = it + SHARED
                for c in range(CH):
                    n = it * CH + (NS + c)
                    following = not (last and c == CH - 1)
                    if c == 0:
                        pe.wait_ge(gu_split, e * 2 + 2)
                        pe.wait_ge(qb_split, it + 1)
                    gate_up(n, c, 0, True)
                    if following:
                        if c == CH - 1:
                            pe.wait_ge(mu_split, it + 2)
                        project_slots(n + 1, 0)
                    gate_up(n, c, 1, True)
                    if following:
                        project_slots(n + 1, 1)
                    gate_up(n, c, 2, True)
                    if following:
                        if c == CH - 1:
                            pe.wait_ge(qa_split, it + 2)
                        low_rank(n + 1, (c + 1) % CH)
                    down(n, c, e, True)

            with pe.Fori(0, F - 1) as it:
                expert(it, False)
            expert(F - 1, True)

        @block.scalar
        def _(act):
            copy = nc.scalar.activation

            def split_gate_up(e, routed):
                act.wait_ge(wa_in, e * 16 + 16)
                copy(gate2[:, 0, :, :], a_of("gate", KD), ACT.Copy).then_inc(gu_hi, 1)
                copy(up2[:, 0, :, :], a_of("up", KD), ACT.Copy).then_inc(gu_hi, 1)
                if routed:
                    act.wait_ge(qb_scaled, e - SHARED + 1)
                    copy(qb2[:, 0, :, :], a_of("qb", 2), ACT.Copy).then_inc(qb_hi, 1)

            def split_down(e, routed):
                act.wait_ge(wb_in, e * 16 + 16)
                copy(down2[:, 0, :, :], a_of("down", 3, BC), ACT.Copy).then_inc(dn_hi, 1)
                if routed:
                    copy(dqa2[:, 0, :, :], a_of("dqa", 3, BC), ACT.Copy).then_inc(dl_hi, 1)
                    act.wait_ge(dqb_scaled, e - SHARED + 1)
                    copy(dqb2[:, 0, :], a_of("dqb", None, BC), ACT.Copy).then_inc(dl_hi, 1)

            def split_early(f):
                act.wait_ge(wc_in, f * 16 + 16)
                copy(mu2[:, :], a_of("mu", None, CC), ACT.Copy).then_inc(early_hi, 1)
                copy(qa2[:, 0, :, :], a_of("qa", KD, CC), ACT.Copy).then_inc(early_hi, 1)

            def input_half(n, c, half, routed):
                m = slice(2 * half, 2 * half + 2)
                if routed:
                    act.wait_ge(xe_sum, (n - NS) * 2 + (half + 2))
                    src = xe32[:, :, :]
                else:
                    src = condT[:, m, chunk(c)]
                copy(xe2[:, c % 2, 0, m, :], src, ACT.Copy).then_inc(xe_hi, 1)

            def slots(n, c):
                act.wait_ge(slot_in[c % 2], slot_loads(n, c))
                copy(slot2[:, :], slot_w[:, c % 2, :], ACT.Copy).then_inc(slot_hi, 1)

            def silu(n, c, m):
                rows = IT[m][1]
                act.wait_ge(wide_full, n * STEP + (m + 1))
                if m == 2:
                    act.wait_ge(hid_split, n * 3 + 1)
                copy(sg[0:rows, parity(c, m), :], wide[0:rows, parity(c, m), 0, :], ACT.Silu).then_inc(silu_done, 1)

            def hidden_hi(n, c, m):
                rows = IT[m][1]
                act.wait_ge(wide_done, n * STEP + (m + 3))
                copy(hid2[0:rows, 0, m, :], sg[0:rows, parity(c, m), :], ACT.Copy).then_inc(hid_hi, 1)

            def low_rank_hi(n):
                act.wait_ge(low_sum, n - NS + 1)
                copy(lowg[0:LR, :], low32[0:LR, :], ACT.Copy).then_inc(low_hi, 1)
                copy(lowu[LR:2 * LR, :], low32[LR:2 * LR, :], ACT.Copy).then_inc(low_hi, 1)

            def dlow_rank_hi(n):
                act.wait_ge(dlow_sum, n - NS + 1)
                copy(dlow2[:, :], low32[:, :], ACT.Copy).then_inc(dlow_hi, 1)

            split_gate_up(0, False)
            input_half(0, 0, 0, False)
            input_half(0, 0, 1, False)
            for n in range(NS):
                e, c = divmod(n, CH)
                nxt = (n + 1, (c + 1) % CH)
                routed = n == NS - 1
                if n < CH:
                    act.wait_ge(rstep, g["r_first"] + n * g["r_all"])
                    copy(score, work, ACT.Exp).then_inc(r_exp, 1)
                if routed:
                    split_early(0)
                    slots(*nxt)
                silu(n, c, 0)
                if c == 0:
                    split_down(e, False)
                input_half(*nxt, 0, routed)
                silu(n, c, 1)
                hidden_hi(n, c, 0)
                input_half(*nxt, 1, routed)
                if 1 <= n <= CH:
                    act.wait_ge(turned, n)
                    if n >= 2:
                        act.wait_ge(route_out, 16 * (n - 1))
                    copy(routeT, xe_ps[0:E + F, 1, :], ACT.Copy).then_inc(turned_out, 1)
                silu(n, c, 2)
                hidden_hi(n, c, 1)
                hidden_hi(n, c, 2)
                if n < CH:
                    act.wait_ge(rstep, g["r_second"] + n * g["r_all"])
                    copy(work, eq, ACT.Exp).then_inc(r_exp, 1)
                if c == CH - 1:
                    split_gate_up(e + 1, n == NS - 1)
                if routed:
                    low_rank_hi(NS)

            def expert(it, last):
                e = it + SHARED
                for c in range(CH):
                    n = it * CH + (NS + c)
                    following = not (last and c == CH - 1)
                    nxt = (n + 1, (c + 1) % CH)
                    if following:
                        if c == CH - 1:
                            split_early(it + 1)
                        slots(*nxt)
                    silu(n, c, 0)
                    if c == 0:
                        split_down(e, True)
                    if following:
                        input_half(*nxt, 0, True)
                    silu(n, c, 1)
                    hidden_hi(n, c, 0)
                    if following:
                        input_half(*nxt, 1, True)
                    silu(n, c, 2)
                    hidden_hi(n, c, 1)
                    hidden_hi(n, c, 2)
                    if following:
                        low_rank_hi(n + 1)
                    dlow_rank_hi(n)
                    if c == CH - 1 and not last:
                        split_gate_up(e + 1, True)

            with act.Fori(0, F - 1) as it:
                expert(it, False)
            expert(F - 1, True)

        @block.gpsimd
        def _(pool):
            sub = nc.gpsimd.tensor_tensor

            def input_half(n, c, half, routed):
                m = slice(2 * half, 2 * half + 2)
                pool.wait_ge(xe_hi, n * 2 + (half + 1))
                src = xe32[:, :, :] if routed else condT[:, m, chunk(c)]
                sub(xe2[:, c % 2, 1, m, :], src, xe2[:, c % 2, 0, m, :].bitcast(F32), ALU.subtract).then_inc(xe_split, 1)

            def scale_qb(e):
                pool.wait_ge(wa_in, e * 16 + 16)
                sub(a_of("qb"), a_of("qb"), a_of("qscale"), ALU.mult).then_inc(qb_scaled, 1)

            def qb_low(e):
                pool.wait_ge(qb_hi, e - SHARED + 1)
                sub(qb2[:, 1, :, :], a_of("qb", 2), qb2[:, 0, :, :].bitcast(F32), ALU.subtract).then_inc(qb_split, 1)

            def down_low(e):
                pool.wait_ge(wb_in, e * 16 + 16)
                sub(a_of("dqb", None, BC), a_of("dqb", None, BC), a_of("dscale", None, BC), ALU.mult
                    ).then_inc(dqb_scaled, 1)
                pool.wait_ge(dl_hi, (e - SHARED) * 2 + 1)
                sub(dqa2[:, 1, :, :], a_of("dqa", 3, BC), dqa2[:, 0, :, :].bitcast(F32), ALU.subtract
                    ).then_inc(dl_split, 1)
                pool.wait_ge(dl_hi, (e - SHARED) * 2 + 2)
                sub(dqb2[:, 1, :], a_of("dqb", None, BC), dqb2[:, 0, :].bitcast(F32), ALU.subtract
                    ).then_inc(dl_split, 1)

            def early_low(f):
                pool.wait_ge(early_hi, f * 2 + 2)
                sub(qa2[:, 1, :, :], a_of("qa", KD, CC), qa2[:, 0, :, :].bitcast(F32), ALU.subtract).then_inc(qa_split, 1)

            input_half(0, 0, 0, False)
            input_half(0, 0, 1, False)
            for n in range(NS):
                c = n % CH
                routed = n == NS - 1
                if routed:
                    early_low(0)
                input_half(n + 1, (c + 1) % CH, 0, routed)
                input_half(n + 1, (c + 1) % CH, 1, routed)
                if routed:
                    scale_qb(SHARED)
                    qb_low(SHARED)

            def expert(it, last):
                e = it + SHARED
                for c in range(CH):
                    n = it * CH + (NS + c)
                    following = not (last and c == CH - 1)
                    if c == CH - 1 and following:
                        early_low(it + 1)
                    if c == 0:
                        down_low(e)
                    if following:
                        input_half(n + 1, (c + 1) % CH, 0, True)
                        input_half(n + 1, (c + 1) % CH, 1, True)
                    if c == CH - 2 and not last:
                        scale_qb(e + 1)
                    if c == CH - 1 and not last:
                        qb_low(e + 1)

            with pool.Fori(0, F - 1) as it:
                expert(it, False)
            expert(F - 1, True)

        @block.vector
        def _(dve):
            tt = nc.vector.tensor_tensor
            dve.sem_inc(wide_done, 2)
            dve.sem_inc(xe_sum, 1)
            dve.sem_inc(dlow_split, 1)
            done = [0]

            def link(op):
                done[0] += 1
                op.then_inc(rstep, 1)
                dve.wait_ge(rstep, done[0])

            def over(x, n):
                return x.unsqueeze(3).to_broadcast([P, x.shape[1], x.shape[2], n])

            def column(x, j, n):
                return x[:, :, j:j + 1].to_broadcast([P, GT, n])

            def by_expert(x):
                return x.rearrange("p t (f k) -> p t f k", k=KR)

            def route_1(q):
                dve.wait_ge(logits_full, q + 1)
                logits = xe_ps[:, 0, 0:GT * E].rearrange("p (t e) -> p t e", e=E)
                link(nc.vector.tensor_reduce(stat[:, :, 0], logits, AX.X, ALU.max))
                link(tt(work, logits, column(stat, 0, E), ALU.subtract))

            def route_2(q):
                dve.wait_ge(r_exp, 2 * q + 1)
                link(nc.vector.tensor_reduce(stat[:, :, 1], score, AX.X, ALU.add))
                link(nc.vector.reciprocal(stat[:, :, 2], stat[:, :, 1]))
                link(tt(score, score, column(stat, 2, E), ALU.mult))
                for t in range(GT):
                    link(nc.vector.max(top[:, t, :], score[:, t, :]))
                    link(nc.vector.max_index(topi[:, t, :].bitcast(U32), top[:, t, :], score[:, t, :]))
                link(nc.vector.tensor_copy(topf, topi.bitcast(U32)))

            def route_3(q):
                inv_b = inv.unsqueeze(1).to_broadcast([P, GT, E])
                for j in range(TOPK):
                    link(tt(eq, inv_b, column(topf, j, E), ALU.is_equal))
                    link(tt(work if j else flat, eq, column(top, j, E), ALU.mult))
                    if j:
                        link(tt(flat, flat, work, ALU.add))

            def route_4(q):
                link(nc.vector.tensor_reduce(soft[:, :, E:E + F], by_expert(flat), AX.X, ALU.add))
                link(nc.vector.tensor_scalar(eq, flat, 0.0, -1.0e9, ALU.is_equal, ALU.mult))
                link(tt(eq, eq, flat, ALU.add))
                link(nc.vector.tensor_reduce(stat, by_expert(eq), AX.X, ALU.max))
                link(tt(by_expert(eq), by_expert(eq), over(stat, KR), ALU.subtract))

            def route_5(q):
                dve.wait_ge(r_exp, 2 * q + 2)
                link(nc.vector.tensor_reduce(stat, by_expert(work), AX.X, ALU.add))
                link(nc.vector.reciprocal(stat2, stat))
                tt(by_expert(soft[:, :, 0:E]), by_expert(work), over(stat2, KR), ALU.mult).then_inc(route_ready, 1)
                dve.wait_ge(route_ready, q + 1)

            def hidden(n, c, m, routed):
                rows = IT[m][1]
                slot = parity(c, m)
                if routed:
                    dve.wait_ge(wide_full, n * STEP + (m + 1))
                    if m == 0:
                        dve.wait_ge(slot_in[c % 2], slot_loads(n, c))
                    tt(wide[0:rows, slot, 1, :], wide[0:rows, slot, 1, :], gate_w[0:rows, c % 2, :], ALU.mult
                       ).then_inc(up_weighed, 1)
                    dve.wait_ge(up_weighed, (n - NS) * 3 + (m + 1))
                dve.wait_ge(silu_done, n * 3 + (m + 1))
                tt(sg[0:rows, slot, :], wide[0:rows, slot, 1, :], sg[0:rows, slot, :], ALU.mult).then_inc(wide_done, 1)

            def hidden_low(n, c, m):
                rows = IT[m][1]
                dve.wait_ge(hid_hi, n * 3 + (m + 1))
                tt(hid2[0:rows, 1, m, :], sg[0:rows, parity(c, m), :], hid2[0:rows, 0, m, :].bitcast(F32), ALU.subtract
                   ).then_inc(hid_split, 1)

            def slots_low(n, c):
                dve.wait_ge(slot_hi, n - NS + 1)
                tt(slot2[LR:2 * LR, :], slot_w[LR:2 * LR, c % 2, :], slot2[LR:2 * LR, :].bitcast(F32), ALU.subtract
                   ).then_inc(slot_split, 1)

            def add_x(n, c, half):
                dve.wait_ge(xe_full, (n - NS) * 2 + (half + 1))
                dve.wait_ge(xe_split, n * 2 + half)
                tt(xe32[:, :, :], xe_ps[:, :, :], condT[:, 2 * half:2 * half + 2, chunk(c)], ALU.add
                   ).then_inc(xe_sum, 1)

            def weigh_low(n, c, after):
                dve.wait_ge(low_full, n - NS + 1)
                if after:
                    dve.wait_ge(low_split, (n - NS) * 2)
                    dve.wait_ge(dlow_split, n - NS)
                tt(low32[:, :], low_ps[:, :], slot_w[:, c % 2, :], ALU.mult).then_inc(low_sum, 1)

            def low_low(n):
                dve.wait_ge(low_hi, (n - NS) * 2 + 1)
                tt(lowg[LR:2 * LR, :], low32[0:LR, :], lowg[0:LR, :].bitcast(F32), ALU.subtract).then_inc(low_split, 1)
                dve.wait_ge(low_hi, (n - NS) * 2 + 2)
                tt(lowu[0:LR, :], low32[LR:2 * LR, :], lowu[LR:2 * LR, :].bitcast(F32), ALU.subtract
                   ).then_inc(low_split, 1)

            def weigh_dlow(n, c, following):
                dve.wait_ge(dlow_full, n - NS + 1)
                dve.wait_ge(low_split, (n - NS + following) * 2 + 2)
                tt(low32[:, :], dlow_ps[:, :], slot_w[:, c % 2, :], ALU.mult).then_inc(dlow_sum, 1)

            def dlow_low(n):
                dve.wait_ge(dlow_hi, n - NS + 1)
                tt(dlow2[LR:2 * LR, :], low32[LR:2 * LR, :], dlow2[LR:2 * LR, :].bitcast(F32), ALU.subtract
                   ).then_inc(dlow_split, 1)

            def add_out(n, c, pair):
                dve.wait_ge(wide_full, n * STEP + (3 + pair + 1))
                acc = x1T[:, 2 * pair:2 * pair + 2, chunk(c)]
                tt(acc, wide[:, parity(c, 3 + pair), :, :], acc, ALU.add).then_inc(wide_done, 1)

            def gate_up_low(e, j):
                dve.wait_ge(gu_hi, e * 2 + (j + 1))
                w, name = ((gate2, "gate"), (up2, "up"))[j]
                tt(w[:, 1, :, :], a_of(name, KD), w[:, 0, :, :].bitcast(F32), ALU.subtract).then_inc(gu_split, 1)

            def down_low(e):
                dve.wait_ge(dn_hi, e + 1)
                tt(down2[:, 1, :, :], a_of("down", 3, BC), down2[:, 0, :, :].bitcast(F32), ALU.subtract
                   ).then_inc(dn_split, 1)

            def mu_low(f):
                dve.wait_ge(early_hi, f * 2 + 1)
                raw = a_of("mu", None, CC)
                tt(raw, raw, mu2[:, :].bitcast(F32), ALU.subtract).then_inc(mu_rest, 1)
                dve.wait_ge(mu_rest, f * 2 + 1)
                nc.vector.tensor_scalar(raw, raw, mu_mask[:, 1:2], None, ALU.mult).then_inc(mu_rest, 1)
                dve.wait_ge(mu_rest, f * 2 + 2)
                nc.vector.scalar_tensor_tensor(mu2[:, :], mu2[:, :].bitcast(F32), mu_mask[:, 0:1], raw,
                                               ALU.mult, ALU.add).then_inc(mu_split, 1)

            gate_up_low(0, 0)
            gate_up_low(0, 1)
            dve.wait_ge(router_in, 48)
            link(nc.vector.tensor_copy(inv, inv_i))
            for n in range(NS):
                e, c = divmod(n, CH)
                if n < CH:
                    route_1(n)
                    assert done[0] == g["r_first"] + n * g["r_all"], done
                if n == NS - 1:
                    mu_low(0)
                    slots_low(NS, 0)
                hidden(n, c, 0, False)
                if c == 0:
                    down_low(e)
                if n == 0:
                    dve.wait_ge(x_res_in, 16 * B)
                if n < CH:
                    route_2(n)
                if n == NS - 1:
                    add_x(NS, 0, 0)
                hidden(n, c, 1, False)
                hidden_low(n, c, 0)
                if n < CH:
                    route_3(n)
                if n == NS - 1:
                    add_x(NS, 0, 1)
                hidden(n, c, 2, False)
                hidden_low(n, c, 1)
                hidden_low(n, c, 2)
                if n < CH:
                    route_4(n)
                    assert done[0] == g["r_second"] + n * g["r_all"], done
                    route_5(n)
                if c == CH - 1:
                    gate_up_low(e + 1, 0)
                    gate_up_low(e + 1, 1)
                if n == NS - 1:
                    weigh_low(NS, 0, False)
                    low_low(NS)
                add_out(n, c, 0)
                add_out(n, c, 1)

            def expert(it, last):
                e = it + SHARED
                for c in range(CH):
                    n = it * CH + (NS + c)
                    following = not (last and c == CH - 1)
                    nc_ = (c + 1) % CH
                    if following:
                        if c == CH - 1:
                            mu_low(it + 1)
                        slots_low(n + 1, nc_)
                    hidden(n, c, 0, True)
                    if c == 0:
                        down_low(e)
                    if following:
                        add_x(n + 1, nc_, 0)
                    hidden(n, c, 1, True)
                    hidden_low(n, c, 0)
                    if following:
                        add_x(n + 1, nc_, 1)
                    hidden(n, c, 2, True)
                    hidden_low(n, c, 1)
                    hidden_low(n, c, 2)
                    if following:
                        weigh_low(n + 1, nc_, True)
                        low_low(n + 1)
                    weigh_dlow(n, c, following)
                    dlow_low(n)
                    if c == CH - 1 and not last:
                        gate_up_low(e + 1, 0)
                        gate_up_low(e + 1, 1)
                    add_out(n, c, 0)
                    add_out(n, c, 1)

            with dve.Fori(0, F - 1) as it:
                expert(it, False)
            expert(F - 1, True)


def ffn(nc, d, g):
    NT = T // P
    GC = 4
    GW = L1I // GC
    RING = 3
    RAW = 8
    FIRST_COND = 9
    with ExitStack() as ctx:
        def sb(name, shape, dt):
            return ctx.enter_context(nc.sbuf_tensor(name, shape, dt))

        def sem(name):
            return ctx.enter_context(nc.semaphore(name))

        x1T = g["x1T"]
        wgT = sb("wgT", [P, KD, L1I], BF16)
        wuT = sb("wuT", [P, KD, L1I], BF16)
        wdT = sb("wdT", [P, L1T, D], BF16)
        gscale = sb("gscale", [P, L1I], F32)
        uscale = sb("uscale", [P, L1I], F32)
        dscale = sb("dscale", [P, D], F32)
        idx = sb("idx", [P, L1T], I32)
        spare = g["condT"][:, :, :].rearrange("p k n -> p (k n)")
        fin = spare[:, RING * L1I:RING * L1I + 3 * D].rearrange("p (a n) -> p a n", a=3)
        x1 = spare[:, RING * L1I + 3 * D:RING * L1I + 7 * D].rearrange("p (a n) -> p a n", a=4)
        wy = sb("wy", [P, RING, L1I], F32)
        wgrid = sb("wgrid", [P, RING, L1I], F32)
        rowq = sb("rowq", [P, 2, L1I], BF16)
        hid = wy[:, 0:2, :]
        hy = wy[:, 2, :]
        hgrid = wgrid[:, 0, :]
        xy = wgrid[:, 1, 0:D]
        xgrid = wgrid[:, 1, D:2 * D]
        colscale = sb("colscale", [P, 2 * L1T + KD], F32)
        amax = sb("amax", [P, 4], F32)
        rcp = sb("rcp", [P, RING], F32)
        condW = sb("condW", [P, KD, D], F32)
        condWb = sb("condWb", [P, 2, KD, D], F32)
        adA = sb("adA", [RANK, 2, D], F32)
        adB = sb("adB", [RANK, 2, D], F32)
        adS = sb("adS", [RANK, 2], F32)
        adBs = sb("adBs", [RANK, 2, D], F32)
        itok = sb("itok", [1, B], I32)
        xq = sb("xq", [P, D], BF16)
        xqT = sb("xqT", [P, KD, P], BF16)
        xs = sb("xs", [P, 4], F32)
        xr = sb("xr", [P, 2], F32)
        zg = sb("zg", [P, 2, GW], F32)
        sg = sb("sg_l1", [P, 2, GW], F32)
        hs = sb("hs", [P, 4], F32)
        hr = sb("hr", [P, 2], F32)
        hq = sb("hq", [P, L1I], BF16)
        hqT = sb("hqT", [P, L1T, P], BF16)

        xc_ps = ctx.enter_context(nc.psum_tensor("xc_ps", [P, D], F32))
        misc = ctx.enter_context(nc.psum_tensor("misc", [P, 2, 512], F32))
        gu = ctx.enter_context(nc.psum_tensor("gu", [P, 2, 2, 512], F32))
        out_ps = ctx.enter_context(nc.psum_tensor("out_ps_l1", [P, D], F32))

        idx_in = sem("idx_in")
        itok_in = sem("itok_in")
        condW_in = sem("condW_in")
        ad_in = [sem(f"ad_in{s}") for s in range(2)]
        row_in = [sem(f"row_in{s}") for s in range(RAW)]
        down_in = [sem(f"down_in{s}") for s in range(KD)]
        dve_step = sem("dve_step")
        wmax_done = sem("wmax_done")
        wy_done = sem("wy_done")
        wgrid_done = sem("wgrid_done")
        wshift_done = sem("wshift_done")
        row_q = sem("row_q")
        misc_full = sem("misc_full")
        misc_done = sem("misc_done")
        scales_out = sem("scales_out")
        scales_in = [sem("scales_in"), sem("dscale_in")]
        adb_done = sem("adb_done")
        wb_full = sem("wb_full")
        wb_done = sem("wb_done")
        xc_full = sem("xc_full")
        xmax_done = sem("xmax_done")
        xy_done = sem("xy_done")
        xgrid_done = sem("xgrid_done")
        xshift_done = sem("xshift_done")
        xq_done = sem("xq_done")
        gu_full = sem("gu_full")
        zg_done = sem("zg_done")
        silu_done = sem("silu_done_l1")
        gu_done = sem("gu_done")
        hid_done = sem("hid_done_l1")
        hmax_done = sem("hmax_done")
        hy_done = sem("hy_done")
        hgrid_done = sem("hgrid_done")
        hshift_done = sem("hshift_done")
        hq_done = sem("hq_done")
        out_full = sem("out_full")
        outs_done = sem("outs_done")
        fin_done = sem("fin_done")
        stored = [sem(f"stored{s}") for s in range(3)]

        rows = [("gate", j) for j in range(L1T)] + [("up", j) for j in range(L1T)] + [("down", j) for j in range(KD)]
        NR = len(rows)
        GATHERED = 2 * L1T

        def raw(n):
            kind, j = rows[n]
            if kind != "down":
                return spare[:, (n % RAW) * D:(n % RAW + 1) * D]
            a = ((RAW * D, RAW * D + L1I, 0, L1I)[j])
            return spare[:, a:a + L1I]
        width = {"gate": D, "up": D, "down": L1I}
        fills = []
        for n, (kind, j) in enumerate(rows):
            nb = width[kind] // P
            for b0 in range(0, nb, 8):
                fills.append((n, b0, min(8, nb - b0)))
        last_fill = {m: f for f, (m, _, _) in enumerate(fills)}

        def step_fills(i):
            out = []
            if 0 <= i - 1 < NT:
                out.append(("xq", i - 1))
            if i < NT:
                out.append(("x1", i))
            if 0 <= i - 3 < NT:
                out += [("hqa", i - 3), ("hqb", i - 3)]
            return out
        order = [f for i in range(NT + 3) for f in step_fills(i)]
        fill_at = {f: len(fills) + n for n, f in enumerate(order)}

        block = ctx.enter_context(nc.Block())

        def bankb(n):
            return misc[:, n % 2, :].bitcast(BF16).rearrange("p (k n) -> p k n", n=P)

        @block.sync
        def _(sp):
            sp.dma_start(idx[:, :], d["didx"]).then_inc(idx_in, 16)
            sp.dma_start(itok[:, :], d["itok"]).then_inc(itok_in, 16)
            sp.dma_start(condW[:, :, :], d["condW"].rearrange("(k p) n -> p k n", p=P)).then_inc(condW_in, 16)
            sp.wait_ge(itok_in, 16)
            for b in range(B):
                s = b % 2
                if b >= 2:
                    sp.wait_ge(wb_done, 4 * (b - 1) + 2)
                a = sp.value_load(itok[0:1, b:b + 1], min_val=0, max_val=NA - 1)
                sp.dma_start(adA[:, s, :], d["adA"][bass.ds(a, 1), :, :].rearrange("a r n -> (a r) n")
                             ).then_inc(ad_in[s], 16)
                sp.dma_start(adB[:, s, :], d["adB"][bass.ds(a, 1), :, :].rearrange("a r n -> (a r) n")
                             ).then_inc(ad_in[s], 16)
                sp.dma_start(adS[:, s:s + 1], d["adS"][bass.ds(a, 1), :].to_broadcast([RANK, 1])
                             ).then_inc(ad_in[s], 16)
                if b == 1:
                    for n, (kind, j) in enumerate(rows):
                        if kind == "down":
                            if j == 2:
                                sp.wait_ge(wy_done, GATHERED)
                            sp.dma_start(raw(n), d["wdown"][j * P:(j + 1) * P, :]).then_inc(down_in[j], 16)
                    flat = d["scales"].rearrange("j p -> (j p)").unsqueeze(0)
                    for i, (j0, j1, scales) in enumerate(((0, GATHERED, (gscale, uscale)), (GATHERED, NR, (dscale,)))):
                        sp.wait_ge(wmax_done, j1)
                        sp.dma_start(d["scales"][j0:j1, :].rearrange("j p -> p j"), colscale[:, j0:j1],
                                     allow_slow_non_contiguous=True).then_inc(scales_out, 16)
                        sp.wait_ge(scales_out, 16 * (i + 1))
                        at = j0 * P
                        for scale in scales:
                            n = scale.shape[1]
                            sp.dma_start(scale[:, :], flat[:, at:at + n].to_broadcast([P, n])
                                         ).then_inc(scales_in[i], 16)
                            at += n
            for t in range(NT):
                sp.wait_ge(fin_done, t + 1)
                sp.dma_start(d["out"][t * P:(t + 1) * P, :], fin[:, t % 3, :]).then_inc(stored[t % 3], 16)
            for s in range(3):
                sp.wait_ge(stored[s], 16 * len(range(s, NT, 3)))

        @block.gpsimd
        def _(pool):
            def gather(n):
                kind, j = rows[n]
                if kind == "down":
                    return
                if n >= RAW:
                    pool.wait_ge(wy_done, n - RAW + 1)
                nc.gpsimd.indirect_dma_start(
                    raw(n), None, d["w" + kind],
                    bass.IndirectOffsetOnAxis(ap=idx[:, j:j + 1].bitcast(U32), axis=0)).then_inc(row_in[n % RAW], 16)

            AHEAD = RAW - 3
            pool.wait_ge(idx_in, 16)
            for n in range(AHEAD):
                gather(n)
            for n, (kind, j) in enumerate(rows):
                if n + AHEAD < NR:
                    gather(n + AHEAD)
                y, wd = n % RING, width[kind]
                pool.wait_ge(wgrid_done, n + 1)
                nc.gpsimd.tensor_tensor(wy[:, y, 0:wd], wy[:, y, 0:wd], wgrid[:, y, 0:wd], ALU.add
                                        ).then_inc(wshift_done, 1)

            def weigh(t, c):
                n = t * GC + c
                cols = slice(c * GW, (c + 1) * GW)
                pool.wait_ge(silu_done, n + 1 + 2)
                pool.wait_ge(gu_done, n + 1 + 2)
                nc.gpsimd.tensor_tensor(hid[:, t % 2, cols], hid[:, t % 2, cols], sg[:, n % 2, :], ALU.mult
                                        ).then_inc(hid_done, 1)

            for i in range(NT + 3):
                x, h, m, o = i, i - 1, i - 2, i - 3
                if 0 <= h < NT:
                    weigh(h, 0)
                    weigh(h, 1)
                if x < NT:
                    pool.wait_ge(xgrid_done, x + 1)
                    nc.gpsimd.tensor_tensor(xy, xy, xgrid, ALU.add).then_inc(xshift_done, 1)
                if 0 <= m < NT:
                    pool.wait_ge(hgrid_done, m + 1)
                    nc.gpsimd.tensor_tensor(hy, hy, hgrid, ALU.add).then_inc(hshift_done, 1)
                if 0 <= h < NT:
                    weigh(h, 2)
                    weigh(h, 3)
                if 0 <= o < NT:
                    pool.wait_ge(outs_done, o + 1)
                    nc.gpsimd.tensor_tensor(fin[:, o % 3, :], fin[:, o % 3, :], x1[:, o % 4, :], ALU.add
                                            ).then_inc(fin_done, 1)

        @block.vector
        def _(dve):
            count = [0]

            def link(op):
                count[0] += 1
                op.then_inc(dve_step, 1)
                dve.wait_ge(dve_step, count[0])

            def scale_of(src, scale, r, j):
                link(nc.vector.tensor_reduce(amax[:, j:j + 1], src, AX.X, ALU.max, apply_absolute_value=True))
                link(nc.vector.tensor_scalar(scale, amax[:, j:j + 1], 1.0 / FP8_MAX, None, ALU.mult))
                return nc.vector.reciprocal(r, scale)

            def grid_of(st, y):
                link(nc.vector.tensor_scalar(st.bitcast(U32), y.bitcast(U32), 0x7F800000, None, ALU.bitwise_and))
                return nc.vector.tensor_scalar(st, st, 2.0 ** -6, 1.5 * 2.0 ** 20, ALU.max, ALU.mult)

            dve.sem_inc(misc_done, 2)
            dve.sem_inc(wb_done, 2)
            dve.sem_inc(gu_done, 2)
            dve.sem_inc(silu_done, 2)
            dve.sem_inc(hid_done, 2)

            def conditioned(b):
                s = b % 2
                dve.wait_ge(ad_in[s], 48 * (b // 2 + 1))
                nc.vector.tensor_scalar(adBs[:, s, :], adB[:, s, :], adS[:, s:s + 1], None, ALU.mult
                                        ).then_inc(adb_done, 1)
                if b == 0:
                    dve.wait_ge(condW_in, 16)
                for k in range(KD):
                    dve.wait_ge(wb_full, 4 * b + k + 1)
                    nc.vector.tensor_tensor(condWb[:, s, k, :], gu[:, k % 2, 0, :], condW[:, k, :], ALU.add
                                            ).then_inc(wb_done, 1)

            for i in range(NR + 2):
                if i == FIRST_COND + 3:
                    conditioned(0)
                if i < NR:
                    kind, j = rows[i]
                    s = i % RING
                    if kind == "down":
                        dve.wait_ge(down_in[j], 16)
                    else:
                        dve.wait_ge(row_in[i % RAW], 16 * (i // RAW + 1))
                    scale_of(raw(i), colscale[:, i:i + 1], rcp[:, s:s + 1], 0).then_inc(wmax_done, 1)
                if 0 <= i - 1 < NR:
                    m = i - 1
                    wd = width[rows[m][0]]
                    dve.wait_ge(wy_done, m + 1)
                    grid_of(wgrid[:, m % RING, 0:wd], wy[:, m % RING, 0:wd]).then_inc(wgrid_done, 1)
                if i - 2 >= 0:
                    m = i - 2
                    wd = width[rows[m][0]]
                    dve.wait_ge(wshift_done, m + 1)
                    if m >= 2:
                        dve.wait_ge(misc_full, last_fill[m - 2] + 1)
                    nc.vector.tensor_tensor(rowq[:, m % 2, 0:wd], wy[:, m % RING, 0:wd], wgrid[:, m % RING, 0:wd],
                                            ALU.subtract).then_inc(row_q, 1)
            dve.wait_ge(row_q, NR)

            def gate_up(t, c):
                n = t * GC + c
                cols = slice(c * GW, (c + 1) * GW)
                dve.wait_ge(gu_full, n + 1)
                dve.wait_ge(silu_done, n + 1)
                nc.vector.tensor_tensor(zg[:, n % 2, :], gu[:, n % 2, 0, 0:GW], gscale[:, cols], ALU.mult
                                        ).then_inc(zg_done, 1)
                nc.vector.scalar_tensor_tensor(hid[:, t % 2, cols], gu[:, n % 2, 1, 0:GW], xs[:, t % 4:t % 4 + 1],
                                               uscale[:, cols], ALU.mult, ALU.mult).then_inc(gu_done, 1)

            for i in range(NT + 3):
                x, h, m, o = i, i - 1, i - 2, i - 3
                if h == 0:
                    dve.wait_ge(scales_in[0], 32)
                if o == 0:
                    dve.wait_ge(scales_in[1], 16)
                if 0 <= o < NT:
                    dve.wait_ge(hshift_done, o + 1)
                    if o >= 1:
                        dve.wait_ge(misc_full, fill_at["hqb", o - 1] + 1)
                    nc.vector.tensor_tensor(hq[:, :], hy, hgrid, ALU.subtract).then_inc(hq_done, 1)
                if 0 <= m < NT:
                    dve.wait_ge(hid_done, 2 + m * GC + GC)
                    scale_of(hid[:, m % 2, :], hs[:, m % 4:m % 4 + 1], hr[:, m % 2:m % 2 + 1], 2).then_inc(hmax_done, 1)
                if x < NT:
                    if x % ST == 0 and x:
                        conditioned(x // ST)
                    dve.wait_ge(xc_full, x + 1)
                    scale_of(xc_ps[:, :], xs[:, x % 4:x % 4 + 1], xr[:, x % 2:x % 2 + 1], 1).then_inc(xmax_done, 1)
                if 0 <= h < NT:
                    gate_up(h, 0)
                    gate_up(h, 1)
                if x < NT:
                    dve.wait_ge(xy_done, x + 1)
                    grid_of(xgrid, xy).then_inc(xgrid_done, 1)
                if 0 <= m < NT:
                    dve.wait_ge(hy_done, m + 1)
                    grid_of(hgrid, hy).then_inc(hgrid_done, 1)
                if 0 <= o < NT:
                    dve.wait_ge(out_full, o + 1)
                    if o >= 3:
                        dve.wait_ge(stored[o % 3], 16 * (o // 3))
                    nc.vector.scalar_tensor_tensor(fin[:, o % 3, :], out_ps[:, :], hs[:, o % 4:o % 4 + 1],
                                                   dscale[:, :], ALU.mult, ALU.mult).then_inc(outs_done, 1)
                if 0 <= h < NT:
                    gate_up(h, 2)
                if x < NT:
                    dve.wait_ge(xshift_done, x + 1)
                    if x >= 1:
                        dve.wait_ge(misc_full, fill_at["xq", x - 1] + 1)
                    nc.vector.tensor_tensor(xq[:, :], xy, xgrid, ALU.subtract).then_inc(xq_done, 1)
                if 0 <= h < NT:
                    gate_up(h, 3)

        @block.scalar
        def _(act):
            def turned_weights(n):
                m, b0, nb = fills[n]
                kind, j = rows[m]
                act.wait_ge(misc_full, n + 1)
                dst = {"gate": wgT, "up": wuT, "down": wdT}[kind]
                nc.scalar.activation(dst[:, b0:b0 + nb, j * P:(j + 1) * P], bankb(n)[:, 0:nb, :], ACT.Copy
                                     ).then_inc(misc_done, 1)

            n = 0
            for m, (kind, j) in enumerate(rows):
                wd = width[kind]
                act.wait_ge(wmax_done, m + 1)
                if m >= RING:
                    act.wait_ge(row_q, m - RING + 1)
                nc.scalar.activation(wy[:, m % RING, 0:wd], raw(m), ACT.Copy,
                                     scale=rcp[:, m % RING:m % RING + 1]).then_inc(wy_done, 1)
                while n < len(fills) and fills[n][0] <= m - RING:
                    turned_weights(n)
                    n += 1
            while n < len(fills):
                turned_weights(n)
                n += 1

            def take(f):
                n = fill_at[f]
                act.wait_ge(misc_full, n + 1)
                kind, t = f
                if kind == "x1":
                    if t >= 4:
                        act.wait_ge(fin_done, t - 3)
                    op = nc.scalar.activation(x1[:, t % 4, :], misc[:, n % 2, :], ACT.Copy)
                elif kind == "xq":
                    op = nc.scalar.activation(xqT[:, :, :], bankb(n)[:, 0:KD, :], ACT.Copy)
                elif kind == "hqa":
                    op = nc.scalar.activation(hqT[:, 0:8, :], bankb(n), ACT.Copy)
                else:
                    op = nc.scalar.activation(hqT[:, 8:L1T, :], bankb(n)[:, 0:L1T - 8, :], ACT.Copy)
                op.then_inc(misc_done, 1)

            def silu(t, c):
                n = t * GC + c
                act.wait_ge(zg_done, n + 1)
                act.wait_ge(hid_done, n + 1)
                nc.scalar.activation(sg[:, n % 2, :], zg[:, n % 2, :], ACT.Silu, scale=xs[:, t % 4:t % 4 + 1]
                                     ).then_inc(silu_done, 1)

            for i in range(NT + 3):
                x, h, m, o = i, i - 1, i - 2, i - 3
                if 0 <= h < NT:
                    take(("xq", h))
                if x < NT:
                    take(("x1", x))
                if 0 <= m < NT:
                    act.wait_ge(hmax_done, m + 1)
                    if m >= 1:
                        act.wait_ge(hq_done, m)
                    nc.scalar.activation(hy, hid[:, m % 2, :], ACT.Copy, scale=hr[:, m % 2:m % 2 + 1]
                                         ).then_inc(hy_done, 1)
                if x < NT:
                    act.wait_ge(xmax_done, x + 1)
                    if x >= 1:
                        act.wait_ge(xq_done, x)
                    else:
                        act.wait_ge(row_q, NR)
                    nc.scalar.activation(xy, xc_ps[:, :], ACT.Copy, scale=xr[:, x % 2:x % 2 + 1]).then_inc(xy_done, 1)
                if 0 <= o < NT:
                    take(("hqa", o))
                    take(("hqb", o))
                if 0 <= h < NT:
                    for c in range(GC):
                        silu(h, c)

        @block.tensor
        def _(pe):
            def conditioned(b):
                s = b % 2
                pe.wait_ge(adb_done, b + 1)
                for k in range(KD):
                    pe.wait_ge(wb_done, 4 * b + k + 1)
                    nc.tensor.matmul(gu[:, k % 2, 0, :], adA[:, s, k * P:(k + 1) * P], adBs[:, s, :],
                                     start=True, stop=True).then_inc(wb_full, 1)
                pe.wait_ge(wb_done, 4 * b + 4 + 2)

            for n, (m, b0, nb) in enumerate(fills):
                if m == FIRST_COND + 1 and b0 == 0:
                    conditioned(0)
                pe.wait_ge(misc_done, n + 1)
                pe.wait_ge(row_q, m + 1)
                for k in range(nb):
                    last = nc.tensor.transpose(bankb(n)[:, k, :], rowq[:, m % 2, (b0 + k) * P:(b0 + k + 1) * P],
                                               g["identb"][:, :])
                last.then_inc(misc_full, 1)

            def project(t):
                if t >= 1:
                    pe.wait_ge(xy_done, t)
                for k in range(KD):
                    last = nc.tensor.matmul(xc_ps[:, :], x1T[:, k, t * P:(t + 1) * P], condWb[:, (t // ST) % 2, k, :],
                                            start=k == 0, stop=k == KD - 1)
                last.then_inc(xc_full, 1)
                n = fill_at["x1", t]
                pe.wait_ge(misc_done, n + 1)
                for k in range(KD):
                    last = nc.tensor.transpose(misc[:, n % 2, k * P:(k + 1) * P], x1T[:, k, t * P:(t + 1) * P],
                                               g["ident"][:, :])
                last.then_inc(misc_full, 1)

            def turn_input(t):
                n = fill_at["xq", t]
                pe.wait_ge(misc_done, n + 1)
                pe.wait_ge(xq_done, t + 1)
                for k in range(KD):
                    last = nc.tensor.transpose(bankb(n)[:, k, :], xq[:, k * P:(k + 1) * P], g["identb"][:, :])
                last.then_inc(misc_full, 1)

            def gate_up(t, chunks):
                pe.wait_ge(misc_done, 2 + fill_at["xq", t] + 1)
                for c in chunks:
                    m = t * GC + c
                    pe.wait_ge(gu_done, m + 1)
                    for j, wT in enumerate((wgT, wuT)):
                        for k in range(KD):
                            last = nc.tensor.matmul(gu[:, m % 2, j, 0:GW], xqT[:, k, :], wT[:, k, c * GW:(c + 1) * GW],
                                                    start=k == 0, stop=k == KD - 1)
                    last.then_inc(gu_full, 1)

            def turn_hidden(t):
                pe.wait_ge(hq_done, t + 1)
                for kind, k0, nb in (("hqa", 0, 8), ("hqb", 8, L1T - 8)):
                    n = fill_at[kind, t]
                    pe.wait_ge(misc_done, n + 1)
                    for k in range(nb):
                        last = nc.tensor.transpose(bankb(n)[:, k, :], hq[:, (k0 + k) * P:(k0 + k + 1) * P],
                                                   g["identb"][:, :])
                    last.then_inc(misc_full, 1)

            def down(t):
                pe.wait_ge(misc_done, 2 + fill_at["hqb", t] + 1)
                if t >= 1:
                    pe.wait_ge(outs_done, t)
                for k in range(L1T):
                    last = nc.tensor.matmul(out_ps[:, :], hqT[:, k, :], wdT[:, k, :], start=k == 0, stop=k == L1T - 1)
                last.then_inc(out_full, 1)

            for i in range(NT + 3):
                x, h, o = i, i - 1, i - 3
                if 0 <= h < NT:
                    turn_input(h)
                if x < NT:
                    if x % ST == 0 and x:
                        pe.wait_ge(gu_done, 2 + (x - 1) * GC)
                        conditioned(x // ST)
                    project(x)
                if 0 <= o < NT:
                    turn_hidden(o)
                if 0 <= h < NT:
                    gate_up(h, (0, 1))
                if 0 <= o < NT:
                    down(o)
                if 0 <= h < NT:
                    gate_up(h, (2, 3))


def build(nc, d):
    with ExitStack() as ctx:
        g = {
            "ident": ctx.enter_context(nc.sbuf_tensor("ident", [P, P], F32)),
            "identb": ctx.enter_context(nc.sbuf_tensor("identb", [P, P], BF16)),
            "condT": ctx.enter_context(nc.sbuf_tensor("condT", [P, KD, T], F32)),
            "blank_done": ctx.enter_context(nc.semaphore("blank_done")),
            "ident_done": ctx.enter_context(nc.semaphore("ident_done")),
            "r_first": 1 + 2,
            "r_second": 1 + 2 + 3 + 2 * (CW // P) + 1 + 3 * TOPK - 1 + 5,
            "r_all": 2 + 3 + 2 * (CW // P) + 1 + 3 * TOPK - 1 + 5 + 2,
        }
        attend(nc, d, g)
        g["x1T"] = ctx.enter_context(nc.sbuf_tensor("x1T", [P, KD, T], F32))
        experts(nc, d, g)
        ffn(nc, d, g)


def kernel(**x):
    import numpy as np
    import concourse.bacc as bacc
    from concourse.bass_utils import run_bass_kernel_spmd

    a = {k: np.asarray(v) for k, v in x.items()}

    def tiles(w, rows):
        full = np.zeros((rows * P,) + w.shape[1:], w.dtype)
        full[:w.shape[0]] = w
        return full.reshape(rows, P, -1).transpose(1, 0, 2).reshape(P, -1)

    def repeated(row, n):
        return np.broadcast_to(row[None, :], (n, row.shape[0]))

    def low_rows(w):
        return w.transpose(0, 2, 1).reshape(LR, -1)

    def twice(w):
        return np.concatenate([w, w])

    q = "L0_ffn_"
    part_a, part_b, part_c = [], [], []
    for f in range(F):
        part_a.append(np.concatenate(
            [tiles(a[q + n + "_W"][f].T, KD) for n in ("gate", "up")]
            + [twice(low_rows(a[q + n + "_qb"][f])) for n in ("gate", "up")]
            + [repeated(a[q + n + "_scale"][f], P) for n in ("gate", "up")], axis=1))
        dqa = a[q + "down_qa"][f].reshape(LR, I).T
        part_b.append(np.concatenate([
            tiles(a[q + "down_W"][f].T, 3), tiles(np.concatenate([dqa, dqa], axis=1), 3),
            twice(low_rows(a[q + "down_qb"][f])), repeated(a[q + "down_scale"][f], P)], axis=1))
        mu = np.zeros((2, KR, R, D), np.float32)
        mu[:, :, 0:2] = a[q + "mask_up_W"][f].T[None, :, None, :]
        qa = np.concatenate([a[q + n + "_qa"][f].reshape(LR, D) for n in ("gate", "up")]).T
        part_c.append(np.concatenate([mu.reshape(P, D), tiles(qa, KD)], axis=1))
    shared_a, shared_b = [], []
    for s in range(2):
        i = slice(s * I, (s + 1) * I)
        shared_a.append(np.concatenate([tiles(a[q + "sh_gate_W"][i].T, KD), tiles(a[q + "sh_up_W"][i].T, KD)], axis=1))
        shared_b.append(tiles(a[q + "sh_down_W"][:, i].T, 3))
    rows = np.arange(P) % R
    mu_mask = np.stack([rows == 0, rows == 1], axis=1).astype(np.float32)
    arrays = {
        "xT": a["x"].transpose(0, 2, 1),
        "cond": a["cond_1"].reshape(1, B),
        "Wq": a["L0_cond_Wq"].T, "Wk": a["L0_cond_Wk"].T, "Wv": a["L0_cond_Wv"].T, "Wo": a["L0_cond_Wo"].T,
        "router": a["L0_ffn_gate_weight"].T,
        "inv": a["L0_ffn_inv_mapping"].reshape(1, E),
        "expert_a": np.stack(part_a), "expert_b": np.stack(part_b), "expert_c": np.stack(part_c),
        "shared_a": np.stack(shared_a), "shared_b": np.stack(shared_b),
        "mu_mask": mu_mask,
        "didx": a["L1_ffn_down_reorder_index"].reshape(L1T, P).T,
        "itok": a["itok_B_0_6"].reshape(1, B),
        "condW": a["L1_cond_W"].T,
        "adA": a["L1_cond_A"],
        "adB": a["L1_cond_Bm"].transpose(0, 2, 1),
        "adS": a["L1_cond_scalings"].reshape(NA, 1),
        "wgate": a["L1_ffn_w_gate"], "wup": a["L1_ffn_w_up"], "wdown": a["L1_ffn_w_down"],
    }
    arrays = {"in_" + k: np.ascontiguousarray(v) for k, v in arrays.items()}
    nc = bacc.Bacc("TRN2", target_bir_lowering=False, num_devices=1)
    d = {k[3:]: nc.dram_tensor(k, v.shape, mybir.dt.from_np(v.dtype), kind="ExternalInput").ap()
         for k, v in arrays.items()}
    d["route"] = nc.dram_tensor("route", [E + F, T], F32, kind="Internal").ap()
    d["scales"] = nc.dram_tensor("scales", [2 * L1T + KD, P], F32, kind="Internal").ap()
    d["out"] = nc.dram_tensor("out", [T, D], F32, kind="ExternalOutput").ap()
    build(nc, d)
    got = run_bass_kernel_spmd(nc, [arrays], core_ids=[0])
    return got.results[0]["out"].reshape(B, S, D)
```
